# Optimizing a Trainium2 kernel written in Bass

```python
import numpy as np
import jax
import jax.numpy as jnp

def _softmax(x, axis=-1):
    return jax.nn.softmax(x, axis=axis)

def _gelu(x):
    return jax.nn.gelu(x, approximate=True)

def _silu(x):
    return jax.nn.silu(x)

def _sigmoid(x):
    return jax.nn.sigmoid(x)

def _layernorm(x, axis=-1, eps=1e-05):
    m = jnp.mean(x, axis=axis, keepdims=True)
    v = jnp.var(x, axis=axis, keepdims=True)
    return (x - m) / jnp.sqrt(v + eps)

def _scatter_add(tgt, idx, src, axis=0):
    return tgt.at[idx].add(src)

def _segment_sum(src, seg, n):
    return jax.ops.segment_sum(src, seg, n)
kernel_name = 'mk_gnn_resnorm_d4_gnn_r16_f1b5cd'

def setup_inputs(seed: int=0):
    np.random.seed(seed)
    _w = jnp.asarray

    def _rec_inputs():
        import jax
        import jax.numpy as jnp
        _gk = jax.random.key(seed)
        x = -0.0005121 + 1.001 * jax.random.normal(jax.random.fold_in(_gk, 1), (6250, 160), jnp.float32)
        src = jax.random.randint(jax.random.fold_in(_gk, 2), (100000,), 0, 6250, jnp.int32)
        dst = jax.random.randint(jax.random.fold_in(_gk, 3), (100000,), 0, 6250, jnp.int32)
        _o = jnp.argsort(dst, stable=True)
        src = src[_o]
        dst = dst[_o]
        edge_attr_16 = jax.random.uniform(jax.random.fold_in(_gk, 12), (100000, 16), jnp.float32, 0.0, 1)
        edge_attr_3 = 0.00047201 + 1.00023 * jax.random.normal(jax.random.fold_in(_gk, 13), (100000, 3), jnp.float32)
        edge_attr_4 = 0.000898722 + 1.00012 * jax.random.normal(jax.random.fold_in(_gk, 14), (100000, 4), jnp.float32)
        edge_attr_64 = 0.000279952 + 1.00013 * jax.random.normal(jax.random.fold_in(_gk, 15), (100000, 64), jnp.float32)
        node_vec1 = jax.random.uniform(jax.random.fold_in(_gk, 17), (6250, 1), jnp.float32, 0.0, 1)
        return (x, src, dst, edge_attr_16, edge_attr_3, edge_attr_4, edge_attr_64, node_vec1)
    x, src, dst, edge_attr_16, edge_attr_3, edge_attr_4, edge_attr_64, node_vec1 = _rec_inputs()

    def _L0_gnn_setup():
        import jax, jax.numpy as jnp
        import numpy as np
        N, E = (1250, 20000)
        CS, CV = (64, 32)
        AS_, AV, H = (16, 8, 4)
        NB = 16
        SQRT3 = 1.7320508075688772
        SQRT2 = 1.4142135623730951
        EPS = 1e-05

        def _cg_tp(s, v, y0, y1, w_ss, w_sv, w_vs, w_vv0, w_vv1):
            out_s = jnp.concatenate([w_ss * s * y0[:, None], w_vv0 * (jnp.einsum('eci,ei->ec', v, y1) / SQRT3)], axis=-1)
            out_v = jnp.concatenate([(w_sv * s)[:, :, None] * y1[:, None, :], (w_vs * jnp.ones_like(v[..., 0]))[..., None] * v * y0[:, None, None], (w_vv1 * jnp.ones_like(v[..., 0]))[..., None] * (jnp.cross(v, y1[:, None, :]) / SQRT2)], axis=1)
            return (out_s, out_v)

        def _equiv_layernorm(s, v, gamma_s, beta_s, gamma_v):
            mu = jnp.mean(s, axis=-1, keepdims=True)
            var = jnp.var(s, axis=-1, keepdims=True)
            s_n = (s - mu) * jax.lax.rsqrt(var + EPS) * gamma_s + beta_s
            rms = jnp.sqrt(jnp.mean(jnp.sum(v * v, axis=-1), axis=-1, keepdims=True) + EPS)
            v_n = v / rms[..., None] * gamma_v[None, :, None]
            return (s_n, v_n)
        key = jax.random.key(seed)
        ks = jax.random.split(key, 26)

        def rn(k, shape, fan):
            return jax.random.normal(k, shape, jnp.float32) / np.sqrt(fan)
        D1S, D1V = (CS + CV, CS + 2 * CV)
        WN = 2 * CS + 3 * CV
        inp = {'node': jax.random.normal(ks[0], (N, CS + 3 * CV), jnp.float32), 'edge_index': jax.random.randint(ks[1], (2, E), 0, N, jnp.int64 if jax.config.jax_enable_x64 else jnp.int32), 'rbf': jax.random.uniform(ks[2], (E, NB), jnp.float32), 'rsh': jax.random.normal(ks[3], (E, 4), jnp.float32), 'gamma_s': jnp.ones((CS,), jnp.float32), 'beta_s': jnp.zeros((CS,), jnp.float32), 'gamma_v': jnp.ones((CV,), jnp.float32), 'Ws_src': rn(ks[4], (CS, CS), CS), 'Wv_src': rn(ks[5], (CV, CV), CV), 'Ws_dst': rn(ks[6], (CS, CS), CS), 'Wv_dst': rn(ks[7], (CV, CV), CV), 'W_rbf': rn(ks[8], (NB, WN), NB), 'W_alpha': rn(ks[9], (D1S, H * AS_), D1S), 'alpha_dot': rn(ks[10], (1, H, AS_), AS_), 'Ws_val': rn(ks[11], (D1S, CS), D1S), 'Wv_val': rn(ks[12], (D1V, CV), D1V), 'Wg': rn(ks[13], (CS, CV), CS), 'w2_ss': rn(ks[14], (CS,), 1), 'w2_sv': rn(ks[15], (CS,), 1), 'w2_vs': rn(ks[16], (CV,), 1), 'w2_vv0': rn(ks[17], (CV,), 1), 'w2_vv1': rn(ks[18], (CV,), 1), 'Ws_vlin': rn(ks[19], (D1S, H * AS_), D1S), 'Wv_vlin': rn(ks[20], (D1V, H * AV), D1V), 'Wps': rn(ks[21], (H * AS_, CS), H * AS_), 'Wpv': rn(ks[22], (H * AV, CV), H * AV)}
        return inp
    _L0_gnn_all = _L0_gnn_setup()
    _L0_gnn_in = {k: v for k, v in _L0_gnn_all.items() if k in ('gamma_s', 'beta_s', 'gamma_v', 'Ws_src', 'Wv_src', 'Ws_dst', 'Wv_dst', 'W_rbf', 'W_alpha', 'alpha_dot', 'Ws_val', 'Wv_val', 'Wg', 'w2_ss', 'w2_sv', 'w2_vs', 'w2_vv0', 'w2_vv1', 'Ws_vlin', 'Wv_vlin', 'Wps', 'Wpv')}
    del _L0_gnn_all

    def _L1_gnn_setup():
        import jax, jax.numpy as jnp
        import numpy as np
        N_NODES = 625
        N_EDGES = 20000
        MUL0, MUL1 = (64, 32)
        EDGE_DIM = 64
        W_NUMEL = 224
        DENOM = 32.0
        SQRT3 = 3.0 ** 0.5
        INV_SQRT3 = 1.0 / SQRT3
        INV_SQRT2 = 2.0 ** (-0.5)

        def _forward(node_feature, edge_attr, edge_feature, W_skip0, W_skip1, W_nl0, W_nl1, W_fc1, W_fc2, W_out_s, W_out_v, edge_index):
            N = node_feature.shape[0]
            E = edge_attr.shape[0]
            s = node_feature[:, :MUL0]
            v = node_feature[:, MUL0:].reshape(N, MUL1, 3)
            skip_s = s @ W_skip0
            skip_v = jnp.einsum('nmi,mk->nki', v, W_skip1)
            s = s @ W_nl0
            v = jnp.einsum('nmi,mk->nki', v, W_nl1)
            rhat = edge_attr / jnp.linalg.norm(edge_attr, axis=-1, keepdims=True)
            sh1 = SQRT3 * rhat
            w = jax.nn.relu(edge_feature @ W_fc1) @ W_fc2
            w0, w1, w2, w3, w4 = jnp.split(w, [64, 128, 160, 192], axis=-1)
            src, dst = (edge_index[0], edge_index[1])
            xs = s[dst]
            xv = v[dst]
            out0a = w0 * xs
            out0b = w3 * (jnp.einsum('emi,ei->em', xv, sh1) * INV_SQRT3)
            out1a = (w1 * xs)[:, :, None] * sh1[:, None, :]
            out1b = w2[:, :, None] * xv
            out1c = w4[:, :, None] * (jnp.cross(xv, sh1[:, None, :]) * INV_SQRT2)
            tp = jnp.concatenate([out0a, out0b, out1a.reshape(E, -1), out1b.reshape(E, -1), out1c.reshape(E, -1)], axis=-1)
            agg = jax.ops.segment_sum(tp, src, num_segments=N) / DENOM
            agg_s = agg[:, :96]
            agg_v = agg[:, 96:].reshape(N, 128, 3)
            out_s = agg_s @ W_out_s + skip_s
            out_v = jnp.einsum('nmi,mk->nki', agg_v, W_out_v) + skip_v
            fs = jax.nn.silu(out_s[:, :MUL0])
            gate = jax.nn.sigmoid(out_s[:, MUL0:MUL0 + 32])
            gv = gate[:, :, None] * out_v
            return jnp.concatenate([fs, gv.reshape(N, -1)], axis=-1)
        key = jax.random.key(seed)
        ks = jax.random.split(key, 12)

        def lin(k, fi, fo):
            return jax.random.normal(k, (fi, fo), jnp.float32) / np.float32(np.sqrt(fi))
        return {'node_feature': jax.random.normal(ks[0], (N_NODES, MUL0 + 3 * MUL1), jnp.float32), 'edge_attr': jax.random.normal(ks[1], (N_EDGES, 3), jnp.float32), 'edge_feature': jax.random.normal(ks[2], (N_EDGES, EDGE_DIM), jnp.float32), 'W_skip0': lin(ks[3], MUL0, 96), 'W_skip1': lin(ks[4], MUL1, 32), 'W_nl0': lin(ks[5], MUL0, MUL0), 'W_nl1': lin(ks[6], MUL1, MUL1), 'W_fc1': lin(ks[7], EDGE_DIM, 64), 'W_fc2': lin(ks[8], 64, W_NUMEL), 'W_out_s': lin(ks[9], 96, 96), 'W_out_v': lin(ks[10], 128, 32), 'edge_index': jax.random.randint(ks[11], (2, N_EDGES), 0, N_NODES)}
    _L1_gnn_all = _L1_gnn_setup()
    _L1_gnn_in = {k: v for k, v in _L1_gnn_all.items() if k in ('W_skip0', 'W_skip1', 'W_nl0', 'W_nl1', 'W_fc1', 'W_fc2', 'W_out_s', 'W_out_v')}
    del _L1_gnn_all

    def _L2_gnn_setup():
        import jax, jax.numpy as jnp
        import numpy as np
        N = 1250
        E = 20000
        MUL0 = 64
        MUL1 = 32
        FC_IN = 16
        FC_H = 64
        WNUM = 192
        key = jax.random.key(seed)
        ks = jax.random.split(key, 16)
        return {'x': jax.random.normal(ks[0], (N, MUL0 + 3 * MUL1), jnp.float32), 'node_attr': jnp.ones((N, 1), jnp.float32), 'edge_scalars': jax.random.normal(ks[1], (E, FC_IN), jnp.float32), 'edge_attr_sh': jax.random.normal(ks[2], (E, 4), jnp.float32), 'edge_src': jax.random.randint(ks[3], (E,), 0, N), 'edge_dst': jax.random.randint(ks[4], (E,), 0, N), 'Wfc1': jax.random.normal(ks[5], (FC_IN, FC_H), jnp.float32), 'Wfc2': jax.random.normal(ks[6], (FC_H, WNUM), jnp.float32), 'Wsc0': jax.random.normal(ks[7], (MUL0, MUL0), jnp.float32), 'Wsc1': jax.random.normal(ks[8], (MUL1, MUL1), jnp.float32), 'Wl1_0': jax.random.normal(ks[9], (MUL0, MUL0), jnp.float32), 'Wl1_1': jax.random.normal(ks[10], (MUL1, MUL1), jnp.float32), 'Wl2_s': jax.random.normal(ks[11], (MUL0 + MUL1, MUL0), jnp.float32), 'Wl2_v': jax.random.normal(ks[12], (MUL0 + MUL1, MUL1), jnp.float32), 'Wa': 0.1 * jax.random.normal(ks[13], (MUL0 + MUL1, 1), jnp.float32)}
    _L2_gnn_all = _L2_gnn_setup()
    _L2_gnn_in = {k: v for k, v in _L2_gnn_all.items() if k in ('Wfc1', 'Wfc2', 'Wsc0', 'Wsc1', 'Wl1_0', 'Wl1_1', 'Wl2_s', 'Wl2_v', 'Wa')}
    del _L2_gnn_all

    def _L3_gnn_setup():
        import jax, jax.numpy as jnp
        import numpy as np
        N, E = (2500, 40000)
        S_IN, V_IN = (64, 32)
        S_MID, V_MID = (96, 128)
        S_OUT, V_OUT = (96, 32)
        R = 64
        FC_HID = 64
        W_NUMEL = 64 + 64 + 32 + 32 + 32
        NUM_NEIGHBORS = 16.0

        def _inv(d):
            return 1.0 / jnp.sqrt(jnp.float32(d))

        def _forward(node_features, node_attr, edge_attr, edge_scalars, lin1_ws, lin1_wv, fc_w1, fc_w2, sc_ws, sc_wv, lin2_ws, lin2_wv, edge_src, edge_dst):
            n = node_features.shape[0]
            s = node_features[:, :S_IN]
            v = node_features[:, S_IN:].reshape(n, V_IN, 3)
            a = node_attr
            sc_s = s @ sc_ws * a * _inv(S_IN)
            sc_v = jnp.einsum('nci,cd->ndi', v, sc_wv) * a[:, :, None] * _inv(V_IN)
            h_s = s @ lin1_ws * a * _inv(S_IN)
            h_v = jnp.einsum('nci,cd->ndi', v, lin1_wv) * a[:, :, None] * _inv(V_IN)
            hid = jax.nn.silu(edge_scalars @ fc_w1 * _inv(R))
            w = hid @ fc_w2 * _inv(FC_HID)
            w1, w2, w3, w4, w5 = jnp.split(w, [64, 128, 160, 192], axis=-1)
            es = h_s[edge_src]
            ev = h_v[edge_src]
            e0 = edge_attr[:, :1]
            e1 = edge_attr[:, 1:4]
            m_s1 = w1 * es * e0
            m_s2 = w4 * jnp.einsum('eci,ei->ec', ev, e1) * _inv(3)
            m_v1 = (w2 * es)[:, :, None] * e1[:, None, :]
            m_v2 = w3[:, :, None] * ev * e0[:, :, None]
            m_v3 = w5[:, :, None] * jnp.cross(ev, e1[:, None, :]) * _inv(2)
            mid_s = jnp.concatenate([m_s1, m_s2], axis=-1)
            mid_v = jnp.concatenate([m_v1, m_v2, m_v3], axis=1)
            inv_nn = 1.0 / jnp.sqrt(jnp.float32(NUM_NEIGHBORS))
            agg_s = jax.ops.segment_sum(mid_s, edge_dst, num_segments=n) * inv_nn
            agg_v = jax.ops.segment_sum(mid_v, edge_dst, num_segments=n) * inv_nn
            o_s = agg_s @ lin2_ws * a * _inv(S_MID)
            o_v = jnp.einsum('nci,cd->ndi', agg_v, lin2_wv) * a[:, :, None] * _inv(V_MID)
            pre_s = sc_s + o_s
            pre_v = sc_v + o_v
            scalars = jax.nn.silu(pre_s[:, :64])
            gates = jax.nn.sigmoid(pre_s[:, 64:96])
            gated = gates[:, :, None] * pre_v
            return jnp.concatenate([scalars, gated.reshape(n, 3 * V_OUT)], axis=-1)
        key = jax.random.key(seed)
        ks = jax.random.split(key, 13)
        return {'node_features': jax.random.normal(ks[0], (N, S_IN + 3 * V_IN), jnp.float32), 'node_attr': jnp.ones((N, 1), jnp.float32), 'edge_src': jax.random.randint(ks[1], (E,), 0, N), 'edge_dst': jax.random.randint(ks[2], (E,), 0, N), 'edge_attr': jax.random.normal(ks[3], (E, 4), jnp.float32), 'edge_scalars': jax.random.normal(ks[4], (E, R), jnp.float32), 'lin1_ws': jax.random.normal(ks[5], (S_IN, S_IN), jnp.float32), 'lin1_wv': jax.random.normal(ks[6], (V_IN, V_IN), jnp.float32), 'fc_w1': jax.random.normal(ks[7], (R, FC_HID), jnp.float32), 'fc_w2': jax.random.normal(ks[8], (FC_HID, W_NUMEL), jnp.float32), 'sc_ws': jax.random.normal(ks[9], (S_IN, S_OUT), jnp.float32), 'sc_wv': jax.random.normal(ks[10], (V_IN, V_OUT), jnp.float32), 'lin2_ws': jax.random.normal(ks[11], (S_MID, S_OUT), jnp.float32), 'lin2_wv': jax.random.normal(ks[12], (V_MID, V_OUT), jnp.float32)}
    _L3_gnn_all = _L3_gnn_setup()
    _L3_gnn_in = {k: v for k, v in _L3_gnn_all.items() if k in ('lin1_ws', 'lin1_wv', 'fc_w1', 'fc_w2', 'sc_ws', 'sc_wv', 'lin2_ws', 'lin2_wv')}
    del _L3_gnn_all
    return {'x': x, 'src': src, 'dst': dst, 'edge_attr_16': edge_attr_16, 'edge_attr_3': edge_attr_3, 'edge_attr_4': edge_attr_4, 'edge_attr_64': edge_attr_64, 'node_vec1': node_vec1, 'L0_gnn_gamma_s': _L0_gnn_in['gamma_s'], 'L0_gnn_beta_s': _L0_gnn_in['beta_s'], 'L0_gnn_gamma_v': _L0_gnn_in['gamma_v'], 'L0_gnn_Ws_src': _L0_gnn_in['Ws_src'], 'L0_gnn_Wv_src': _L0_gnn_in['Wv_src'], 'L0_gnn_Ws_dst': _L0_gnn_in['Ws_dst'], 'L0_gnn_Wv_dst': _L0_gnn_in['Wv_dst'], 'L0_gnn_W_rbf': _L0_gnn_in['W_rbf'], 'L0_gnn_W_alpha': _L0_gnn_in['W_alpha'], 'L0_gnn_alpha_dot': _L0_gnn_in['alpha_dot'], 'L0_gnn_Ws_val': _L0_gnn_in['Ws_val'], 'L0_gnn_Wv_val': _L0_gnn_in['Wv_val'], 'L0_gnn_Wg': _L0_gnn_in['Wg'], 'L0_gnn_w2_ss': _L0_gnn_in['w2_ss'], 'L0_gnn_w2_sv': _L0_gnn_in['w2_sv'], 'L0_gnn_w2_vs': _L0_gnn_in['w2_vs'], 'L0_gnn_w2_vv0': _L0_gnn_in['w2_vv0'], 'L0_gnn_w2_vv1': _L0_gnn_in['w2_vv1'], 'L0_gnn_Ws_vlin': _L0_gnn_in['Ws_vlin'], 'L0_gnn_Wv_vlin': _L0_gnn_in['Wv_vlin'], 'L0_gnn_Wps': _L0_gnn_in['Wps'], 'L0_gnn_Wpv': _L0_gnn_in['Wpv'], 'L1_gnn_W_skip0': _L1_gnn_in['W_skip0'], 'L1_gnn_W_skip1': _L1_gnn_in['W_skip1'], 'L1_gnn_W_nl0': _L1_gnn_in['W_nl0'], 'L1_gnn_W_nl1': _L1_gnn_in['W_nl1'], 'L1_gnn_W_fc1': _L1_gnn_in['W_fc1'], 'L1_gnn_W_fc2': _L1_gnn_in['W_fc2'], 'L1_gnn_W_out_s': _L1_gnn_in['W_out_s'], 'L1_gnn_W_out_v': _L1_gnn_in['W_out_v'], 'L2_gnn_Wfc1': _L2_gnn_in['Wfc1'], 'L2_gnn_Wfc2': _L2_gnn_in['Wfc2'], 'L2_gnn_Wsc0': _L2_gnn_in['Wsc0'], 'L2_gnn_Wsc1': _L2_gnn_in['Wsc1'], 'L2_gnn_Wl1_0': _L2_gnn_in['Wl1_0'], 'L2_gnn_Wl1_1': _L2_gnn_in['Wl1_1'], 'L2_gnn_Wl2_s': _L2_gnn_in['Wl2_s'], 'L2_gnn_Wl2_v': _L2_gnn_in['Wl2_v'], 'L2_gnn_Wa': _L2_gnn_in['Wa'], 'L3_gnn_lin1_ws': _L3_gnn_in['lin1_ws'], 'L3_gnn_lin1_wv': _L3_gnn_in['lin1_wv'], 'L3_gnn_fc_w1': _L3_gnn_in['fc_w1'], 'L3_gnn_fc_w2': _L3_gnn_in['fc_w2'], 'L3_gnn_sc_ws': _L3_gnn_in['sc_ws'], 'L3_gnn_sc_wv': _L3_gnn_in['sc_wv'], 'L3_gnn_lin2_ws': _L3_gnn_in['lin2_ws'], 'L3_gnn_lin2_wv': _L3_gnn_in['lin2_wv']}

def reference(x, src, dst, edge_attr_16, edge_attr_3, edge_attr_4, edge_attr_64, node_vec1, L0_gnn_gamma_s, L0_gnn_beta_s, L0_gnn_gamma_v, L0_gnn_Ws_src, L0_gnn_Wv_src, L0_gnn_Ws_dst, L0_gnn_Wv_dst, L0_gnn_W_rbf, L0_gnn_W_alpha, L0_gnn_alpha_dot, L0_gnn_Ws_val, L0_gnn_Wv_val, L0_gnn_Wg, L0_gnn_w2_ss, L0_gnn_w2_sv, L0_gnn_w2_vs, L0_gnn_w2_vv0, L0_gnn_w2_vv1, L0_gnn_Ws_vlin, L0_gnn_Wv_vlin, L0_gnn_Wps, L0_gnn_Wpv, L1_gnn_W_skip0, L1_gnn_W_skip1, L1_gnn_W_nl0, L1_gnn_W_nl1, L1_gnn_W_fc1, L1_gnn_W_fc2, L1_gnn_W_out_s, L1_gnn_W_out_v, L2_gnn_Wfc1, L2_gnn_Wfc2, L2_gnn_Wsc0, L2_gnn_Wsc1, L2_gnn_Wl1_0, L2_gnn_Wl1_1, L2_gnn_Wl2_s, L2_gnn_Wl2_v, L2_gnn_Wa, L3_gnn_lin1_ws, L3_gnn_lin1_wv, L3_gnn_fc_w1, L3_gnn_fc_w2, L3_gnn_sc_ws, L3_gnn_sc_wv, L3_gnn_lin2_ws, L3_gnn_lin2_wv):
    import jax
    import jax.numpy as jnp

    def _L0_gnn_ref(node, rbf, rsh, gamma_s, beta_s, gamma_v, Ws_src, Wv_src, Ws_dst, Wv_dst, W_rbf, W_alpha, alpha_dot, Ws_val, Wv_val, Wg, w2_ss, w2_sv, w2_vs, w2_vv0, w2_vv1, Ws_vlin, Wv_vlin, Wps, Wpv, edge_index):
        import jax, jax.numpy as jnp
        import numpy as np
        N, E = (1250, 20000)
        CS, CV = (64, 32)
        AS_, AV, H = (16, 8, 4)
        NB = 16
        SQRT3 = 1.7320508075688772
        SQRT2 = 1.4142135623730951
        EPS = 1e-05

        def _cg_tp(s, v, y0, y1, w_ss, w_sv, w_vs, w_vv0, w_vv1):
            out_s = jnp.concatenate([w_ss * s * y0[:, None], w_vv0 * (jnp.einsum('eci,ei->ec', v, y1) / SQRT3)], axis=-1)
            out_v = jnp.concatenate([(w_sv * s)[:, :, None] * y1[:, None, :], (w_vs * jnp.ones_like(v[..., 0]))[..., None] * v * y0[:, None, None], (w_vv1 * jnp.ones_like(v[..., 0]))[..., None] * (jnp.cross(v, y1[:, None, :]) / SQRT2)], axis=1)
            return (out_s, out_v)

        def _equiv_layernorm(s, v, gamma_s, beta_s, gamma_v):
            mu = jnp.mean(s, axis=-1, keepdims=True)
            var = jnp.var(s, axis=-1, keepdims=True)
            s_n = (s - mu) * jax.lax.rsqrt(var + EPS) * gamma_s + beta_s
            rms = jnp.sqrt(jnp.mean(jnp.sum(v * v, axis=-1), axis=-1, keepdims=True) + EPS)
            v_n = v / rms[..., None] * gamma_v[None, :, None]
            return (s_n, v_n)
        n = node.shape[0]
        e = rsh.shape[0]
        s = node[:, :CS]
        v = node[:, CS:].reshape(n, CV, 3)
        s_n, v_n = _equiv_layernorm(s, v, gamma_s, beta_s, gamma_v)
        src, dst = (edge_index[0], edge_index[1])
        msg_s = (s_n @ Ws_src)[src] + (s_n @ Ws_dst)[dst]
        msg_v = jnp.einsum('ncx,cd->ndx', v_n, Wv_src)[src] + jnp.einsum('ncx,cd->ndx', v_n, Wv_dst)[dst]
        y0, y1 = (rsh[:, 0], rsh[:, 1:4])
        w1 = rbf @ W_rbf
        m1_s, m1_v = _cg_tp(msg_s, msg_v, y0, y1, w1[:, :CS], w1[:, CS:2 * CS], w1[:, 2 * CS:2 * CS + CV], w1[:, 2 * CS + CV:2 * CS + 2 * CV], w1[:, 2 * CS + 2 * CV:])
        a = (m1_s @ W_alpha).reshape(e, H, AS_)
        a = jnp.where(a > 0, a, 0.2 * a)
        a = jnp.sum(a * alpha_dot, axis=-1, keepdims=True)
        amax = jax.ops.segment_max(a, dst, num_segments=n)
        amax = jnp.where(jnp.isfinite(amax), amax, 0.0)
        ex = jnp.exp(a - amax[dst])
        den = jax.ops.segment_sum(ex, dst, num_segments=n)
        alpha = ex / (den[dst] + 1e-16)
        val_s = m1_s @ Ws_val
        val_v = jnp.einsum('ecx,cd->edx', m1_v, Wv_val)
        val_v = val_v * jax.nn.sigmoid(val_s @ Wg)[..., None]
        val_s = jax.nn.sigmoid(val_s)
        m2_s, m2_v = _cg_tp(val_s, val_v, y0, y1, w2_ss, w2_sv, w2_vs, w2_vv0, w2_vv1)
        hs = (m2_s @ Ws_vlin).reshape(e, H, AS_)
        hv = jnp.einsum('ecx,cd->edx', m2_v, Wv_vlin).reshape(e, H, AV, 3)
        h = jnp.concatenate([hs, hv.reshape(e, H, AV * 3)], axis=-1)
        agg = jax.ops.segment_sum(alpha * h, dst, num_segments=n)
        agg_s = agg[:, :, :AS_].reshape(n, H * AS_)
        agg_v = agg[:, :, AS_:].reshape(n, H * AV, 3)
        out = node + jnp.concatenate([agg_s @ Wps, jnp.einsum('ncx,cd->ndx', agg_v, Wpv).reshape(n, CV * 3)], axis=-1)
        return out

    def _L1_gnn_ref(node_feature, edge_attr, edge_feature, W_skip0, W_skip1, W_nl0, W_nl1, W_fc1, W_fc2, W_out_s, W_out_v, edge_index):
        import jax, jax.numpy as jnp
        import numpy as np
        N_NODES = 625
        N_EDGES = 20000
        MUL0, MUL1 = (64, 32)
        EDGE_DIM = 64
        W_NUMEL = 224
        DENOM = 32.0
        SQRT3 = 3.0 ** 0.5
        INV_SQRT3 = 1.0 / SQRT3
        INV_SQRT2 = 2.0 ** (-0.5)

        def _forward(node_feature, edge_attr, edge_feature, W_skip0, W_skip1, W_nl0, W_nl1, W_fc1, W_fc2, W_out_s, W_out_v, edge_index):
            N = node_feature.shape[0]
            E = edge_attr.shape[0]
            s = node_feature[:, :MUL0]
            v = node_feature[:, MUL0:].reshape(N, MUL1, 3)
            skip_s = s @ W_skip0
            skip_v = jnp.einsum('nmi,mk->nki', v, W_skip1)
            s = s @ W_nl0
            v = jnp.einsum('nmi,mk->nki', v, W_nl1)
            rhat = edge_attr / jnp.linalg.norm(edge_attr, axis=-1, keepdims=True)
            sh1 = SQRT3 * rhat
            w = jax.nn.relu(edge_feature @ W_fc1) @ W_fc2
            w0, w1, w2, w3, w4 = jnp.split(w, [64, 128, 160, 192], axis=-1)
            src, dst = (edge_index[0], edge_index[1])
            xs = s[dst]
            xv = v[dst]
            out0a = w0 * xs
            out0b = w3 * (jnp.einsum('emi,ei->em', xv, sh1) * INV_SQRT3)
            out1a = (w1 * xs)[:, :, None] * sh1[:, None, :]
            out1b = w2[:, :, None] * xv
            out1c = w4[:, :, None] * (jnp.cross(xv, sh1[:, None, :]) * INV_SQRT2)
            tp = jnp.concatenate([out0a, out0b, out1a.reshape(E, -1), out1b.reshape(E, -1), out1c.reshape(E, -1)], axis=-1)
            agg = jax.ops.segment_sum(tp, src, num_segments=N) / DENOM
            agg_s = agg[:, :96]
            agg_v = agg[:, 96:].reshape(N, 128, 3)
            out_s = agg_s @ W_out_s + skip_s
            out_v = jnp.einsum('nmi,mk->nki', agg_v, W_out_v) + skip_v
            fs = jax.nn.silu(out_s[:, :MUL0])
            gate = jax.nn.sigmoid(out_s[:, MUL0:MUL0 + 32])
            gv = gate[:, :, None] * out_v
            return jnp.concatenate([fs, gv.reshape(N, -1)], axis=-1)
        return _forward(node_feature, edge_attr, edge_feature, W_skip0, W_skip1, W_nl0, W_nl1, W_fc1, W_fc2, W_out_s, W_out_v, edge_index)

    def _L2_gnn_ref(x, node_attr, edge_scalars, edge_attr_sh, edge_src, edge_dst, Wfc1, Wfc2, Wsc0, Wsc1, Wl1_0, Wl1_1, Wl2_s, Wl2_v, Wa):
        import jax, jax.numpy as jnp
        import numpy as np
        N = 1250
        E = 20000
        MUL0 = 64
        MUL1 = 32
        FC_IN = 16
        FC_H = 64
        WNUM = 192
        n = x.shape[0]
        x0 = x[:, :MUL0]
        x1 = x[:, MUL0:].reshape(n, MUL1, 3)
        a = node_attr
        h = jax.nn.silu(edge_scalars @ (Wfc1 / jnp.sqrt(jnp.float32(FC_IN))))
        w = h @ (Wfc2 / jnp.sqrt(jnp.float32(FC_H)))
        w0 = w[:, :64]
        w1 = w[:, 64:128]
        w2 = w[:, 128:160]
        w3 = w[:, 160:192]
        inv8 = 1.0 / jnp.sqrt(jnp.float32(MUL0))
        inv32 = 1.0 / jnp.sqrt(jnp.float32(MUL1))
        sc = jnp.concatenate([x0 @ Wsc0 * a * inv8, (jnp.einsum('num,uv->nvm', x1, Wsc1) * a[..., None] * inv32).reshape(n, 3 * MUL1)], axis=1)
        f0 = x0 @ Wl1_0 * a * inv8
        f1 = jnp.einsum('num,uv->nvm', x1, Wl1_1) * a[..., None] * inv32
        e0 = f0[edge_src]
        e1 = f1[edge_src]
        sh0 = edge_attr_sh[:, :1]
        sh1 = edge_attr_sh[:, 1:4]
        mid0 = w0 * e0 * sh0
        mid1 = w3 * jnp.einsum('eum,em->eu', e1, sh1) / jnp.sqrt(3.0)
        mid2 = w1[:, :, None] * e0[:, :, None] * sh1[:, None, :]
        mid3 = w2[:, :, None] * e1 * sh0[:, :, None]
        cnt = jnp.clip(jax.ops.segment_sum(jnp.ones(edge_dst.shape, x.dtype), edge_dst, num_segments=n), 1.0)

        def smean(v):
            s = jax.ops.segment_sum(v, edge_dst, num_segments=n)
            return s / cnt.reshape((n,) + (1,) * (v.ndim - 1))
        n0, n1 = (smean(mid0), smean(mid1))
        n2, n3 = (smean(mid2), smean(mid3))
        scal = jnp.concatenate([n0, n1], axis=1)
        vec = jnp.concatenate([n2, n3], axis=1)
        inv96 = 1.0 / jnp.sqrt(jnp.float32(MUL0 + MUL1))
        alpha = scal @ Wa * a * inv96
        out_s = scal @ Wl2_s * a * inv96
        out_v = jnp.einsum('num,uv->nvm', vec, Wl2_v) * a[..., None] * inv96
        conv = jnp.concatenate([out_s, out_v.reshape(n, 3 * MUL1)], axis=1)
        return sc + alpha * conv

    def _L3_gnn_ref(node_features, node_attr, edge_src, edge_dst, edge_attr, edge_scalars, lin1_ws, lin1_wv, fc_w1, fc_w2, sc_ws, sc_wv, lin2_ws, lin2_wv):
        import jax, jax.numpy as jnp
        import numpy as np
        N, E = (2500, 40000)
        S_IN, V_IN = (64, 32)
        S_MID, V_MID = (96, 128)
        S_OUT, V_OUT = (96, 32)
        R = 64
        FC_HID = 64
        W_NUMEL = 64 + 64 + 32 + 32 + 32
        NUM_NEIGHBORS = 16.0

        def _inv(d):
            return 1.0 / jnp.sqrt(jnp.float32(d))

        def _forward(node_features, node_attr, edge_attr, edge_scalars, lin1_ws, lin1_wv, fc_w1, fc_w2, sc_ws, sc_wv, lin2_ws, lin2_wv, edge_src, edge_dst):
            n = node_features.shape[0]
            s = node_features[:, :S_IN]
            v = node_features[:, S_IN:].reshape(n, V_IN, 3)
            a = node_attr
            sc_s = s @ sc_ws * a * _inv(S_IN)
            sc_v = jnp.einsum('nci,cd->ndi', v, sc_wv) * a[:, :, None] * _inv(V_IN)
            h_s = s @ lin1_ws * a * _inv(S_IN)
            h_v = jnp.einsum('nci,cd->ndi', v, lin1_wv) * a[:, :, None] * _inv(V_IN)
            hid = jax.nn.silu(edge_scalars @ fc_w1 * _inv(R))
            w = hid @ fc_w2 * _inv(FC_HID)
            w1, w2, w3, w4, w5 = jnp.split(w, [64, 128, 160, 192], axis=-1)
            es = h_s[edge_src]
            ev = h_v[edge_src]
            e0 = edge_attr[:, :1]
            e1 = edge_attr[:, 1:4]
            m_s1 = w1 * es * e0
            m_s2 = w4 * jnp.einsum('eci,ei->ec', ev, e1) * _inv(3)
            m_v1 = (w2 * es)[:, :, None] * e1[:, None, :]
            m_v2 = w3[:, :, None] * ev * e0[:, :, None]
            m_v3 = w5[:, :, None] * jnp.cross(ev, e1[:, None, :]) * _inv(2)
            mid_s = jnp.concatenate([m_s1, m_s2], axis=-1)
            mid_v = jnp.concatenate([m_v1, m_v2, m_v3], axis=1)
            inv_nn = 1.0 / jnp.sqrt(jnp.float32(NUM_NEIGHBORS))
            agg_s = jax.ops.segment_sum(mid_s, edge_dst, num_segments=n) * inv_nn
            agg_v = jax.ops.segment_sum(mid_v, edge_dst, num_segments=n) * inv_nn
            o_s = agg_s @ lin2_ws * a * _inv(S_MID)
            o_v = jnp.einsum('nci,cd->ndi', agg_v, lin2_wv) * a[:, :, None] * _inv(V_MID)
            pre_s = sc_s + o_s
            pre_v = sc_v + o_v
            scalars = jax.nn.silu(pre_s[:, :64])
            gates = jax.nn.sigmoid(pre_s[:, 64:96])
            gated = gates[:, :, None] * pre_v
            return jnp.concatenate([scalars, gated.reshape(n, 3 * V_OUT)], axis=-1)
        return _forward(node_features, node_attr, edge_attr, edge_scalars, lin1_ws, lin1_wv, fc_w1, fc_w2, sc_ws, sc_wv, lin2_ws, lin2_wv, edge_src, edge_dst)
    edge_index = jnp.stack([src, dst])
    x = _layernorm(x + _L0_gnn_ref(x, edge_attr_16, edge_attr_4, L0_gnn_gamma_s, L0_gnn_beta_s, L0_gnn_gamma_v, L0_gnn_Ws_src, L0_gnn_Wv_src, L0_gnn_Ws_dst, L0_gnn_Wv_dst, L0_gnn_W_rbf, L0_gnn_W_alpha, L0_gnn_alpha_dot, L0_gnn_Ws_val, L0_gnn_Wv_val, L0_gnn_Wg, L0_gnn_w2_ss, L0_gnn_w2_sv, L0_gnn_w2_vs, L0_gnn_w2_vv0, L0_gnn_w2_vv1, L0_gnn_Ws_vlin, L0_gnn_Wv_vlin, L0_gnn_Wps, L0_gnn_Wpv, edge_index), axis=-1)
    x = _layernorm(x + _L1_gnn_ref(x, edge_attr_3, edge_attr_64, L1_gnn_W_skip0, L1_gnn_W_skip1, L1_gnn_W_nl0, L1_gnn_W_nl1, L1_gnn_W_fc1, L1_gnn_W_fc2, L1_gnn_W_out_s, L1_gnn_W_out_v, edge_index), axis=-1)
    x = _layernorm(x + _L2_gnn_ref(x, node_vec1, edge_attr_16, edge_attr_4, src, dst, L2_gnn_Wfc1, L2_gnn_Wfc2, L2_gnn_Wsc0, L2_gnn_Wsc1, L2_gnn_Wl1_0, L2_gnn_Wl1_1, L2_gnn_Wl2_s, L2_gnn_Wl2_v, L2_gnn_Wa), axis=-1)
    x = _layernorm(x + _L3_gnn_ref(x, node_vec1, src, dst, edge_attr_4, edge_attr_64, L3_gnn_lin1_ws, L3_gnn_lin1_wv, L3_gnn_fc_w1, L3_gnn_fc_w2, L3_gnn_sc_ws, L3_gnn_sc_wv, L3_gnn_lin2_ws, L3_gnn_lin2_wv), axis=-1)
    return x

_drawn_inputs = setup_inputs


def setup_inputs(seed=0):
    import zlib

    import numpy as np

    out = dict(_drawn_inputs(seed))
    spreads = {'L0_gnn_gamma_s': (1.0, 0.6), 'L0_gnn_beta_s': (0.0, 0.8), 'L0_gnn_gamma_v': (1.0, 0.6)}
    factors = {'L0_gnn_w2_vv1': 2.907,
     'L2_gnn_Wfc1': 8.0,
     'L2_gnn_Wfc2': 8.0,
     'L2_gnn_Wl1_0': 8.0,
     'L2_gnn_Wl1_1': 8.0,
     'L2_gnn_Wl2_s': 8.0,
     'L2_gnn_Wl2_v': 8.0,
     'L2_gnn_Wa': 8.0,
     'L2_gnn_Wsc0': 4.666,
     'L2_gnn_Wsc1': 4.333}
    for name, (base, spread) in spreads.items():
        noise = np.random.default_rng([zlib.crc32(name.encode()), seed]).standard_normal(out[name].shape)
        drawn = base * np.exp(spread * noise) if base else spread * noise
        out[name] = jnp.asarray(drawn.astype(out[name].dtype))
    for name, factor in factors.items():
        out[name] = (out[name] * factor).astype(out[name].dtype)
    return out
```

```python
import concourse.bass as bass
from concourse import mybir
from contextlib import ExitStack

P = 128
G = 2
F = 160
CS, CV = 64, 32
RD, RS = 86, 69
RW = 91
NEG = 1.0e30
EPS = 1e-5
R3, R2 = 3.0 ** 0.5, 2.0 ** 0.5


class Sig:

    def __init__(self, handle, per):
        self.h, self.per, self.base, self.total = handle, per, 0, 0

    def done(self, i, u, m=None):
        return i * (2 * self.per) + (self.base + 2 * self.per + u * self.per + (self.per if m is None else m))

    def free(self, i, u, slots=2):
        return i * (2 * self.per) + (self.base + 2 * self.per + u * self.per + self.per - slots * self.per)


class Mark:

    def __init__(self, handle):
        self.h, self.base, self.total = handle, 0, 0

    def at(self, k):
        return k + self.base


def sizes(n, e, ch):
    nb = -(-n // P)
    t = -(-e // (P * 2 * ch)) * 2 * ch
    pairs = (e + nb * (G * P - 1)) // (G * P)
    pairs += pairs % 2
    return nb, nb + nb % 2, t, pairs


def build(nc, ins, out, N, E, CH):
    fp32, i32 = mybir.dt.float32, mybir.dt.int32
    ALU, ACT, AX = mybir.AluOpType, mybir.ActivationFunctionType, mybir.AxisListType
    IOff = bass.IndirectOffsetOnAxis
    NB, NBX, T, NP = sizes(N, E, CH)
    LAST = N - (NB - 1) * P
    NCH = T // CH
    ACCW = max(NBX * 480, 16000)
    ctx = ExitStack()
    with ctx:
        def sb(name, shape, dt=fp32):
            return ctx.enter_context(nc.sbuf_tensor(name, shape, dt))

        def ps(name):
            return ctx.enter_context(nc.psum_tensor(name, [P, 512], fp32))

        def sem(name):
            return ctx.enter_context(nc.semaphore(name))

        fresh, known = [], {}

        def sig(name, per=1, steps=0):
            if name not in known:
                known[name] = Sig(sem(name), per)
                fresh.append(known[name])
            s = known[name]
            assert s.per == per
            s.base += s.total
            s.total = per * steps
            return s

        def mark(name, total):
            if name not in known:
                known[name] = Mark(sem(name))
            known[name].base += known[name].total
            known[name].total = total
            return known[name]

        def start(eng):
            while fresh:
                s = fresh.pop()
                eng.sem_inc(s.h, 2 * s.per)

        rec_dst = nc.dram_tensor("rec_dst", (NP * G * P, RD), fp32).ap()
        rec_src = nc.dram_tensor("rec_src", (NP * G * P, RS), fp32).ap()
        tables = [nc.dram_tensor(f"table{n}", (NBX * P, F), fp32).ap() for n in range(4)]
        rec_dst_v = rec_dst.rearrange("(i u p g) r -> i u p g r", u=2, g=G, p=P)
        rec_src_v = rec_src.rearrange("(i u p g) r -> i u p g r", u=2, g=G, p=P)
        tables_v = [t.rearrange("(i u p) f -> i u p f", u=2, p=P) for t in tables]

        X = sb("X", [P, NBX, F])
        ACC = sb("ACC", [P, ACCW])
        node_a = sb("node_a", [P, NBX])
        a_rows = sb("a_rows", [NBX, P])
        ident = sb("ident", [P, P])
        iota1 = sb("iota1", [P, P])
        ones = sb("ones", [P, P])
        tril = sb("tril", [P, P])
        pair_block = [sb(f"pair_block{s}", [1, NP], i32) for s in range(2)]
        bn6 = sb("bn6", [P, 2, 6])
        mean_var = sb("mean_var", [P, 2, 2])
        stat = sb("stat", [P, NBX, 2])
        rstd = sb("rstd", [P, NBX])
        vsq = sb("vsq", [P, NBX])
        rstd_v = sb("rstd_v", [P, NBX])

        w_specs = {
            "rbf0": (32, 448), "alpha0": (96, 160), "val0": (P, 32), "svlin0": (96, 64), "vvlin0": (P, 32),
            "proj0": (80, 320), "ts0": (64, 128), "tv0": (96, 192), "gam_s": (64, 1), "bet_s": (64, 1),
            "gam_v": (96, 1), "sc_s": (96, 1), "sc_v": (P, 1), "adr": (1, 64), "wg": (64, 32),
            "svT": (64, 96), "ad": (P, 64),
            "fc1_1": (P, P), "fc2_1": (P, 448), "ts1": (64, 64), "tv1": (96, 96),
            "xs1": (64, 96), "xv1": (96, 96), "os1": (96, 96), "ov1": (P, 32),
            "fc1_2": (32, P), "fc2_2": (P, 448), "ts2": (64, 64), "tv2": (96, 96),
            "xs2": (64, 64), "xv2": (96, 96), "os2": (96, 65), "ov2": (96, 32),
            "fc1_3": (P, P), "fc2_3": (P, 448), "ts3": (64, 64), "tv3": (96, 96),
            "xs3": (64, 96), "xv3": (96, 96), "os3": (96, 96), "ov3": (P, 32),
        }
        W = {k: sb("w_" + k, list(s)) for k, s in w_specs.items()}

        rec = sb("rec", [P, 2, G, 6])
        efr = sb("efr", [P, 2, G * 64])
        gat = sb("gat", [P, 2, G, F])
        oh = sb("oh", [P, 2, G, P])
        yx = sb("yx", [P, 2, G, 5])
        ysq = sb("ysq", [P, 2, G, 3])
        yn = sb("yn", [P, 2, G])
        yr = sb("yr", [P, 2, G])
        efT = sb("efT", [P, 2, P])
        hT = sb("hT", [P, 2, P])
        tp = sb("tp", [P, 2, G, 480])
        wy = sb("wy", [P, G, 96])
        t_sv = sb("t_sv", [P, G, 64])
        t_dot = sb("t_dot", [P, 2, G, 3, 32])
        t_cr = sb("t_cr", [P, 2, G, 3, 32])
        t_cr2 = sb("t_cr2", [P, G, 3, 32])
        t_cr3 = sb("t_cr3", [P, G, 3, 32])
        t_sum = sb("t_sum", [P, G, 32])
        t_sum2 = sb("t_sum2", [P, G, 32])
        mhalf = sb("mhalf", [P, G])
        msg = sb("msg", [P, 2, G, F])
        ohT = sb("ohT", [P, 2, G, P])
        mT = sb("mT", [P, G, 512])
        mTb = sb("mTb", [P, G, 512])
        th = sb("th", [P, 2, G, 96])
        th2 = sb("th2", [P, G, 96])
        la2 = sb("la2", [P, G, 64])
        lk = sb("lk", [P, G, 64])
        la = sb("la", [P, G, 64])
        a4 = sb("a4", [P, 2, G, 4])
        mb = sb("mb", [P, G, P])
        xm = sb("xm", [P, G, 4, P])
        tm = sb("tm", [P, 4])
        mnew = sb("mnew", [P, 2, 4])
        mdiff = sb("mdiff", [P, 2, 4])
        msc = sb("msc", [P, 2, 4])
        dlt = sb("dlt", [P, 2, G, 4])
        pex = sb("pex", [P, 2, G, 4])
        vsv = sb("vsv", [P, 2, G, F])
        hw = sb("hw", [P, 2, G, 164])
        xn = sb("xn", [P, 2, F])
        xT = sb("xT", [P, 2, 256])
        aT = mT
        accrow = tp[:, :, 0, :]
        tb = sb("tb", [P, 2, F])
        nrm = sb("nrm", [P, 2, 4])
        nrm2 = sb("nrm2", [P, 2, 4])
        y_s = sb("y_s", [P, 2, 160])
        sgm = sb("sgm", [P, 2, 96])

        BK = [ps(f"bank{k}") for k in range(8)]

        setup_zero = sem("setup_zero")
        weights_in = sem("weights_in")
        x_in = sem("x_in")
        const_ready = sem("const_ready")
        ramp_done = sem("ramp_done")
        fill_done = [sem("fill_dst_done"), sem("fill_src_done")]
        keys_in = sem("keys_in")
        wprep = sem("wprep")
        wpe = sem("wpe")

        ZP = max(d for d in range(1, 23) if NP % d == 0)
        ZCOL = ZP * G * RD
        zeros_t = ACC[:, ACCW - ZCOL:ACCW]
        o = [0]

        def scratch(cols):
            o[0] += cols
            return ACC[:, o[0] - cols:o[0]]

        raw = [scratch(T).bitcast(i32) for _ in range(2)]
        blki = scratch(T).bitcast(i32)
        loci = scratch(T).bitcast(i32)
        keyf = [scratch(T) for _ in range(2)]
        blkf = [scratch(T) for _ in range(2)]
        posi = [scratch(T).bitcast(i32) for _ in range(2)]
        posf = scratch(T)
        zrow = scratch(T)
        eqb = scratch(2 * T).rearrange("p (u t) -> p u t", u=2)
        scb = scratch(2 * T).rearrange("p (u t) -> p u t", u=2)
        tmb = scratch(2 * T).rearrange("p (u t) -> p u t", u=2)
        bidx = scratch(NBX)
        cnt = scratch(NBX)
        tot = scratch(NBX)
        toti = scratch(NBX).bitcast(i32)
        toti2 = scratch(NBX).bitcast(i32)
        prs = scratch(NBX)
        endp = scratch(NBX)
        offp = scratch(NBX)
        jrow = scratch(NP)
        blkacc = scratch(2 * NP).rearrange("p (u t) -> p u t", u=2)
        stage = scratch(2 * CH * RW).rearrange("p (u c r) -> p u c r", u=2, r=RW)
        sidx = scratch(4 * CH).bitcast(i32).rearrange("p (u s c) -> p u s c", u=2, s=2)
        assert o[0] <= ACCW - ZCOL

        attrs_v = ins["attrs"].rearrange("(p i u c) r -> p i u c r", p=P, u=2, c=CH)
        loads = []

        def load(dst, src):
            loads.append((dst, src))

        A = ins
        for g in range(G):
            load(W["rbf0"][16 * g:16 * g + 16, 224 * g:224 * g + 224], A["L0_gnn_W_rbf"])
            load(W["fc1_1"][64 * g:64 * g + 64, 64 * g:64 * g + 64], A["L1_gnn_W_fc1"])
            load(W["fc2_1"][64 * g:64 * g + 64, 224 * g:224 * g + 224], A["L1_gnn_W_fc2"])
            load(W["fc1_2"][16 * g:16 * g + 16, 64 * g:64 * g + 64], A["L2_gnn_Wfc1"])
            load(W["fc2_2"][64 * g:64 * g + 64, 224 * g:224 * g + 192], A["L2_gnn_Wfc2"])
            load(W["fc1_3"][64 * g:64 * g + 64, 64 * g:64 * g + 64], A["L3_gnn_fc_w1"])
            load(W["fc2_3"][64 * g:64 * g + 64, 224 * g:224 * g + 224], A["L3_gnn_fc_w2"])
        load(W["alpha0"][:, 0:64], A["L0_gnn_W_alpha"])
        load(W["alpha0"][:, 64:128], A["L0_gnn_Ws_val"])
        load(W["val0"][:, :], A["L0_gnn_Wv_val"])
        load(W["svlin0"][:, :], A["L0_gnn_Ws_vlin"])
        load(W["vvlin0"][:, :], A["L0_gnn_Wv_vlin"])
        for h in range(4):
            k, r = h // 2, 40 * (h % 2)
            load(W["proj0"][r:r + 16, 160 * k:160 * k + 64], A["L0_gnn_Wps"][16 * h:16 * h + 16, :])
            for i in range(3):
                load(W["proj0"][r + 16 + 8 * i:r + 24 + 8 * i, 160 * k + 64 + 32 * i:160 * k + 96 + 32 * i],
                     A["L0_gnn_Wpv"][8 * h:8 * h + 8, :])
        load(W["ts0"][:, 0:64], A["L0_gnn_Ws_src"])
        load(W["ts0"][:, 64:128], A["L0_gnn_Ws_dst"])
        for i in range(3):
            r = slice(32 * i, 32 * i + 32)
            load(W["tv0"][r, 32 * i:32 * i + 32], A["L0_gnn_Wv_src"])
            load(W["tv0"][r, 96 + 32 * i:128 + 32 * i], A["L0_gnn_Wv_dst"])
            load(W["gam_v"][r, :], A["L0_gnn_gamma_v"].rearrange("(c o) -> c o", o=1))
            load(W["tv1"][r, r], A["L1_gnn_W_nl1"])
            load(W["xv1"][r, r], A["L1_gnn_W_skip1"])
            load(W["tv2"][r, r], A["L2_gnn_Wl1_1"])
            load(W["xv2"][r, r], A["L2_gnn_Wsc1"])
            load(W["tv3"][r, r], A["L3_gnn_lin1_wv"])
            load(W["xv3"][r, r], A["L3_gnn_sc_wv"])
        load(W["gam_s"][:, :], A["L0_gnn_gamma_s"].rearrange("(c o) -> c o", o=1))
        load(W["bet_s"][:, :], A["L0_gnn_beta_s"].rearrange("(c o) -> c o", o=1))
        load(W["sc_s"][0:64, :], A["L0_gnn_w2_ss"].rearrange("(c o) -> c o", o=1))
        load(W["sc_s"][64:96, :], A["L0_gnn_w2_vv0"].rearrange("(c o) -> c o", o=1))
        load(W["sc_v"][0:64, :], A["L0_gnn_w2_sv"].rearrange("(c o) -> c o", o=1))
        load(W["sc_v"][64:96, :], A["L0_gnn_w2_vs"].rearrange("(c o) -> c o", o=1))
        load(W["sc_v"][96:128, :], A["L0_gnn_w2_vv1"].rearrange("(c o) -> c o", o=1))
        load(W["adr"][:, :], A["L0_gnn_alpha_dot"].rearrange("o h d -> o (h d)"))
        load(W["wg"][:, :], A["L0_gnn_Wg"])
        load(W["ts1"][:, :], A["L1_gnn_W_nl0"])
        load(W["xs1"][:, :], A["L1_gnn_W_skip0"])
        load(W["os1"][:, :], A["L1_gnn_W_out_s"])
        load(W["ov1"][:, :], A["L1_gnn_W_out_v"])
        load(W["ts2"][:, :], A["L2_gnn_Wl1_0"])
        load(W["xs2"][:, :], A["L2_gnn_Wsc0"])
        load(W["os2"][:, 0:64], A["L2_gnn_Wl2_s"])
        load(W["os2"][:, 64:65], A["L2_gnn_Wa"])
        load(W["ov2"][:, :], A["L2_gnn_Wl2_v"])
        load(W["ts3"][:, :], A["L3_gnn_lin1_ws"])
        load(W["xs3"][:, :], A["L3_gnn_sc_ws"])
        load(W["os3"][:, :], A["L3_gnn_lin2_ws"])
        load(W["ov3"][:, :], A["L3_gnn_lin2_wv"])
        zeroed = ["rbf0", "fc1_1", "fc2_1", "fc1_2", "fc2_2", "fc1_3", "fc2_3", "proj0", "tv0", "tv1", "xv1",
                  "tv2", "xv2", "tv3", "xv3"]
        NFILL = NP // ZP

        with nc.Block() as block:
            @block.sync
            def _(sp):
                sp.wait_ge(setup_zero, 1)
                sp.dma_start(X[:, :, :], A["x"].rearrange("(b p) f -> p b f", p=P)).then_inc(x_in, 16)
                sp.dma_start(a_rows[:, :], A["node_vec1"].rearrange("(b p) o -> b (p o)", p=P)).then_inc(x_in, 16)
                sp.dma_start(raw[0], A["dst"].rearrange("(p t) -> p t", p=P)).then_inc(keys_in, 16)
                sp.dma_start(raw[1], A["src"].rearrange("(p t) -> p t", p=P)).then_inc(keys_in, 16)
                for dst, src in loads:
                    sp.dma_start(dst, src, allow_slow_non_contiguous=dst.shape[-1] == 1).then_inc(weights_in, 16)
                sp.wait_ge(x_in, 32)
                sp.wait_ge(keys_in, 32)
                sp.wait_ge(weights_in, 16 * len(loads))

            @block.vector
            def _(ve):
                for k in zeroed:
                    nc.vector.memset(W[k][:, :], 0.0)
                nc.vector.memset(zrow, 0.0).then_inc(setup_zero, 1)
                nc.vector.memset(ones[:, :], 1.0).then_inc(const_ready, 1)

                def scale(name, r0, r1, by):
                    nc.vector.tensor_scalar_mul(W[name][r0:r1, :], W[name][r0:r1, :], by).then_inc(wprep, 1)

                ve.wait_ge(weights_in, 16 * len(loads))
                scale("os1", 0, 96, 1 / 32)
                scale("ov1", 0, 64, R3 / 32)
                scale("ov1", 64, 96, 1 / 32)
                scale("ov1", 96, 128, R3 / R2 / 32)
                scale("ts2", 0, 64, 1 / 8)
                scale("tv2", 0, 96, 32 ** -0.5)
                scale("xs2", 0, 64, 1 / 8)
                scale("xv2", 0, 96, 32 ** -0.5)
                scale("os2", 0, 64, 96 ** -0.5 / 8)
                scale("os2", 64, 96, 96 ** -0.5 / 8 / R3)
                scale("ov2", 0, 96, 96 ** -0.5 / 8)
                scale("ts3", 0, 64, 1 / 8)
                scale("tv3", 0, 96, 32 ** -0.5)
                scale("xs3", 0, 64, 1 / 8)
                scale("xv3", 0, 96, 32 ** -0.5)
                scale("os3", 0, 64, 96 ** -0.5 / 32)
                scale("os3", 64, 96, 96 ** -0.5 / 32 / R3)
                scale("ov3", 0, 96, 128 ** -0.5 / 32)
                scale("ov3", 96, 128, 128 ** -0.5 / 32 / R2)
                scale("sc_s", 64, 96, 1 / R3)
                scale("sc_v", 96, 128, 1 / R2)
                scale("val0", 96, 128, 1 / R2)
                n = 22
                ve.wait_ge(wprep, n)
                nc.vector.tensor_scalar_mul(W["svlin0"][:, :], W["svlin0"][:, :], W["sc_s"][:, :]).then_inc(wprep, 1)
                nc.vector.tensor_scalar_mul(W["vvlin0"][:, :], W["vvlin0"][:, :], W["sc_v"][:, :]).then_inc(wprep, 1)
                ve.wait_ge(wpe, 1)
                nc.vector.tensor_copy(W["svT"][:, :], BK[0][0:64, 0:96]).then_inc(wprep, 1)
                nc.vector.tensor_copy(W["ad"][:, :], BK[1][:, 0:64]).then_inc(wprep, 1)
                nc.vector.tensor_copy(node_a[:, :], BK[3][:, 0:NBX]).then_inc(wprep, 1)
                ve.wait_ge(wpe, 2)
                nc.vector.tensor_copy(W["alpha0"][:, 128:160], BK[2][0:96, 0:32]).then_inc(wprep, 1)
                ve.wait_ge(wprep, n + 6)
                scale("alpha0", 64, 96, 1 / R3)

            @block.gpsimd
            def _(po):
                nc.gpsimd.memset(ident[:, :], 0.0).then_inc(ramp_done, 1)
                nc.gpsimd.memset(tril[:, :], 1.0).then_inc(ramp_done, 1)
                nc.gpsimd.memset(mhalf[:, :], -0.5)
                po.wait_ge(ramp_done, 2)
                nc.gpsimd.affine_select(out=ident[:, :], in_=ident[:, :], compare_op=ALU.not_equal, fill=1.0,
                                        base=0, pattern=[[-1, P]], channel_multiplier=1).then_inc(ramp_done, 1)
                nc.gpsimd.affine_select(out=tril[:, :], in_=tril[:, :], compare_op=ALU.is_gt, fill=0.0,
                                        base=0, pattern=[[1, P]], channel_multiplier=-1).then_inc(ramp_done, 1)
                nc.gpsimd.iota(iota1[:, :], pattern=[[1, P]], base=1, channel_multiplier=0,
                               allow_small_or_imprecise_dtypes=True).then_inc(ramp_done, 1)
                nc.gpsimd.iota(bidx, pattern=[[1, NBX]], base=0, channel_multiplier=0,
                               allow_small_or_imprecise_dtypes=True).then_inc(ramp_done, 1)
                nc.gpsimd.iota(jrow, pattern=[[1, NP]], base=0, channel_multiplier=0,
                               allow_small_or_imprecise_dtypes=True).then_inc(ramp_done, 1)

            @block.tensor
            def _(pe):
                pe.wait_ge(ramp_done, 7)
                pe.wait_ge(const_ready, 1)
                pe.wait_ge(weights_in, 16 * len(loads))
                pe.wait_ge(x_in, 32)
                nc.tensor.transpose(BK[3][:, 0:NBX], a_rows[:, :], ident[0:NBX, 0:NBX])
                nc.tensor.transpose(BK[0][0:64, 0:96], W["alpha0"][:, 64:128], ident[0:96, 0:96])
                nc.tensor.matmul(BK[1][:, 0:64], ones[0:1, :], W["adr"][:, :], start=True, stop=True).then_inc(wpe, 1)
                pe.wait_ge(wprep, 26)
                nc.tensor.matmul(BK[2][0:96, 0:32], W["svT"][:, :], W["wg"][:, :], start=True, stop=True)\
                    .then_inc(wpe, 1)

        keys_split = sem("keys_split")
        pads_marked = sem("pads_marked")
        zero_tile = sem("zero_tile")
        hot = [sig(f"bucket_hot{s}") for s in range(2)]
        ranked = [sig(f"bucket_ranked{s}") for s in range(2)]
        picked = [sig(f"bucket_picked{s}") for s in range(2)]
        added = [sig(f"bucket_added{s}") for s in range(2)]
        shifted = [sig(f"bucket_shifted{s}") for s in range(2)]
        added2 = [sig(f"bucket_shift_added{s}") for s in range(2)]
        counted = sem("counted")
        off_step = sem("off_step")
        pos_done = sem("pos_done")
        pos_ready = sem("pos_ready")
        tbl_step = sem("tbl_step")
        pool_tick = sem("pool_tick")
        sp_tick = sem("sp_tick")
        ve_tick = sem("ve_tick")
        TH = [(0, min(512, T))] + ([(512, T)] if T > 512 else [])
        PADPOS = float(1 << 24)
        HB = NBX // 2
        with nc.Block() as block:
            @block.sync
            def _(sp):
                start(sp)
                sp.wait_ge(zero_tile, 1)
                for s, (r, w) in enumerate(((rec_dst, RD), (rec_src, RS))):
                    v = r.rearrange("(k p g) r -> k p (g r)", p=P, g=ZP * G)
                    for k in range(NFILL):
                        sp.dma_start(v[k], zeros_t[:, 0:ZP * G * w]).then_inc(fill_done[s], 16)
                for s in range(2):
                    sp.wait_ge(fill_done[s], 16 * NFILL)

            @block.vector
            def _(ve):
                nc.vector.memset(zeros_t, 0.0).then_inc(zero_tile, 1)
                for s in range(2):
                    if s:
                        ve.wait_ge(keys_split, 4)
                    nc.vector.tensor_scalar(blki, raw[s], 7, None, ALU.logical_shift_right).then_inc(keys_split, 1)
                    nc.vector.tensor_scalar(loci, raw[s], 127, None, ALU.bitwise_and).then_inc(keys_split, 1)
                    ve.wait_ge(keys_split, 4 * s + 2)
                    nc.vector.tensor_copy(blkf[s], blki).then_inc(keys_split, 1)
                    nc.vector.tensor_scalar_add(keyf[s], loci, 1.0).then_inc(keys_split, 1)

                for s in range(2):
                    ve.wait_ge(pads_marked, s + 1)
                    with ve.Fori(0, HB) as i:
                        for u in range(2):
                            b = bass.ds(i * 2 + u, 1)
                            ve.wait_ge(picked[s].h, picked[s].free(i, u))
                            nc.vector.tensor_scalar(eqb[:, u, :], blkf[s], bidx[:, b], None, ALU.is_equal)\
                                .then_inc(hot[s].h, 1)
                            ve.wait_ge(hot[s].h, hot[s].done(i, u))
                            nc.vector.tensor_tensor_scan(scb[:, u, :], eqb[:, u, :], zrow, 0.0, ALU.add, ALU.add)\
                                .then_inc(ranked[s].h, 1)
                            ve.wait_ge(ranked[s].h, ranked[s].done(i, u))
                            nc.vector.tensor_copy(cnt[:, b], scb[:, u, T - 1:T]).then_inc(counted, 1)
                    c = 9 * s
                    ve.wait_ge(off_step, c + 1)
                    nc.vector.tensor_copy(tot, BK[7][:, 0:NBX]).then_inc(off_step, 1)
                    ve.wait_ge(off_step, c + 2)
                    nc.vector.tensor_scalar_add(toti, tot, float(G * P - 1)).then_inc(off_step, 1)
                    ve.wait_ge(off_step, c + 3)
                    nc.vector.tensor_scalar(toti2, toti, 8, None, ALU.logical_shift_right).then_inc(off_step, 1)
                    ve.wait_ge(off_step, c + 4)
                    nc.vector.tensor_copy(prs, toti2).then_inc(off_step, 1)
                    ve.wait_ge(off_step, c + 5)
                    nc.vector.tensor_tensor_scan(endp, prs, zrow[:, 0:NBX], 0.0, ALU.add, ALU.add)\
                        .then_inc(off_step, 1)
                    ve.wait_ge(off_step, c + 6)
                    nc.vector.tensor_tensor(offp, endp, prs, ALU.subtract).then_inc(off_step, 1)
                    ve.wait_ge(off_step, c + 7)
                    nc.vector.tensor_scalar(offp, offp, float(G * P), -1.0, ALU.mult, ALU.add).then_inc(off_step, 1)
                    ve.wait_ge(off_step, c + 8)
                    nc.vector.tensor_tensor(offp, offp, BK[7][:, 64:64 + NBX], ALU.add).then_inc(off_step, 1)
                    ve.wait_ge(off_step, c + 9)
                    ve.wait_ge(picked[s].h, picked[s].done(HB - 1, 1))
                    with ve.Fori(0, HB) as i:
                        for u in range(2):
                            b = bass.ds(i * 2 + u, 1)
                            ve.wait_ge(added2[s].h, added2[s].free(i, u))
                            nc.vector.tensor_scalar(eqb[:, u, :], blkf[s], bidx[:, b], offp[:, b],
                                                    ALU.is_equal, ALU.mult).then_inc(shifted[s].h, 1)
                    ve.wait_ge(added2[s].h, added2[s].done(HB - 1, 1) + 1)
                    if s:
                        ve.wait_ge(pos_ready, 1)
                    for lo, hi in TH:
                        nc.vector.tensor_copy(posf[:, lo:hi], BK[2 * s + (lo > 0)][:, 0:hi - lo]).then_inc(pos_done, 1)
                    nc.vector.memset(blkacc[:, 0, :], 0.0).then_inc(tbl_step, 1)
                    for b in range(NB):
                        ve.wait_ge(tbl_step, s * (NB + 2) + b + 1)
                        nc.vector.scalar_tensor_tensor(blkacc[:, (b + 1) % 2, :], jrow, endp[:, b:b + 1],
                                                       blkacc[:, b % 2, :], ALU.is_ge, ALU.add).then_inc(tbl_step, 1)
                    ve.wait_ge(tbl_step, s * (NB + 2) + NB + 1)
                    nc.vector.tensor_scalar_min(pair_block[s][:, :], blkacc[0:1, NB % 2, :], float(NB - 1))\
                        .then_inc(tbl_step, 1)
                    ve.wait_ge(pads_marked, 3 + s)
                    nc.vector.tensor_copy(posi[s], posf).then_inc(pos_ready, 1)
                    ve.wait_ge(tbl_step, (s + 1) * (NB + 2))

            @block.gpsimd
            def _(po):
                for s in range(2):
                    po.wait_ge(keys_split, 4 * s + 4)
                    nc.gpsimd.affine_select(out=blkf[s], in_=blkf[s], compare_op=ALU.is_ge, fill=float(NBX),
                                            base=E - 1, pattern=[[-1, T]], channel_multiplier=-T)\
                        .then_inc(pads_marked, 1)
                for s in range(2):
                    with po.Fori(0, HB) as i:
                        for u in range(2):
                            po.wait_ge(ranked[s].h, ranked[s].done(i, u))
                            po.sem_inc(pool_tick, 1)
                            po.wait_ge(added[s].h, added[s].free(i, u))
                            nc.gpsimd.tensor_tensor(tmb[:, u, :], eqb[:, u, :], scb[:, u, :], ALU.mult)\
                                .then_inc(picked[s].h, 1)
                    po.wait_ge(pos_done, len(TH) * (s + 1))
                    nc.gpsimd.affine_select(out=posf, in_=posf, compare_op=ALU.is_ge, fill=PADPOS,
                                            base=E - 1, pattern=[[-1, T]], channel_multiplier=-T)\
                        .then_inc(pads_marked, 1)

            @block.tensor
            def _(pe):
                for s in range(2):
                    def add(rows, **kw):
                        for n, (lo, hi) in enumerate(TH):
                            last = nc.tensor.matmul(BK[2 * s + n][:, 0:hi - lo], ident[:, :], rows[:, lo:hi], **kw)
                        return last

                    add(zrow, start=True, stop=False)
                    with pe.Fori(0, HB) as i:
                        for u in range(2):
                            pe.wait_ge(picked[s].h, picked[s].done(i, u))
                            add(tmb[:, u, :], start=False, stop=False).then_inc(added[s].h, 1)
                    pe.wait_ge(counted, NBX * (s + 1))
                    nc.tensor.matmul(BK[7][:, 0:NBX], ones[:, :], cnt, start=True, stop=True)
                    nc.tensor.matmul(BK[7][:, 64:64 + NBX], tril[:, :], cnt, start=True, stop=True)\
                        .then_inc(off_step, 1)
                    with pe.Fori(0, HB) as i:
                        for u in range(2):
                            pe.wait_ge(shifted[s].h, shifted[s].done(i, u))
                            add(eqb[:, u, :], start=False, stop=False).then_inc(added2[s].h, 1)
                    add(zrow, start=False, stop=True).then_inc(added2[s].h, 1)

        attr_in = [sem(f"attr_in{u}") for u in range(2)]
        placed = [sem(f"placed{u}") for u in range(2)]
        staged = sig("staged")
        stage_i = stage.bitcast(i32)
        with nc.Block() as block:
            @block.sync
            def _(sp):
                start(sp)

                def attr(i, u, first):
                    if not first:
                        sp.wait_ge(placed[u], i * (32 * CH))
                        sp.sem_inc(sp_tick, 1)
                    sp.dma_start(stage[:, u, :, 2:89], attrs_v[:, i, u, :, :]).then_inc(attr_in[u], 16)

                for u in range(2):
                    attr(0, u, True)
                with sp.Fori(1, NCH // 2) as i:
                    for u in range(2):
                        attr(i, u, False)

            @block.vector
            def _(ve):
                def fields(i, u, first):
                    if not first:
                        ve.wait_ge(placed[u], i * (32 * CH))
                    c = bass.ds(i * (2 * CH) + u * CH, CH)
                    nc.vector.tensor_copy(stage[:, u, :, 0], keyf[0][:, c])
                    nc.vector.tensor_copy(stage_i[:, u, :, 1], raw[1][:, c])
                    nc.vector.tensor_copy(stage_i[:, u, :, 89], raw[0][:, c])
                    nc.vector.tensor_copy(stage[:, u, :, 90], keyf[1][:, c])
                    nc.vector.tensor_copy(sidx[:, u, 0, :], posi[0][:, c])
                    nc.vector.tensor_copy(sidx[:, u, 1, :], posi[1][:, c]).then_inc(staged.h, 1)

                for u in range(2):
                    fields(0, u, True)
                with ve.Fori(1, NCH // 2) as i:
                    for u in range(2):
                        fields(i, u, False)

            @block.gpsimd
            def _(po):
                with po.Fori(0, NCH // 2) as i:
                    for u in range(2):
                        po.wait_ge(attr_in[u], i * 16 + 16)
                        po.sem_inc(pool_tick, 1)
                        po.wait_ge(staged.h, staged.done(i, u))
                        po.sem_inc(pool_tick, 1)
                        for c in range(CH):
                            for s, table, lo, w in ((0, rec_dst, 0, RD), (1, rec_src, 22, RS)):
                                nc.gpsimd.indirect_dma_start(
                                    out=table[:, :], out_offset=IOff(ap=sidx[:, u, s, c:c + 1], axis=0),
                                    in_=stage[:, u, c, lo:lo + w], in_offset=None,
                                    bounds_check=NP * G * P - 1, oob_is_err=False).then_inc(placed[u], 16)
                for u in range(2):
                    po.wait_ge(placed[u], (NCH // 2) * 32 * CH)



        def product_pool(L, sv, u, slot):
            v = sv[:, :, 64:160].rearrange("p g (i c) -> p g i c", i=3)

            def bc(lo, hi):
                return yx[:, u, :, lo:hi].unsqueeze(3).to_broadcast([P, G, hi - lo, 32])
            if L.cross:
                for g in range(G):
                    nc.gpsimd.tensor_tensor(t_cr[:, slot, g, 0:2, :], v[:, g, 1:3, :], bc(2, 4)[:, g], ALU.mult)
                nc.gpsimd.tensor_tensor(t_cr[:, slot, :, 2, :], v[:, :, 0, :], bc(4, 5)[:, :, 0], ALU.mult)
            for g in range(G):
                last = nc.gpsimd.tensor_tensor(t_dot[:, slot, g], v[:, g], bc(0, 3)[:, g], ALU.mult)
            return last

        def product_vector(ve, L, i, u, sv, w, y0, slot, pooled, part1, part2):
            s, v = sv[:, :, 0:64], sv[:, :, 64:160].rearrange("p g (i c) -> p g i c", i=3)
            t = tp[:, u]
            tv = t[:, :, 96:96 + 3 * L.vs].rearrange("p g (i f) -> p g i f", i=3)

            def bc(lo, hi, c):
                return yx[:, u, :, lo:hi].unsqueeze(3).to_broadcast([P, G, hi - lo, c])

            def axes(a, c):
                return a.unsqueeze(2).to_broadcast([P, G, 3, c])

            if w is None:
                ws, wsv, wv = y0.to_broadcast([P, G, 64]), s, y0.to_broadcast([P, G, 32])
            elif y0 is None:
                ws, wsv, wv = w[:, :, 0:64], t_sv[:, :, :], w[:, :, 128:160]
            else:
                ws, wsv, wv = wy[:, :, 0:64], t_sv[:, :, :], wy[:, :, 64:96]
                nc.vector.tensor_tensor(ws, w[:, :, 0:64], y0.to_broadcast([P, G, 64]), ALU.mult)
                nc.vector.tensor_tensor(wv, w[:, :, 128:160], y0.to_broadcast([P, G, 32]), ALU.mult)
            if w is not None:
                nc.vector.tensor_tensor(wsv, w[:, :, 64:128], s, ALU.mult)
            if L.cross:
                nc.vector.tensor_tensor(t_cr2[:, :, 0:1, :], v[:, :, 2:3, :], bc(1, 2, 32), ALU.mult)
                nc.vector.tensor_tensor(t_cr2[:, :, 1:3, :], v[:, :, 0:2, :], bc(2, 4, 32), ALU.mult)
            ve.wait_ge(pooled.h, pooled.done(i, u))
            nc.vector.tensor_tensor(t_sum[:, :, :], t_dot[:, slot, :, 0, :], t_dot[:, slot, :, 1, :], ALU.add)\
                .then_inc(part1.h, 1)
            ve.wait_ge(part1.h, part1.done(i, u))
            dot = t[:, :, 64:96] if w is None else t_sum2[:, :, :]
            nc.vector.tensor_tensor(dot, t_sum[:, :, :], t_dot[:, slot, :, 2, :], ALU.add)
            if L.cross:
                cr = tv[:, :, :, 96:128] if w is None else t_cr3[:, :, :, :]
                nc.vector.tensor_tensor(cr, t_cr[:, slot], t_cr2[:, :, :, :], ALU.subtract)
            nc.vector.tensor_tensor(t[:, :, 0:64], ws, s, ALU.mult)
            nc.vector.tensor_tensor(tv[:, :, :, 0:64], axes(wsv, 64), bc(0, 3, 64), ALU.mult)
            last = nc.vector.tensor_tensor(tv[:, :, :, 64:96], v, axes(wv, 32), ALU.mult)
            if w is None:
                return last
            last.then_inc(part2.h, 1)
            ve.wait_ge(part2.h, part2.done(i, u))
            if L.cross:
                nc.vector.tensor_tensor(tv[:, :, :, 96:128], t_cr3[:, :, :, :], axes(w[:, :, 192:224], 32), ALU.mult)
            return nc.vector.tensor_tensor(t[:, :, 64:96], t_sum2[:, :, :], w[:, :, 160:192], ALU.mult)

        def directions(po, L, i, u, y_step, y_ready):
            r = rec[:, u, :, L.y:L.y + 3]
            k = [0]

            def step(ins):
                k[0] += 1
                ins.then_inc(y_step.h, 1)
                po.wait_ge(y_step.h, y_step.done(i, u, k[0]))
                po.sem_inc(pool_tick, 1)

            if L.n == 1:
                step(nc.gpsimd.tensor_tensor(ysq[:, u], r, r, ALU.mult))
                step(nc.gpsimd.tensor_tensor(yn[:, u], ysq[:, u, :, 0], ysq[:, u, :, 1], ALU.add))
                step(nc.gpsimd.tensor_tensor(yr[:, u], yn[:, u], ysq[:, u, :, 2], ALU.add))
                step(nc.gpsimd.tensor_scalar(yn[:, u], rec[:, u, :, L.key], 0.0, None, ALU.is_equal))
                step(nc.gpsimd.tensor_tensor(yr[:, u], yr[:, u], yn[:, u], ALU.add))
                step(nc.gpsimd.tensor_tensor(yn[:, u], yr[:, u], mhalf[:, :], ALU.pow))
                step(nc.gpsimd.tensor_tensor(yx[:, u, :, 0:3], r, yn[:, u].unsqueeze(2).to_broadcast([P, G, 3]),
                                             ALU.mult))
                nc.gpsimd.tensor_copy(yx[:, u, :, 3:5], yx[:, u, :, 0:2]).then_inc(y_ready.h, 1)
            else:
                nc.gpsimd.tensor_copy(yx[:, u, :, 0:3], r)
                nc.gpsimd.tensor_copy(yx[:, u, :, 3:5], rec[:, u, :, L.y:L.y + 2]).then_inc(y_ready.h, 1)

        class Layer:
            pass

        def layer(n):
            L = Layer()
            L.n = n
            L.src_order = n == 1
            L.records = rec_src_v if n == 1 else rec_dst_v
            L.head = (64, 5) if n == 1 else (0, 6)
            L.ef, L.efw = {0: (6, 16), 1: (0, 64), 2: (6, 16), 3: (22, 64)}[n]
            L.idx, L.key, L.y = (3, 4, 0) if n == 1 else (1, 0, 3)
            L.y0 = None if n == 1 else 2
            L.cross = n != 2
            L.vs = 128 if L.cross else 96
            L.width = 96 + 3 * L.vs + (n == 2)
            L.blocks = pair_block[1 if n == 1 else 0]
            return L

        def load_records(sp, L, i, u, done):
            lo, w = L.head
            sp.dma_start(rec[:, u, :, 0:w], L.records[i, u, :, :, lo:lo + w]).then_inc(done, 16)
            sp.dma_start(efr[:, u, 0:G * L.efw].rearrange("p (g f) -> p g f", g=G),
                         L.records[i, u, :, :, L.ef:L.ef + L.efw]).then_inc(done, 16)

        def edge_loop(L):
            rec_in = [mark(f"rec_in{u}", 32 * (NP // 2)) for u in range(2)]
            gat_in = [mark(f"gat_in{u}", 32 * (NP // 2)) for u in range(2)]
            y_ready = sig("y_ready", 1, NP)
            y_step = sig("y_step", 7, NP if L.n == 1 else 0)
            pooled = sig("pooled", 1, NP)
            ef_t = sig("ef_t", 1, NP)
            ef_ready = sig("ef_ready", 1, NP)
            hid = sig("hid", 1, NP)
            hid_ready = sig("hid_ready", 1, NP)
            w_ready = sig("w_ready", 1, NP)
            part1 = sig("part1", 1, NP)
            part2 = sig("part2", 1, NP)
            tp_ready = sig("tp_ready", 1, NP)
            summed = sig("summed", 1, NP)
            kept = sig("kept", 1, NP)
            zeroed = mark("sums_zeroed", 1 + (L.n == 2))
            TW = L.width
            HALF = NP // 2
            fc1, fc2 = W[f"fc1_{L.n}"], W[f"fc2_{L.n}"]
            EW = G * L.efw
            pE, pH, pW, pS = BK[0], BK[1], [BK[2], BK[3]], [BK[4], BK[5]]

            def w_of(u):
                return pW[u][:, 0:448].rearrange("p (g f) -> p g f", g=G)

            with nc.Block() as block:
                @block.sync
                def _(sp):
                    start(sp)

                    def records(i, u, first=False):
                        if not first:
                            sp.wait_ge(tp_ready.h, tp_ready.free(i, u))
                            sp.sem_inc(sp_tick, 1)
                        load_records(sp, L, i, u, rec_in[u].h)

                    for u in range(2):
                        records(0, u, True)
                    with sp.Fori(1, HALF) as i:
                        for u in range(2):
                            records(i, u)

                @block.gpsimd
                def _(po):
                    if L.n == 2:
                        nc.gpsimd.memset(tp[:, :, :, 384:385], 1.0).then_inc(zeroed.h, 1)

                    def gather(i, u):
                        po.wait_ge(rec_in[u].h, rec_in[u].at(i * 32 + 32))
                        po.sem_inc(pool_tick, 1)
                        po.wait_ge(tp_ready.h, tp_ready.free(i, u))
                        po.sem_inc(pool_tick, 1)
                        for g in range(G):
                            nc.gpsimd.indirect_dma_start(
                                out=gat[:, u, g, :], out_offset=None, in_=tables[L.n][:, :],
                                in_offset=IOff(ap=rec[:, u, g, L.idx:L.idx + 1].bitcast(i32), axis=0))\
                                .then_inc(gat_in[u].h, 16)
                        directions(po, L, i, u, y_step, y_ready)

                    def part(i, u):
                        po.wait_ge(gat_in[u].h, gat_in[u].at(i * 32 + 32))
                        po.sem_inc(pool_tick, 1)
                        po.wait_ge(y_ready.h, y_ready.done(i, u))
                        product_pool(L, gat[:, u], u, u).then_inc(pooled.h, 1)

                    gather(0, 0)
                    gather(0, 1)
                    with po.Fori(0, HALF - 1) as i:
                        for u in range(2):
                            part(i, u)
                            gather(i + 1, u)
                    part(HALF - 1, 0)
                    part(HALF - 1, 1)

                @block.scalar
                def _(ac):
                    def front(i, u):
                        ac.wait_ge(ef_t.h, ef_t.done(i, u))
                        nc.scalar.activation(efT[0:EW, u, :], pE[0:EW, 128 * u:128 * u + 128], ACT.Copy)\
                            .then_inc(ef_ready.h, 1)
                        ac.wait_ge(hid.h, hid.done(i, u))
                        func, by = {1: (ACT.Relu, 1.0), 2: (ACT.Silu, 0.25), 3: (ACT.Silu, 0.125)}[L.n]
                        nc.scalar.activation(hT[:, u, :], pH[:, 128 * u:128 * u + 128], func, scale=by)\
                            .then_inc(hid_ready.h, 1)

                    with ac.Fori(0, HALF) as i:
                        for u in range(2):
                            front(i, u)

                @block.tensor
                def _(pe):
                    def transposed(i, u):
                        pe.wait_ge(rec_in[u].h, rec_in[u].at(i * 32 + 32))
                        pe.wait_ge(ef_ready.h, ef_ready.free(i, u))
                        nc.tensor.transpose(pE[0:EW, 128 * u:128 * u + 128], efr[:, u, 0:G * L.efw],
                                            ident[:, :]).then_inc(ef_t.h, 1)

                    def hidden(i, u):
                        pe.wait_ge(ef_ready.h, ef_ready.done(i, u))
                        pe.wait_ge(hid_ready.h, hid_ready.free(i, u))
                        nc.tensor.matmul(pH[:, 128 * u:128 * u + 128], fc1[0:EW, :], efT[0:EW, u, :],
                                         start=True, stop=True).then_inc(hid.h, 1)

                    def weights(i, u):
                        pe.wait_ge(hid_ready.h, hid_ready.done(i, u))
                        pe.wait_ge(tp_ready.h, tp_ready.free(i, u))
                        nc.tensor.matmul(pW[u][:, 0:448], hT[:, u, :], fc2[:, :], start=True, stop=True)\
                            .then_inc(w_ready.h, 1)

                    def sums(i, u, g):
                        if g == 0:
                            pe.wait_ge(tp_ready.h, tp_ready.done(i, u))
                            pe.wait_ge(kept.h, kept.free(i, u))
                        last = nc.tensor.matmul(pS[u][:, 0:TW], oh[:, u, g, :], tp[:, u, g, 0:TW],
                                                start=g == 0, stop=g == G - 1)
                        if g == G - 1:
                            last.then_inc(summed.h, 1)

                    for u in range(2):
                        transposed(0, u)
                        hidden(0, u)
                        weights(0, u)
                    with pe.Fori(0, HALF - 1) as i:
                        for u in range(2):
                            transposed(i + 1, u)
                            sums(i, u, 0)
                            hidden(i + 1, u)
                            sums(i, u, 1)
                            weights(i + 1, u)
                    for u in range(2):
                        for g in range(G):
                            sums(HALF - 1, u, g)

                @block.vector
                def _(ve):
                    nc.vector.memset(ACC[:, 0:NBX * TW], 0.0).then_inc(zeroed.h, 1)
                    acc = ACC[:, 0:NBX * TW].rearrange("p (b f) -> p b f", b=NBX)

                    def product(i, u):
                        ve.wait_ge(rec_in[u].h, rec_in[u].at(i * 32 + 32))
                        ve.wait_ge(summed.h, summed.free(i, u))
                        for g in range(G):
                            nc.vector.tensor_scalar(oh[:, u, g, :], iota1[:, :], rec[:, u, g, L.key:L.key + 1],
                                                    None, ALU.is_equal)
                        ve.wait_ge(w_ready.h, w_ready.done(i, u))
                        ve.wait_ge(gat_in[u].h, gat_in[u].at(i * 32 + 32))
                        ve.wait_ge(y_ready.h, y_ready.done(i, u))
                        y0 = None if L.y0 is None else rec[:, u, :, L.y0:L.y0 + 1]
                        product_vector(ve, L, i, u, gat[:, u], w_of(u), y0, u, pooled, part1, part2)\
                            .then_inc(tp_ready.h, 1)

                    def keep(i, u):
                        ve.wait_ge(summed.h, summed.done(i, u))
                        b = ve.value_load(L.blocks[0:1, bass.ds(i * 2 + u, 1)], min_val=0, max_val=NB - 1)
                        row = acc[:, bass.ds(b, 1), :].rearrange("p o f -> p (o f)")
                        ve.wait_ge(kept.h, kept.free(i, u, 1))
                        nc.vector.tensor_tensor(row, row, pS[u][:, 0:TW], ALU.add).then_inc(kept.h, 1)

                    ve.wait_ge(zeroed.h, zeroed.at(1 + (L.n == 2)))
                    product(0, 0)
                    with ve.Fori(0, HALF - 1) as i:
                        product(i, 1)
                        keep(i, 0)
                        product(i + 1, 0)
                        keep(i, 1)
                    product(HALF - 1, 1)
                    keep(HALF - 1, 0)
                    keep(HALF - 1, 1)
                    ve.wait_ge(kept.h, kept.done(HALF - 1, 1))

        HNB = NBX // 2

        def node_table(n):
            rows = sig("rows", 1, NBX)
            rows_t = sig("rows_t", 1, NBX)
            rowsT = sig("rowsT", 1, NBX)
            made = sig("made", 1, NBX)
            tb_ready = sig("tb_ready", 1, NBX)
            normed = sig("normed", 1, NBX if n else 0)
            rooted = mark("rooted", 1 if n else 2)
            rstd_ready = mark("rstd_ready", 2 if n else 3)
            stored = [mark(f"stored{u}", 16 * (NBX // 2)) for u in range(2)]
            ts, tv_ = W[f"ts{n}"], W[f"tv{n}"]
            SW, VW = (128, 192) if n == 0 else (64, 96)
            TD = ACC[:, 8400:8400 + NBX * F].rearrange("p (b f) -> p b f", b=NBX)
            pT, pM = [BK[0], BK[1]], [BK[2], BK[3]]
            with nc.Block() as block:
                @block.scalar
                def _(ac):
                    ac.wait_ge(rstd_ready.h, rstd_ready.at(1))
                    nc.scalar.activation(rstd[:, :], rstd[:, :], ACT.Sqrt).then_inc(rooted.h, 1)
                    if n == 0:
                        nc.scalar.activation(rstd_v[:, :], rstd_v[:, :], ACT.Sqrt).then_inc(rooted.h, 1)

                    def copies(i, u):
                        ac.wait_ge(rows_t.h, rows_t.done(i, u))
                        ac.wait_ge(made.h, made.free(i, u))
                        if n == 0:
                            nc.scalar.activation(xT[0:64, u, 0:128], pT[u][0:64, 0:128], ACT.Identity,
                                                 bias=W["bet_s"][:, :], scale=W["gam_s"][:, :])
                            nc.scalar.activation(xT[0:96, u, 128:256], pT[u][0:96, 128:256], ACT.Copy,
                                                 scale=W["gam_v"][:, :]).then_inc(rowsT.h, 1)
                        else:
                            nc.scalar.activation(xT[0:64, u, 0:128], pT[u][0:64, 0:128], ACT.Copy)
                            nc.scalar.activation(xT[0:96, u, 128:256], pT[u][0:96, 128:256], ACT.Copy)\
                                .then_inc(rowsT.h, 1)

                    with ac.Fori(0, HNB) as i:
                        for u in range(2):
                            copies(i, u)

                @block.vector
                def _(ve):
                    first = nc.vector.tensor_scalar_add(rstd[:, :], stat[:, :, 1], EPS)
                    if n != 0:
                        first.then_inc(rstd_ready.h, 1)
                    else:
                        nc.vector.tensor_scalar(rstd_v[:, :], vsq[:, :], 1.0 / CV, EPS, ALU.mult, ALU.add)\
                            .then_inc(rstd_ready.h, 1)
                    ve.wait_ge(rooted.h, rooted.at(2 if n == 0 else 1))
                    nc.vector.reciprocal(rstd[:, :], rstd[:, :]).then_inc(rstd_ready.h, 1)
                    if n == 0:
                        nc.vector.reciprocal(rstd_v[:, :], rstd_v[:, :]).then_inc(rstd_ready.h, 1)
                    ve.wait_ge(rstd_ready.h, rstd_ready.at(3 if n == 0 else 2))

                    def norm(i, u):
                        b = i * 2 + u
                        xb = X[:, bass.ds(b, 1), :].rearrange("p o f -> p (o f)")
                        mu = stat[:, bass.ds(b, 1), 0]
                        rs = rstd[:, bass.ds(b, 1)]
                        ve.wait_ge(rows_t.h, rows_t.free(i, u))
                        xv = xn[:, u, 64:160].rearrange("p (i c) -> p i c", i=3)
                        src = X[:, bass.ds(b, 1), 64:160].rearrange("p o (c i) -> p i (o c)", i=3)
                        if n == 0:
                            nc.vector.tensor_scalar(xn[:, u, 0:64], X[:, bass.ds(b, 1), 0:64].rearrange(
                                "p o f -> p (o f)"), mu, rs, ALU.subtract, ALU.mult)
                            nc.vector.tensor_scalar(xv, src, rstd_v[:, bass.ds(b, 1)], None, ALU.mult)\
                                .then_inc(rows.h, 1)
                        else:
                            nc.vector.tensor_scalar(xb, xb, mu, rs, ALU.subtract, ALU.mult).then_inc(normed.h, 1)
                            ve.wait_ge(normed.h, normed.done(i, u))
                            ve.sem_inc(ve_tick, 1)
                            nc.vector.tensor_copy(xn[:, u, 0:64], X[:, bass.ds(b, 1), 0:64].rearrange(
                                "p o f -> p (o f)"))
                            nc.vector.tensor_copy(xv, src).then_inc(rows.h, 1)

                    def table(i, u):
                        b = i * 2 + u
                        ve.wait_ge(made.h, made.done(i, u))
                        if not (isinstance(i, int) and i == 0):
                            ve.wait_ge(stored[u].h, stored[u].at(i * 16))
                            ve.sem_inc(ve_tick, 1)
                        if n == 0:
                            ve.sem_inc(ve_tick, 1)
                            nc.vector.tensor_copy(TD[:, bass.ds(b, 1), 0:64].rearrange("p o f -> p (o f)"),
                                                  pM[u][:, 64:128])
                            nc.vector.tensor_copy(TD[:, bass.ds(b, 1), 64:160].rearrange("p o f -> p (o f)"),
                                                  pM[u][:, 224:320])
                            nc.vector.tensor_copy(tb[:, u, 0:64], pM[u][:, 0:64])
                            nc.vector.tensor_copy(tb[:, u, 64:160], pM[u][:, 128:224]).then_inc(tb_ready.h, 1)
                        elif n == 1:
                            nc.vector.tensor_copy(tb[:, u, :], pM[u][:, 0:160]).then_inc(tb_ready.h, 1)
                        else:
                            nc.vector.tensor_scalar(tb[:, u, :], pM[u][:, 0:160], node_a[:, bass.ds(b, 1)], None,
                                                    ALU.mult).then_inc(tb_ready.h, 1)

                    norm(0, 0)
                    norm(0, 1)
                    table(0, 0)
                    table(0, 1)
                    with ve.Fori(1, HNB) as i:
                        norm(i, 0)
                        norm(i, 1)
                        table(i, 0)
                        table(i, 1)

                @block.tensor
                def _(pe):
                    def turn(i, u):
                        pe.wait_ge(rows.h, rows.done(i, u))
                        pe.wait_ge(rowsT.h, rowsT.free(i, u))
                        nc.tensor.transpose(pT[u][0:96, 128:256], xn[:, u, 64:160], ident[:, :])
                        nc.tensor.transpose(pT[u][0:64, 0:128], xn[:, u, 0:64], ident[:, :]).then_inc(rows_t.h, 1)

                    def make(i, u):
                        pe.wait_ge(rowsT.h, rowsT.done(i, u))
                        pe.wait_ge(tb_ready.h, tb_ready.free(i, u))
                        nc.tensor.matmul(pM[u][:, 0:SW], xT[0:64, u, 0:128], ts[:, :], start=True, stop=True)
                        nc.tensor.matmul(pM[u][:, SW:SW + VW], xT[0:96, u, 128:256], tv_[:, :], start=True, stop=True)\
                            .then_inc(made.h, 1)

                    with pe.Fori(0, HNB) as i:
                        for u in range(2):
                            turn(i, u)
                        for u in range(2):
                            make(i, u)

                @block.sync
                def _(sp):
                    start(sp)
                    with sp.Fori(0, HNB) as i:
                        for u in range(2):
                            sp.wait_ge(tb_ready.h, tb_ready.done(i, u))
                            sp.sem_inc(sp_tick, 1)
                            sp.dma_start(tables_v[n][i, u], tb[:, u, :]).then_inc(stored[u].h, 16)
                    for u in range(2):
                        sp.wait_ge(stored[u].h, stored[u].at(HNB * 16))

        def statistics(ve, i, u, cols, seen):
            b = i * 2 + u
            x = X[:, bass.ds(b, 1), 0:cols].rearrange("p o f -> p (o f)")
            nc.vector.bn_stats(bn6[:, u, :], x).then_inc(seen.h, 1)
            ve.wait_ge(seen.h, seen.done(i, u, 1))
            ve.sem_inc(ve_tick, 1)
            nc.vector.bn_aggr(mean_var[:, u, :], bn6[:, u, :]).then_inc(seen.h, 1)
            ve.wait_ge(seen.h, seen.done(i, u, 2))
            ve.sem_inc(ve_tick, 1)
            nc.vector.tensor_copy(stat[:, bass.ds(b, 1), :].rearrange("p o f -> p (o f)"), mean_var[:, u, :])

        def node_update(L):
            n = L.n
            copied_in = sig("copied_in", 1, NBX)
            turned = sig("turned", 1, NBX)
            copied = sig("copied", 1, NBX)
            made = sig("made", 1, NBX)
            gated = sig("gated_out", 1, NBX)
            upd = sig("upd", 3, NBX if n == 2 else 0)
            alpha_made = sig("alpha_made", 1, NBX if n == 2 else 0)
            y_made = sig("y_made", 1, NBX)
            updated = sig("updated", 1, NBX)
            seen = sig("seen", 2, NBX)
            pX_, pA, pO = [BK[0], BK[1]], [BK[2], BK[3]], [BK[4], BK[5]]
            TW, VS = L.width, L.vs
            acc = ACC[:, 0:NBX * TW].rearrange("p (b f) -> p b f", b=NBX)
            nS = 64 if n == 2 else 96
            with nc.Block() as block:
                @block.vector
                def _(ve):
                    def rows(i, u):
                        b = bass.ds(i * 2 + u, 1)
                        ve.wait_ge(turned.h, turned.free(i, u))
                        ve.sem_inc(ve_tick, 1)
                        if n == 2:
                            c = acc[:, b, 384:385].rearrange("p o f -> p (o f)")
                            nc.vector.tensor_scalar_max(nrm[:, u, 0:1], c, 1.0).then_inc(upd.h, 1)
                            ve.wait_ge(upd.h, upd.done(i, u, 1))
                            nc.vector.reciprocal(nrm[:, u, 1:2], nrm[:, u, 0:1]).then_inc(upd.h, 1)
                            ve.wait_ge(upd.h, upd.done(i, u, 2))
                            nc.vector.tensor_scalar(nrm[:, u, 2:3], nrm[:, u, 1:2], node_a[:, b], None, ALU.mult)\
                                .then_inc(upd.h, 1)
                            ve.wait_ge(upd.h, upd.done(i, u, 3))
                            ve.sem_inc(ve_tick, 1)
                        nc.vector.tensor_copy(xn[:, u, 64:160].rearrange("p (i c) -> p i c", i=3),
                                              X[:, b, 64:160].rearrange("p o (c i) -> p i (o c)", i=3))
                        nc.vector.tensor_copy(xn[:, u, 0:64], X[:, b, 0:64].rearrange("p o f -> p (o f)"))
                        a = acc[:, b, 0:96 + 3 * VS].rearrange("p o f -> p (o f)")
                        nc.vector.tensor_copy(accrow[:, u, 0:96 + 3 * VS], a).then_inc(copied_in.h, 1)

                    def outputs(i, u):
                        b = bass.ds(i * 2 + u, 1)
                        ys = y_s[:, u, 0:64]
                        yv = y_s[:, u, 64:160].rearrange("p (i c) -> p i c", i=3)
                        a = node_a[:, b]
                        if n == 2:
                            ve.wait_ge(made.h, made.done(i, u))
                            nc.vector.tensor_scalar(nrm[:, u, 3:4], pO[u][:, 224:225], nrm[:, u, 2:3], nrm[:, u, 2:3],
                                                    ALU.mult, ALU.mult).then_inc(alpha_made.h, 1)
                            ve.wait_ge(alpha_made.h, alpha_made.done(i, u))
                            nc.vector.tensor_scalar(y_s[:, u, 0:64], pO[u][:, 160:224], nrm[:, u, 3:4], None, ALU.mult)
                            nc.vector.tensor_scalar(y_s[:, u, 64:160], pO[u][:, 225:321], nrm[:, u, 3:4], None,
                                                    ALU.mult).then_inc(gated.h, 1)
                            ve.wait_ge(gated.h, gated.done(i, u))
                            nc.vector.scalar_tensor_tensor(y_s[:, u, :], pO[u][:, 0:160], a, y_s[:, u, :],
                                                           ALU.mult, ALU.add).then_inc(y_made.h, 1)
                            ve.wait_ge(y_made.h, y_made.done(i, u))
                        else:
                            ve.wait_ge(gated.h, gated.done(i, u))
                            by = a if n == 3 else 1.0
                            nc.vector.scalar_tensor_tensor(ys, pO[u][:, 0:64], by, sgm[:, u, 0:64],
                                                           ALU.mult, ALU.mult)
                            nc.vector.scalar_tensor_tensor(
                                yv, pO[u][:, 96:192].rearrange("p (i c) -> p i c", i=3), by,
                                sgm[:, u, 64:96].unsqueeze(1).to_broadcast([P, 3, 32]), ALU.mult, ALU.mult)\
                                .then_inc(y_made.h, 1)
                            ve.wait_ge(y_made.h, y_made.done(i, u))
                        xs = X[:, b, 0:64].rearrange("p o f -> p (o f)")
                        xv = X[:, b, 64:160].rearrange("p o (c i) -> p i (o c)", i=3)
                        nc.vector.tensor_tensor(xs, xs, ys, ALU.add)
                        nc.vector.tensor_tensor(xv, xv, yv, ALU.add).then_inc(updated.h, 1)
                        ve.wait_ge(updated.h, updated.done(i, u))
                        ve.sem_inc(ve_tick, 1)
                        statistics(ve, i, u, F, seen)

                    with ve.Fori(0, HNB) as i:
                        rows(i, 0)
                        rows(i, 1)
                        outputs(i, 0)
                        outputs(i, 1)

                @block.tensor
                def _(pe):
                    def turn(i, u):
                        pe.wait_ge(copied_in.h, copied_in.done(i, u))
                        pe.wait_ge(copied.h, copied.free(i, u))
                        nc.tensor.transpose(pX_[u][0:96, 128:256], xn[:, u, 64:160], ident[:, :])
                        nc.tensor.transpose(pX_[u][0:64, 0:128], xn[:, u, 0:64], ident[:, :])
                        nc.tensor.transpose(pA[u][0:96, 0:128], accrow[:, u, 0:96], ident[:, :])
                        for k in range(3):
                            last = nc.tensor.transpose(pA[u][0:VS, 128 * k + 128:128 * k + 256],
                                                       accrow[:, u, 96 + VS * k:96 + VS * k + VS], ident[:, :])
                        last.then_inc(turned.h, 1)

                    def make(i, u):
                        pe.wait_ge(copied.h, copied.done(i, u))
                        pe.wait_ge(updated.h, updated.free(i, u))
                        xs, xv, os_, ov = (W[k + str(n)] for k in ("xs", "xv", "os", "ov"))
                        o_ = pO[u]
                        if n == 2:
                            nc.tensor.matmul(o_[:, 0:64], xT[0:64, u, 0:128], xs[:, :], start=True, stop=True)
                            nc.tensor.matmul(o_[:, 64:160], xT[0:96, u, 128:256], xv[:, :], start=True, stop=True)
                            nc.tensor.matmul(o_[:, 160:225], aT[0:96, u, 0:128], os_[:, :], start=True, stop=True)
                            for k in range(3):
                                last = nc.tensor.matmul(o_[:, 225 + 32 * k:257 + 32 * k],
                                                        aT[0:96, u, 128 * k + 128:128 * k + 256], ov[:, :],
                                                        start=True, stop=True)
                        else:
                            nc.tensor.matmul(o_[:, 0:96], xT[0:64, u, 0:128], xs[:, :], start=True, stop=False)
                            nc.tensor.matmul(o_[:, 0:96], aT[0:96, u, 0:128], os_[:, :], start=False, stop=True)
                            for k in range(3):
                                oc = slice(96 + 32 * k, 128 + 32 * k)
                                nc.tensor.matmul(o_[:, oc], xT[0:96, u, 128:256], xv[:, 32 * k:32 * k + 32],
                                                 start=True, stop=False)
                                last = nc.tensor.matmul(o_[:, oc], aT[:, u, 128 * k + 128:128 * k + 256], ov[:, :],
                                                        start=False, stop=True)
                        last.then_inc(made.h, 1)

                    with pe.Fori(0, HNB) as i:
                        for u in range(2):
                            turn(i, u)
                        for u in range(2):
                            make(i, u)

                @block.scalar
                def _(ac):
                    with ac.Fori(0, HNB) as i:
                        for u in range(2):
                            ac.wait_ge(turned.h, turned.done(i, u))
                            ac.wait_ge(made.h, made.free(i, u))
                            nc.scalar.activation(xT[0:64, u, 0:128], pX_[u][0:64, 0:128], ACT.Copy)
                            nc.scalar.activation(xT[0:96, u, 128:256], pX_[u][0:96, 128:256], ACT.Copy)
                            nc.scalar.activation(aT[0:96, u, 0:128], pA[u][0:96, 0:128], ACT.Copy)
                            nc.scalar.activation(aT[0:VS, u, 128:512], pA[u][0:VS, 128:512], ACT.Copy)\
                                .then_inc(copied.h, 1)
                        for u in range(2):
                            if n == 2:
                                continue
                            ac.wait_ge(made.h, made.done(i, u))
                            ac.wait_ge(updated.h, updated.free(i, u))
                            by = node_a[:, bass.ds(i * 2 + u, 1)] if n == 3 else 1.0
                            nc.scalar.activation(sgm[:, u, :], pO[u][:, 0:96], ACT.Sigmoid, scale=by)\
                                .then_inc(gated.h, 1)

                @block.sync
                def _(sp):
                    start(sp)

        def last_norm():
            rooted = mark("rooted", 1)
            rstd_ready = mark("rstd_ready", 2)
            normed = sig("normed", 1, NBX)
            out_done = sem("out_done")
            with nc.Block() as block:
                @block.scalar
                def _(ac):
                    ac.wait_ge(rstd_ready.h, rstd_ready.at(1))
                    nc.scalar.activation(rstd[:, :], rstd[:, :], ACT.Sqrt).then_inc(rooted.h, 1)

                @block.vector
                def _(ve):
                    nc.vector.tensor_scalar_add(rstd[:, :], stat[:, :, 1], EPS).then_inc(rstd_ready.h, 1)
                    ve.wait_ge(rooted.h, rooted.at(1))
                    nc.vector.reciprocal(rstd[:, :], rstd[:, :]).then_inc(rstd_ready.h, 1)
                    ve.wait_ge(rstd_ready.h, rstd_ready.at(2))
                    with ve.Fori(0, HNB) as i:
                        for u in range(2):
                            b = bass.ds(i * 2 + u, 1)
                            xb = X[:, b, :].rearrange("p o f -> p (o f)")
                            nc.vector.tensor_scalar(xb, xb, stat[:, b, 0], rstd[:, b], ALU.subtract, ALU.mult)\
                                .then_inc(normed.h, 1)

                @block.sync
                def _(sp):
                    start(sp)
                    sp.wait_ge(normed.h, normed.done(HNB - 1, 1))
                    if NB > 1:
                        sp.dma_start(out[0:(NB - 1) * P, :].rearrange("(b p) f -> p b f", p=P), X[:, 0:NB - 1, :])\
                            .then_inc(out_done, 16)
                    sp.dma_start(out[(NB - 1) * P:N, :], X[0:LAST, NB - 1, :]).then_inc(out_done, 16)
                    sp.wait_ge(out_done, 32 if NB > 1 else 16)

        def first_statistics():
            seen = sig("seen", 2, NBX)
            squared = sig("squared", 1, NBX)
            with nc.Block() as block:
                @block.sync
                def _(sp):
                    start(sp)

                @block.vector
                def _(ve):
                    with ve.Fori(0, HNB) as i:
                        for u in range(2):
                            statistics(ve, i, u, 64, seen)

                @block.scalar
                def _(ac):
                    with ac.Fori(0, HNB) as i:
                        for u in range(2):
                            b = bass.ds(i * 2 + u, 1)
                            ac.wait_ge(squared.h, squared.free(i, u))
                            nc.scalar.activation(y_s[:, u, 64:160], X[:, b, 64:160].rearrange("p o f -> p (o f)"),
                                                 ACT.Square, accum_out=vsq[:, b]).then_inc(squared.h, 1)

        def layer0_edges(L):
            rec_in = [mark(f"rec_in{u}", 32 * (NP // 2)) for u in range(2)]
            gat_in = [mark(f"gat_in{u}", 32 * (NP // 2)) for u in range(2)]
            y_step, y_ready = sig("y_step", 7, 0), sig("y_ready", 1, NP)
            pooled1, pooled2 = sig("pooled", 1, NP), sig("pooled2", 1, NP)
            oh_ready = sig("oh_ready", 1, NP)
            turned = sig("turned_e", 1, NP)
            copied = sig("copied_e", 1, NP)
            w_ready = sig("w_ready", 1, NP)
            dst_ready = sig("dst_ready", 1, NP)
            msg_ready = sig("msg_ready", 1, NP)
            part1a, part2a, tp1_ready = sig("part1", 1, NP), sig("part2", 1, NP), sig("tp_ready", 1, NP)
            part1b, part2b, tp2_ready = sig("part1b", 1, NP), sig("part2b", 1, NP), sig("tp2_ready", 1, NP)
            t1, t1c = sig("t1", 2, NP), sig("t1c", 2, NP)
            t2, t2c = sig("t2", 2, NP), sig("t2c", 2, NP)
            val_ready = sig("val_ready", 1, NP)
            squashed = sig("squashed", 1, NP)
            gate_step = sig("gate_step", 1, NP)
            gated = sig("gated_e", 1, NP)
            leak = sig("leak", 3, NP)
            xm_ready = sig("xm_ready", 1, NP)
            xm_t = sig("xm_t", 2, NP)
            top = sig("top", 2, NP)
            m_step, mnew_ready = sig("m_step", 1, NP), sig("mnew_ready", 1, NP)
            msc_ready = sig("msc_ready", 1, NP)
            mg_ready = sig("mg_ready", 1, NP)
            dlt_ready = sig("dlt_ready", 1, NP)
            pex_ready = sig("pex_ready", 1, NP)
            h_ready = sig("h_ready", 1, NP)
            hw_ready = sig("hw_ready", 1, NP)
            summed = sig("summed", 1, NP)
            scaled = sig("scaled", 1, NP)
            kept = sig("kept", 1, NP)
            zeroed_acc = mark("sums_zeroed", 1)
            HALF = NP // 2
            acc = ACC[:, 0:NBX * 164].rearrange("p (b f) -> p b f", b=NBX)
            M = ACC[:, 8200:8200 + NBX * 4].rearrange("p (b h) -> p b h", b=NBX)
            TD = ACC[:, 8400:8400 + NBX * F].rearrange("p (b f) -> p b f", b=NBX)
            pE, pW, pB, pT, pV, pX = BK[0], BK[1], BK[2], [BK[3], BK[4]], BK[5], BK[6]
            pH, pG, pS = BK[7][:, 0:320], BK[7][:, 320:328], BK[7][:, 328:492]
            pVv = pV[:, :].rearrange("p (g f) -> p g f", g=G)
            pHv = pH.rearrange("p (g f) -> p g f", g=G)
            mT1, mT2 = mT, mTb

            def flat(a):
                return a.rearrange("p o f -> p (o f)")

            with nc.Block() as block:
                @block.sync
                def _(sp):
                    start(sp)

                    def records(i, u, first=False):
                        if not first:
                            sp.wait_ge(tp2_ready.h, tp2_ready.free(i, u))
                            sp.sem_inc(sp_tick, 1)
                        load_records(sp, L, i, u, rec_in[u].h)

                    for u in range(2):
                        records(0, u, True)
                    with sp.Fori(1, HALF) as i:
                        for u in range(2):
                            records(i, u)

                @block.gpsimd
                def _(po):
                    def gather(i, u):
                        po.wait_ge(rec_in[u].h, rec_in[u].at(i * 32 + 32))
                        po.sem_inc(pool_tick, 1)
                        po.wait_ge(msg_ready.h, msg_ready.free(i, u))
                        po.sem_inc(pool_tick, 1)
                        for g in range(G):
                            nc.gpsimd.indirect_dma_start(
                                out=gat[:, u, g, :], out_offset=None, in_=tables[0][:, :],
                                in_offset=IOff(ap=rec[:, u, g, 1:2].bitcast(i32), axis=0)).then_inc(gat_in[u].h, 16)
                        directions(po, L, i, u, y_step, y_ready)

                    def part(i, u, sv, ready, used, slot, pooled):
                        po.wait_ge(ready.h, ready.done(i, u))
                        po.sem_inc(pool_tick, 1)
                        po.wait_ge(used.h, used.free(i, u, 1))
                        po.sem_inc(pool_tick, 1)
                        po.wait_ge(y_ready.h, y_ready.done(i, u))
                        product_pool(L, sv, u, slot).then_inc(pooled.h, 1)

                    def part1(i, u):
                        part(i, u, msg[:, u], msg_ready, tp1_ready, 0, pooled1)

                    def part2(i, u):
                        part(i, u, vsv[:, u], gated, tp2_ready, 1, pooled2)

                    gather(0, 0)
                    gather(0, 1)
                    part1(0, 0)
                    with po.Fori(0, HALF - 1) as i:
                        part1(i, 1)
                        part2(i, 0)
                        gather(i + 1, 0)
                        part1(i + 1, 0)
                        part2(i, 1)
                        gather(i + 1, 1)
                    part1(HALF - 1, 1)
                    part2(HALF - 1, 0)
                    part2(HALF - 1, 1)

                def skewed(eng, front, back):
                    front(0, 0)
                    with eng.Fori(0, HALF - 1) as i:
                        front(i, 1, (i, 0))
                        front(i + 1, 0, (i, 1))
                    front(HALF - 1, 1, (HALF - 1, 0))
                    front(None, None, (HALF - 1, 1))

                @block.scalar
                def _(ac):
                    def step(i, u, old=None):
                        if i is not None:
                            ac.wait_ge(turned.h, turned.done(i, u))
                            nc.scalar.activation(efT[0:32, u, :], pE[0:32, 0:128], ACT.Copy)
                            ac.wait_ge(mg_ready.h, mg_ready.free(i, u))
                            nc.scalar.activation(ohT[:, u].rearrange("p g e -> p (g e)"), pE[:, 128:384], ACT.Copy)\
                                .then_inc(copied.h, 1)
                            ac.wait_ge(val_ready.h, val_ready.free(i, u, 1))
                            for g in range(G):
                                ac.wait_ge(t1.h, t1.done(i, u, g + 1))
                                nc.scalar.activation(mT1[:, g, :], pT[g][:, :], ACT.Copy).then_inc(t1c.h, 1)
                        if old:
                            oi, ou = old
                            ac.wait_ge(h_ready.h, h_ready.free(oi, ou, 1))
                            for g in range(G):
                                ac.wait_ge(t2.h, t2.done(oi, ou, g + 1))
                                nc.scalar.activation(mT2[:, g, :], pT[g][:, :], ACT.Copy).then_inc(t2c.h, 1)
                        if i is not None:
                            ac.wait_ge(val_ready.h, val_ready.done(i, u))
                            ac.wait_ge(gated.h, gated.free(i, u, 1))
                            nc.scalar.activation(th[:, u], pVv[:, :, 64:160], ACT.Tanh, scale=0.5)
                            nc.scalar.activation(lk[:, :, :], pVv[:, :, 0:64], ACT.Copy, scale=0.2)\
                                .then_inc(squashed.h, 1)
                            ac.wait_ge(mnew_ready.h, mnew_ready.done(i, u))
                            ac.wait_ge(scaled.h, scaled.free(i, u))
                            nc.scalar.activation(msc[:, u], mdiff[:, u], ACT.Exp).then_inc(msc_ready.h, 1)
                            ac.wait_ge(dlt_ready.h, dlt_ready.done(i, u))
                            ac.wait_ge(hw_ready.h, hw_ready.free(i, u))
                            nc.scalar.activation(pex[:, u], dlt[:, u], ACT.Exp).then_inc(pex_ready.h, 1)

                    skewed(ac, step, None)

                @block.tensor
                def _(pe):
                    def step(i, u, old=None):
                        if i is not None:
                            pe.wait_ge(rec_in[u].h, rec_in[u].at(i * 32 + 32))
                            pe.wait_ge(oh_ready.h, oh_ready.done(i, u))
                            pe.wait_ge(copied.h, copied.free(i, u, 1))
                            nc.tensor.transpose(pE[0:32, 0:128], efr[:, u, 0:G * L.efw], ident[:, :])
                            for g in range(G):
                                last = nc.tensor.transpose(pE[:, 128 + 128 * g:256 + 128 * g], oh[:, u, g, :],
                                                           ident[:, :])
                            last.then_inc(turned.h, 1)
                            b = pe.value_load(L.blocks[0:1, bass.ds(i * 2 + u, 1)], min_val=0, max_val=NB - 1)
                            pe.wait_ge(copied.h, copied.done(i, u))
                            pe.wait_ge(tp1_ready.h, tp1_ready.free(i, u, 1))
                            nc.tensor.matmul(pW[:, 0:448], efT[0:32, u, :], W["rbf0"][:, :], start=True, stop=True)\
                                .then_inc(w_ready.h, 1)
                            pe.wait_ge(msg_ready.h, msg_ready.free(i, u, 1))
                            for g in range(G):
                                last = nc.tensor.matmul(pB[:, F * g:F * g + F], ohT[:, u, g, :],
                                                        flat(TD[:, bass.ds(b, 1), :]), start=True, stop=True)
                            last.then_inc(dst_ready.h, 1)
                            for g in range(G):
                                if g == 0:
                                    pe.wait_ge(tp1_ready.h, tp1_ready.done(i, u))
                                pe.wait_ge(t1c.h, t1c.free(i, u, 1))
                                pe.wait_ge(t2c.h, t2c.free(i, u))
                                for k in range(4):
                                    lo = 0 if k == 0 else 96 + 128 * (k - 1)
                                    last = nc.tensor.transpose(pT[g][:, 128 * k:128 * k + 128],
                                                               tp[:, u, g, lo:lo + 128], ident[:, :])
                                last.then_inc(t1.h, 1)
                        if old:
                            oi, ou = old
                            for g in range(G):
                                if g == 0:
                                    pe.wait_ge(tp2_ready.h, tp2_ready.done(oi, ou))
                                    pe.wait_ge(t2c.h, t2c.free(oi, ou, 1))
                                if i is not None:
                                    pe.wait_ge(t1c.h, t1c.done(i, u, g + 1))
                                for k in range(4):
                                    lo = 0 if k == 0 else 96 + 128 * (k - 1)
                                    last = nc.tensor.transpose(pT[g][:, 128 * k:128 * k + 128],
                                                               tp[:, ou, g, lo:lo + 128], ident[:, :])
                                last.then_inc(t2.h, 1)
                        if i is not None:
                            pe.wait_ge(gated.h, gated.free(i, u, 1))
                            pe.wait_ge(leak.h, leak.free(i, u, 1))
                            for g in range(G):
                                pe.wait_ge(t1c.h, t1c.done(i, u, g + 1))
                                nc.tensor.matmul(pV[:, 256 * g:256 * g + 160], mT1[0:96, g, 0:128],
                                                 W["alpha0"][:, :], start=True, stop=True)
                                for k in range(3):
                                    last = nc.tensor.matmul(pV[:, 256 * g + 160 + 32 * k:256 * g + 192 + 32 * k],
                                                            mT1[:, g, 128 * k + 128:128 * k + 256],
                                                            W["val0"][:, :], start=True, stop=True)
                            last.then_inc(val_ready.h, 1)
                        if old:
                            pe.wait_ge(hw_ready.h, hw_ready.free(oi, ou, 1))
                            for g in range(G):
                                pe.wait_ge(t2c.h, t2c.done(oi, ou, g + 1))
                                hd = pHv[:, g, :].rearrange("p (h f) -> p h f", h=4)
                                nc.tensor.matmul(hd[:, :, 0:16], mT2[0:96, g, 0:128], W["svlin0"][:, :],
                                                 start=True, stop=True)
                                for k in range(3):
                                    last = nc.tensor.matmul(hd[:, :, 16 + 8 * k:24 + 8 * k],
                                                            mT2[:, g, 128 * k + 128:128 * k + 256],
                                                            W["vvlin0"][:, :], start=True, stop=True)
                            last.then_inc(h_ready.h, 1)
                        if i is not None:
                            pe.wait_ge(xm_ready.h, xm_ready.done(i, u))
                            for r in range(2):
                                if r == 0:
                                    pe.wait_ge(top.h, top.free(i, u, 1))
                                else:
                                    pe.wait_ge(top.h, top.done(i, u, 1))
                                for h in range(2):
                                    for g in range(G):
                                        c = 256 * h + 128 * g
                                        last = nc.tensor.transpose(pX[:, c:c + 128], xm[:, g, 2 * r + h, :],
                                                                   ident[:, :])
                                last.then_inc(xm_t.h, 1)
                            pe.wait_ge(mnew_ready.h, mnew_ready.done(i, u))
                            pe.wait_ge(dlt_ready.h, dlt_ready.free(i, u, 1))
                            for g in range(G):
                                last = nc.tensor.matmul(pG[:, 4 * g:4 * g + 4], ohT[:, u, g, :], mnew[:, u, :],
                                                        start=True, stop=True)
                            last.then_inc(mg_ready.h, 1)
                        if old:
                            pe.wait_ge(hw_ready.h, hw_ready.done(oi, ou))
                            pe.wait_ge(kept.h, kept.free(oi, ou, 1))
                            for g in range(G):
                                last = nc.tensor.matmul(pS, oh[:, ou, g, :], hw[:, ou, g, :],
                                                        start=g == 0, stop=g == G - 1)
                            last.then_inc(summed.h, 1)

                    skewed(pe, step, None)

                @block.vector
                def _(ve):
                    nc.vector.memset(ACC[:, 0:8200], 0.0)
                    nc.vector.memset(ACC[:, 8200:8200 + NBX * 4], -NEG).then_inc(zeroed_acc.h, 1)
                    ve.wait_ge(zeroed_acc.h, zeroed_acc.at(1))

                    def step(i, u, old=None):
                        if i is not None:
                            ve.wait_ge(rec_in[u].h, rec_in[u].at(i * 32 + 32))
                            ve.wait_ge(summed.h, summed.free(i, u))
                            for g in range(G):
                                last = nc.vector.tensor_scalar(oh[:, u, g, :], iota1[:, :], rec[:, u, g, 0:1], None,
                                                               ALU.is_equal)
                            last.then_inc(oh_ready.h, 1)
                            ve.wait_ge(oh_ready.h, oh_ready.done(i, u))
                            nc.vector.tensor_scalar(mb[:, :, :], oh[:, u], 1.0, NEG, ALU.subtract, ALU.mult)
                            ve.wait_ge(dst_ready.h, dst_ready.done(i, u))
                            ve.wait_ge(gat_in[u].h, gat_in[u].at(i * 32 + 32))
                            nc.vector.tensor_tensor(msg[:, u], gat[:, u], pB[:, 0:320].rearrange(
                                "p (g f) -> p g f", g=G), ALU.add).then_inc(msg_ready.h, 1)
                            ve.wait_ge(msg_ready.h, msg_ready.done(i, u))
                            ve.wait_ge(w_ready.h, w_ready.done(i, u))
                            ve.wait_ge(y_ready.h, y_ready.done(i, u))
                            product_vector(ve, L, i, u, msg[:, u], pW[:, 0:448].rearrange("p (g f) -> p g f", g=G),
                                           rec[:, u, :, 2:3], 0, pooled1, part1a, part2a).then_inc(tp1_ready.h, 1)
                        if old:
                            oi, ou = old
                            ve.wait_ge(t1.h, t1.done(oi, ou))
                            product_vector(ve, L, oi, ou, vsv[:, ou], None, rec[:, ou, :, 2:3], 1, pooled2,
                                           part1b, part2b).then_inc(tp2_ready.h, 1)
                        if i is not None:
                            ve.wait_ge(squashed.h, squashed.done(i, u))
                            nc.vector.tensor_scalar(th2[:, :, :], th[:, u], 0.5, 0.5, ALU.mult, ALU.add)\
                                .then_inc(gate_step.h, 1)
                            nc.vector.tensor_tensor(la[:, :, :], pVv[:, :, 0:64], lk[:, :, :], ALU.max)\
                                .then_inc(leak.h, 1)
                            ve.wait_ge(gate_step.h, gate_step.done(i, u))
                            nc.vector.tensor_copy(vsv[:, u, :, 0:64], th2[:, :, 0:64])
                            for g in range(G):
                                last = nc.vector.tensor_tensor(
                                    vsv[:, u, g, 64:160].rearrange("p (i c) -> p i c", i=3),
                                    pVv[:, g, 160:256].rearrange("p (i c) -> p i c", i=3),
                                    th2[:, g, 64:96].unsqueeze(1).to_broadcast([P, 3, 32]), ALU.mult)
                            last.then_inc(gated.h, 1)
                            ve.wait_ge(leak.h, leak.done(i, u, 1))
                            nc.vector.tensor_tensor(la2[:, :, :], la[:, :, :],
                                                    W["ad"][:, :].unsqueeze(1).to_broadcast([P, G, 64]), ALU.mult)\
                                .then_inc(leak.h, 1)
                            ve.wait_ge(leak.h, leak.done(i, u, 2))
                            nc.vector.reduce_sum(a4[:, u], la2[:, :, :].rearrange("p g (h d) -> p g h d", h=4), AX.X)\
                                .then_inc(leak.h, 1)
                            ve.wait_ge(leak.h, leak.done(i, u, 3))
                            ve.wait_ge(xm_t.h, xm_t.free(i, u, 1))
                            for g in range(G):
                                last = nc.vector.tensor_tensor(
                                    xm[:, g], mb[:, g, :].unsqueeze(1).to_broadcast([P, 4, P]),
                                    a4[:, u, g, :].unsqueeze(2).to_broadcast([P, 4, P]), ALU.add)
                            last.then_inc(xm_ready.h, 1)
                            for r in range(2):
                                ve.wait_ge(xm_t.h, xm_t.done(i, u, r + 1))
                                nc.vector.reduce_max(tm[:, 2 * r:2 * r + 2], pX[:, :].rearrange(
                                    "p (h e) -> p h e", h=2), AX.X).then_inc(top.h, 1)
                            ve.wait_ge(top.h, top.done(i, u))
                            b = ve.value_load(L.blocks[0:1, bass.ds(i * 2 + u, 1)], min_val=0, max_val=NB - 1)
                            mrow = flat(M[:, bass.ds(b, 1), :])
                            nc.vector.tensor_tensor(mnew[:, u, :], mrow, tm[:, :], ALU.max).then_inc(m_step.h, 1)
                            ve.wait_ge(m_step.h, m_step.done(i, u))
                            nc.vector.tensor_tensor(mdiff[:, u, :], mrow, mnew[:, u, :], ALU.subtract)\
                                .then_inc(mnew_ready.h, 1)
                            ve.wait_ge(mnew_ready.h, mnew_ready.done(i, u))
                            ve.sem_inc(ve_tick, 1)
                            nc.vector.tensor_copy(mrow, mnew[:, u, :])
                            ve.wait_ge(mg_ready.h, mg_ready.done(i, u))
                            nc.vector.tensor_tensor(dlt[:, u], a4[:, u], pG.rearrange("p (g h) -> p g h", g=G),
                                                    ALU.subtract).then_inc(dlt_ready.h, 1)
                        if old:
                            ve.wait_ge(h_ready.h, h_ready.done(oi, ou))
                            ve.wait_ge(pex_ready.h, pex_ready.done(oi, ou))
                            for g in range(G):
                                hv = hw[:, ou, g, :].rearrange("p (h f) -> p h f", h=4)
                                nc.vector.tensor_tensor(
                                    hv[:, :, 0:40], pHv[:, g, :].rearrange("p (h f) -> p h f", h=4),
                                    pex[:, ou, g, :].unsqueeze(2).to_broadcast([P, 4, 40]), ALU.mult)
                            last = nc.vector.tensor_copy(
                                hw[:, ou].rearrange("p g (h f) -> p g h f", h=4)[:, :, :, 40], pex[:, ou])
                            last.then_inc(hw_ready.h, 1)
                            b = ve.value_load(L.blocks[0:1, bass.ds(oi * 2 + ou, 1)], min_val=0, max_val=NB - 1)
                            row = flat(acc[:, bass.ds(b, 1), :])
                            rowh = row.rearrange("p (h f) -> p h f", h=4)
                            ve.wait_ge(msc_ready.h, msc_ready.done(oi, ou))
                            ve.wait_ge(kept.h, kept.free(oi, ou, 1))
                            nc.vector.tensor_tensor(rowh, rowh, msc[:, ou, :].unsqueeze(2).to_broadcast([P, 4, 41]),
                                                    ALU.mult).then_inc(scaled.h, 1)
                            ve.wait_ge(scaled.h, scaled.done(oi, ou))
                            ve.wait_ge(summed.h, summed.done(oi, ou))
                            nc.vector.tensor_tensor(row, row, pS, ALU.add).then_inc(kept.h, 1)

                    skewed(ve, step, None)
                    ve.wait_ge(kept.h, kept.done(HALF - 1, 1))

        def layer0_update():
            den = sig("den", 2, NBX)
            divided = sig("divided", 1, NBX)
            turned = sig("turned", 1, NBX)
            copied = sig("copied", 1, NBX)
            made = sig("made", 1, NBX)
            updated = sig("updated", 1, NBX)
            seen = sig("seen", 2, NBX)
            acc = ACC[:, 0:NBX * 164].rearrange("p (b f) -> p b f", b=NBX)
            pT, pO = [BK[0], BK[1]], [BK[2], BK[3]]
            with nc.Block() as block:
                @block.sync
                def _(sp):
                    start(sp)

                @block.vector
                def _(ve):
                    def rows(i, u):
                        b = bass.ds(i * 2 + u, 1)
                        a = acc[:, b, :].rearrange("p o (h f) -> p (o h) f", h=4)
                        nc.vector.tensor_scalar_add(nrm[:, u, :], a[:, :, 40], 1e-16).then_inc(den.h, 1)
                        ve.wait_ge(den.h, den.done(i, u, 1))
                        nc.vector.reciprocal(nrm2[:, u, :], nrm[:, u, :]).then_inc(den.h, 1)
                        ve.wait_ge(den.h, den.done(i, u, 2))
                        ve.wait_ge(turned.h, turned.free(i, u))
                        nc.vector.tensor_tensor(xn[:, u, :].rearrange("p (h f) -> p h f", h=4), a[:, :, 0:40],
                                                nrm2[:, u, :].unsqueeze(2).to_broadcast([P, 4, 40]), ALU.mult)\
                            .then_inc(divided.h, 1)

                    def outputs(i, u):
                        b = bass.ds(i * 2 + u, 1)
                        ve.wait_ge(made.h, made.done(i, u))
                        xs = X[:, b, 0:64].rearrange("p o f -> p (o f)")
                        xv = X[:, b, 64:160].rearrange("p o (c i) -> p i (o c)", i=3)
                        nc.vector.scalar_tensor_tensor(xs, xs, 2.0, pO[u][:, 0:64], ALU.mult, ALU.add)
                        nc.vector.scalar_tensor_tensor(xv, xv, 2.0, pO[u][:, 64:160].rearrange(
                            "p (i c) -> p i c", i=3), ALU.mult, ALU.add).then_inc(updated.h, 1)
                        ve.wait_ge(updated.h, updated.done(i, u))
                        ve.sem_inc(ve_tick, 1)
                        statistics(ve, i, u, F, seen)

                    with ve.Fori(0, HNB) as i:
                        rows(i, 0)
                        rows(i, 1)
                        outputs(i, 0)
                        outputs(i, 1)

                @block.tensor
                def _(pe):
                    with pe.Fori(0, HNB) as i:
                        for u in range(2):
                            pe.wait_ge(divided.h, divided.done(i, u))
                            pe.wait_ge(copied.h, copied.free(i, u))
                            for k in range(2):
                                last = nc.tensor.transpose(pT[u][0:80, 128 * k:128 * k + 128],
                                                           xn[:, u, 80 * k:80 * k + 80], ident[:, :])
                            last.then_inc(turned.h, 1)
                        for u in range(2):
                            pe.wait_ge(copied.h, copied.done(i, u))
                            pe.wait_ge(updated.h, updated.free(i, u))
                            for k in range(2):
                                last = nc.tensor.matmul(pO[u][:, 0:160], xT[0:80, u, 128 * k:128 * k + 128],
                                                        W["proj0"][:, 160 * k:160 * k + 160],
                                                        start=k == 0, stop=k == 1)
                            last.then_inc(made.h, 1)

                @block.scalar
                def _(ac):
                    with ac.Fori(0, HNB) as i:
                        for u in range(2):
                            ac.wait_ge(turned.h, turned.done(i, u))
                            ac.wait_ge(made.h, made.free(i, u))
                            nc.scalar.activation(xT[0:80, u, :], pT[u][0:80, 0:256], ACT.Copy).then_inc(copied.h, 1)

        first_statistics()
        node_table(0)
        layer0_edges(layer(0))
        layer0_update()
        for k in range(1, 4):
            node_table(k)
            edge_loop(layer(k))
            node_update(layer(k))
        last_norm()


def lay_out(x, src, dst, edge_attr_16, edge_attr_3, edge_attr_4, edge_attr_64, node_vec1, ch, **weights):
    import numpy as np
    e = src.shape[0]
    _, _, t, _ = sizes(x.shape[0], e, ch)
    nbx = sizes(x.shape[0], e, ch)[1]
    attrs = np.zeros((P * t, 87), np.float32)
    attrs[:e, 0:4] = edge_attr_4
    attrs[:e, 4:20] = edge_attr_16
    attrs[:e, 20:84] = edge_attr_64
    attrs[:e, 84:87] = edge_attr_3
    ids = []
    for a in (src, dst):
        padded = np.zeros((P * t,), np.int32)
        padded[:e] = a
        ids.append(padded)
    rows = []
    for a in (x, node_vec1):
        padded = np.zeros((P * nbx, a.shape[1]), np.float32)
        padded[:a.shape[0]] = a
        rows.append(padded)
    return {"x": rows[0], "attrs": attrs, "src": ids[0], "dst": ids[1], "node_vec1": rows[1],
            **{k: np.asarray(v) for k, v in weights.items()}}


def program(nc, arrays, n, e, ch):
    aps = {name: nc.dram_tensor(f"in_{name}", a.shape, mybir.dt.from_np(a.dtype), kind="ExternalInput").ap()
           for name, a in arrays.items()}
    out = nc.dram_tensor("out", (n, F), mybir.dt.float32, kind="ExternalOutput").ap()
    build(nc, aps, out, n, e, ch)


def kernel(**inputs):
    import numpy as np
    import concourse.bacc as bacc
    from concourse.bass_utils import run_bass_kernel_spmd
    arrays = lay_out(ch=23, **inputs)
    nc = bacc.Bacc("TRN2", target_bir_lowering=False, num_devices=1)
    program(nc, arrays, inputs["x"].shape[0], inputs["src"].shape[0], 23)
    maps = {f"in_{name}": np.ascontiguousarray(a) for name, a in arrays.items()}
    return run_bass_kernel_spmd(nc, [maps], core_ids=[0]).results[0]["out"]
```

```python
import concourse.bass as bass
from concourse import mybir
from contextlib import ExitStack

P = 128
G = 2
F = 160
CS, CV = 64, 32
RD, RS = 86, 69
RW = 91
NEG = 1.0e30
EPS = 1e-5
R3, R2 = 3.0 ** 0.5, 2.0 ** 0.5


class Sig:

    def __init__(self, handle, per):
        self.h, self.per, self.base, self.total, self.unroll = handle, per, 0, 0, 2

    def done(self, i, u, m=None):
        return i * (self.unroll * self.per) + (
            self.base + 4 * self.per + u * self.per + (self.per if m is None else m))

    def free(self, i, u, slots=2):
        return i * (self.unroll * self.per) + (
            self.base + 4 * self.per + u * self.per + self.per - slots * self.per)


class Mark:

    def __init__(self, handle):
        self.h, self.base, self.total = handle, 0, 0

    def at(self, k):
        return k + self.base


def sizes(n, e, ch):
    nb = -(-n // P)
    t = -(-e // (P * 2 * ch)) * 2 * ch
    pairs = (e + nb * (G * P - 1)) // (G * P)
    pairs += -pairs % 4
    return nb, nb + nb % 2, t, pairs


def build(nc, ins, out, N, E, CH):
    fp32, i32 = mybir.dt.float32, mybir.dt.int32
    ALU, ACT, AX = mybir.AluOpType, mybir.ActivationFunctionType, mybir.AxisListType
    IOff = bass.IndirectOffsetOnAxis
    NB, NBX, T, NP = sizes(N, E, CH)
    LAST = N - (NB - 1) * P
    NCH = T // CH
    ACCW = max(NBX * 480, 16000)
    ctx = ExitStack()
    with ctx:
        def sb(name, shape, dt=fp32):
            return ctx.enter_context(nc.sbuf_tensor(name, shape, dt))

        def ps(name):
            return ctx.enter_context(nc.psum_tensor(name, [P, 512], fp32))

        def sem(name):
            return ctx.enter_context(nc.semaphore(name))

        fresh, known = [], {}

        def sig(name, per=1, steps=0, unroll=2):
            if name not in known:
                known[name] = Sig(sem(name), per)
                fresh.append(known[name])
            s = known[name]
            assert s.per == per
            s.base += s.total
            s.total = per * steps
            s.unroll = unroll
            return s

        def sig4(name, per=1, steps=0):
            return sig(name, per, steps, 4)

        def mark(name, total):
            if name not in known:
                known[name] = Mark(sem(name))
            known[name].base += known[name].total
            known[name].total = total
            return known[name]

        def start(eng):
            while fresh:
                s = fresh.pop()
                eng.sem_inc(s.h, 4 * s.per)

        QP = NP // 4
        rec_dst = nc.dram_tensor("rec_dst", (NP * G * P, RD), fp32).ap()
        rec_src = nc.dram_tensor("rec_src", (NP * G * P, RS), fp32).ap()
        tables = [nc.dram_tensor(f"table{n}", (NBX * P, F), fp32).ap() for n in range(4)]
        rec_dst_v = rec_dst.rearrange("(i u p g) r -> i u p g r", u=4, g=G, p=P)
        rec_src_v = rec_src.rearrange("(i u p g) r -> i u p g r", u=4, g=G, p=P)
        tables_v = [t.rearrange("(i u p) f -> i u p f", u=2, p=P) for t in tables]

        X = sb("X", [P, NBX, F])
        ACC = sb("ACC", [P, ACCW])
        node_a = sb("node_a", [P, NBX])
        a_rows = sb("a_rows", [NBX, P])
        ident = sb("ident", [P, P])
        iota1 = sb("iota1", [P, P])
        ones = sb("ones", [P, P])
        tril = sb("tril", [P, P])
        pair_block = [sb(f"pair_block{s}", [1, NP], i32) for s in range(2)]
        bn6 = sb("bn6", [P, 2, 6])
        mean_var = sb("mean_var", [P, 2, 2])
        stat = sb("stat", [P, NBX, 2])
        rstd = sb("rstd", [P, NBX])
        vsq = sb("vsq", [P, NBX])
        rstd_v = sb("rstd_v", [P, NBX])

        w_specs = {
            "rbf0": (32, 448), "alpha0": (96, 160), "val0": (P, 32), "svlin0": (96, 64), "vvlin0": (P, 32),
            "proj0": (80, 320), "ts0": (64, 128), "tv0": (96, 192), "gam_s": (64, 1), "bet_s": (64, 1),
            "gam_v": (96, 1), "sc_s": (96, 1), "sc_v": (P, 1), "adr": (1, 64), "wg": (64, 32),
            "svT": (64, 96), "ad": (P, 64),
            "fc1_1": (P, P), "fc2_1": (P, 448), "ts1": (64, 64), "tv1": (96, 96),
            "xs1": (64, 96), "xv1": (96, 96), "os1": (96, 96), "ov1": (P, 32),
            "fc1_2": (32, P), "fc2_2": (P, 448), "ts2": (64, 64), "tv2": (96, 96),
            "xs2": (64, 64), "xv2": (96, 96), "os2": (96, 65), "ov2": (96, 32),
            "fc1_3": (P, P), "fc2_3": (P, 448), "ts3": (64, 64), "tv3": (96, 96),
            "xs3": (64, 96), "xv3": (96, 96), "os3": (96, 96), "ov3": (P, 32),
        }
        W = {k: sb("w_" + k, list(s)) for k, s in w_specs.items()}

        rec = sb("rec", [P, 4, G, 6])
        efr = sb("efr", [P, 4, G * 64])
        gat = sb("gat", [P, 4, G, F])
        oh = sb("oh", [P, 4, G, P])
        yx = sb("yx", [P, 4, G, 5])
        ysq = sb("ysq", [P, 2, G, 3])
        yn = sb("yn", [P, 2, G])
        yr = sb("yr", [P, 2, G])
        efT = sb("efT", [P, 2, P])
        hT = sb("hT", [P, 2, P])
        tp = sb("tp", [P, 2, G, 480])
        wy = sb("wy", [P, G, 96])
        t_sv = sb("t_sv", [P, G, 64])
        t_dot = sb("t_dot", [P, 2, G, 3, 32])
        t_cr = sb("t_cr", [P, 2, G, 3, 32])
        t_cr2 = sb("t_cr2", [P, G, 3, 32])
        t_cr3 = sb("t_cr3", [P, G, 3, 32])
        t_sum = sb("t_sum", [P, G, 32])
        t_sum2 = sb("t_sum2", [P, G, 32])
        mhalf = sb("mhalf", [P, G])
        msg = sb("msg", [P, 2, G, F])
        ohT = sb("ohT", [P, 4, G, P])
        mT = sb("mT", [P, G, 512])
        mTb = sb("mTb", [P, G, 512])
        th = sb("th", [P, 2, G, 96])
        th2 = sb("th2", [P, G, 96])
        la2 = sb("la2", [P, G, 64])
        lk = sb("lk", [P, G, 64])
        la = sb("la", [P, G, 64])
        a4 = sb("a4", [P, 2, G, 4])
        mb = sb("mb", [P, G, P])
        xm = sb("xm", [P, G, 4, P])
        tm = sb("tm", [P, 4])
        mnew = sb("mnew", [P, 2, 4])
        mdiff = sb("mdiff", [P, 2, 4])
        msc = sb("msc", [P, 4, 4])
        dlt = sb("dlt", [P, 2, G, 4])
        pex = sb("pex", [P, 2, G, 4])
        vsv = sb("vsv", [P, 2, G, F])
        hw = sb("hw", [P, 2, G, 164])
        xn = msg[:, :, 0, :]
        xT = mTb[:, :, 0:256]
        aT = mT
        accrow = tp[:, :, 0, :]
        tb = vsv[:, :, 0, :]
        nrm = sb("nrm", [P, 2, 4])
        nrm2 = sb("nrm2", [P, 2, 4])
        y_s = hw[:, :, 0, 0:160]
        sgm = th[:, :, 0, :]

        BK = [ps(f"bank{k}") for k in range(8)]

        setup_zero = sem("setup_zero")
        weights_in = sem("weights_in")
        x_in = sem("x_in")
        const_ready = sem("const_ready")
        ramp_done = sem("ramp_done")
        fill_done = [sem("fill_dst_done"), sem("fill_src_done")]
        keys_in = sem("keys_in")
        wprep = sem("wprep")
        wpe = sem("wpe")

        ZP = max(d for d in range(1, 23) if NP % d == 0)
        ZCOL = ZP * G * RD
        zeros_t = ACC[:, ACCW - ZCOL:ACCW]
        o = [0]

        def scratch(cols):
            o[0] += cols
            return ACC[:, o[0] - cols:o[0]]

        raw = [scratch(T).bitcast(i32) for _ in range(2)]
        blki = scratch(T).bitcast(i32)
        loci = scratch(T).bitcast(i32)
        keyf = [scratch(T) for _ in range(2)]
        blkf = [scratch(T) for _ in range(2)]
        posi = [scratch(T).bitcast(i32) for _ in range(2)]
        posf = scratch(T)
        zrow = scratch(T)
        eqb = scratch(2 * T).rearrange("p (u t) -> p u t", u=2)
        scb = scratch(2 * T).rearrange("p (u t) -> p u t", u=2)
        tmb = scratch(2 * T).rearrange("p (u t) -> p u t", u=2)
        bidx = scratch(NBX)
        cnt = scratch(NBX)
        tot = scratch(NBX)
        toti = scratch(NBX).bitcast(i32)
        toti2 = scratch(NBX).bitcast(i32)
        prs = scratch(NBX)
        endp = scratch(NBX)
        offp = scratch(NBX)
        jrow = scratch(NP)
        blkacc = scratch(2 * NP).rearrange("p (u t) -> p u t", u=2)
        stage = scratch(2 * CH * RW).rearrange("p (u c r) -> p u c r", u=2, r=RW)
        sidx = scratch(4 * CH).bitcast(i32).rearrange("p (u s c) -> p u s c", u=2, s=2)
        assert o[0] <= ACCW - ZCOL

        attrs_v = ins["attrs"].rearrange("(p i u c) r -> p i u c r", p=P, u=2, c=CH)
        loads = []

        def load(dst, src):
            loads.append((dst, src))

        A = ins
        for g in range(G):
            load(W["rbf0"][16 * g:16 * g + 16, 224 * g:224 * g + 224], A["L0_gnn_W_rbf"])
            load(W["fc1_1"][64 * g:64 * g + 64, 64 * g:64 * g + 64], A["L1_gnn_W_fc1"])
            load(W["fc2_1"][64 * g:64 * g + 64, 224 * g:224 * g + 224], A["L1_gnn_W_fc2"])
            load(W["fc1_2"][16 * g:16 * g + 16, 64 * g:64 * g + 64], A["L2_gnn_Wfc1"])
            load(W["fc2_2"][64 * g:64 * g + 64, 224 * g:224 * g + 192], A["L2_gnn_Wfc2"])
            load(W["fc1_3"][64 * g:64 * g + 64, 64 * g:64 * g + 64], A["L3_gnn_fc_w1"])
            load(W["fc2_3"][64 * g:64 * g + 64, 224 * g:224 * g + 224], A["L3_gnn_fc_w2"])
        load(W["alpha0"][:, 0:64], A["L0_gnn_W_alpha"])
        load(W["alpha0"][:, 64:128], A["L0_gnn_Ws_val"])
        load(W["val0"][:, :], A["L0_gnn_Wv_val"])
        load(W["svlin0"][:, :], A["L0_gnn_Ws_vlin"])
        load(W["vvlin0"][:, :], A["L0_gnn_Wv_vlin"])
        for h in range(4):
            k, r = h // 2, 40 * (h % 2)
            load(W["proj0"][r:r + 16, 160 * k:160 * k + 64], A["L0_gnn_Wps"][16 * h:16 * h + 16, :])
            for i in range(3):
                load(W["proj0"][r + 16 + 8 * i:r + 24 + 8 * i, 160 * k + 64 + 32 * i:160 * k + 96 + 32 * i],
                     A["L0_gnn_Wpv"][8 * h:8 * h + 8, :])
        load(W["ts0"][:, 0:64], A["L0_gnn_Ws_src"])
        load(W["ts0"][:, 64:128], A["L0_gnn_Ws_dst"])
        for i in range(3):
            r = slice(32 * i, 32 * i + 32)
            load(W["tv0"][r, 32 * i:32 * i + 32], A["L0_gnn_Wv_src"])
            load(W["tv0"][r, 96 + 32 * i:128 + 32 * i], A["L0_gnn_Wv_dst"])
            load(W["gam_v"][r, :], A["L0_gnn_gamma_v"].rearrange("(c o) -> c o", o=1))
            load(W["tv1"][r, r], A["L1_gnn_W_nl1"])
            load(W["xv1"][r, r], A["L1_gnn_W_skip1"])
            load(W["tv2"][r, r], A["L2_gnn_Wl1_1"])
            load(W["xv2"][r, r], A["L2_gnn_Wsc1"])
            load(W["tv3"][r, r], A["L3_gnn_lin1_wv"])
            load(W["xv3"][r, r], A["L3_gnn_sc_wv"])
        load(W["gam_s"][:, :], A["L0_gnn_gamma_s"].rearrange("(c o) -> c o", o=1))
        load(W["bet_s"][:, :], A["L0_gnn_beta_s"].rearrange("(c o) -> c o", o=1))
        load(W["sc_s"][0:64, :], A["L0_gnn_w2_ss"].rearrange("(c o) -> c o", o=1))
        load(W["sc_s"][64:96, :], A["L0_gnn_w2_vv0"].rearrange("(c o) -> c o", o=1))
        load(W["sc_v"][0:64, :], A["L0_gnn_w2_sv"].rearrange("(c o) -> c o", o=1))
        load(W["sc_v"][64:96, :], A["L0_gnn_w2_vs"].rearrange("(c o) -> c o", o=1))
        load(W["sc_v"][96:128, :], A["L0_gnn_w2_vv1"].rearrange("(c o) -> c o", o=1))
        load(W["adr"][:, :], A["L0_gnn_alpha_dot"].rearrange("o h d -> o (h d)"))
        load(W["wg"][:, :], A["L0_gnn_Wg"])
        load(W["ts1"][:, :], A["L1_gnn_W_nl0"])
        load(W["xs1"][:, :], A["L1_gnn_W_skip0"])
        load(W["os1"][:, :], A["L1_gnn_W_out_s"])
        load(W["ov1"][:, :], A["L1_gnn_W_out_v"])
        load(W["ts2"][:, :], A["L2_gnn_Wl1_0"])
        load(W["xs2"][:, :], A["L2_gnn_Wsc0"])
        load(W["os2"][:, 0:64], A["L2_gnn_Wl2_s"])
        load(W["os2"][:, 64:65], A["L2_gnn_Wa"])
        load(W["ov2"][:, :], A["L2_gnn_Wl2_v"])
        load(W["ts3"][:, :], A["L3_gnn_lin1_ws"])
        load(W["xs3"][:, :], A["L3_gnn_sc_ws"])
        load(W["os3"][:, :], A["L3_gnn_lin2_ws"])
        load(W["ov3"][:, :], A["L3_gnn_lin2_wv"])
        zeroed = ["rbf0", "fc1_1", "fc2_1", "fc1_2", "fc2_2", "fc1_3", "fc2_3", "proj0", "tv0", "tv1", "xv1",
                  "tv2", "xv2", "tv3", "xv3"]
        NFILL = NP // ZP

        with nc.Block() as block:
            @block.sync
            def _(sp):
                sp.wait_ge(setup_zero, 1)
                sp.dma_start(X[:, :, :], A["x"].rearrange("(b p) f -> p b f", p=P)).then_inc(x_in, 16)
                sp.dma_start(a_rows[:, :], A["node_vec1"].rearrange("(b p) o -> b (p o)", p=P)).then_inc(x_in, 16)
                sp.dma_start(raw[0], A["dst"].rearrange("(p t) -> p t", p=P)).then_inc(keys_in, 16)
                sp.dma_start(raw[1], A["src"].rearrange("(p t) -> p t", p=P)).then_inc(keys_in, 16)
                for dst, src in loads:
                    sp.dma_start(dst, src, allow_slow_non_contiguous=dst.shape[-1] == 1).then_inc(weights_in, 16)
                sp.wait_ge(x_in, 32)
                sp.wait_ge(keys_in, 32)
                sp.wait_ge(weights_in, 16 * len(loads))

            @block.vector
            def _(ve):
                for k in zeroed:
                    nc.vector.memset(W[k][:, :], 0.0)
                nc.vector.memset(zrow, 0.0).then_inc(setup_zero, 1)
                nc.vector.memset(ones[:, :], 1.0).then_inc(const_ready, 1)

                def scale(name, r0, r1, by):
                    nc.vector.tensor_scalar_mul(W[name][r0:r1, :], W[name][r0:r1, :], by).then_inc(wprep, 1)

                ve.wait_ge(weights_in, 16 * len(loads))
                scale("os1", 0, 96, 1 / 32)
                scale("ov1", 0, 64, R3 / 32)
                scale("ov1", 64, 96, 1 / 32)
                scale("ov1", 96, 128, R3 / R2 / 32)
                scale("ts2", 0, 64, 1 / 8)
                scale("tv2", 0, 96, 32 ** -0.5)
                scale("xs2", 0, 64, 1 / 8)
                scale("xv2", 0, 96, 32 ** -0.5)
                scale("os2", 0, 64, 96 ** -0.5 / 8)
                scale("os2", 64, 96, 96 ** -0.5 / 8 / R3)
                scale("ov2", 0, 96, 96 ** -0.5 / 8)
                scale("ts3", 0, 64, 1 / 8)
                scale("tv3", 0, 96, 32 ** -0.5)
                scale("xs3", 0, 64, 1 / 8)
                scale("xv3", 0, 96, 32 ** -0.5)
                scale("os3", 0, 64, 96 ** -0.5 / 32)
                scale("os3", 64, 96, 96 ** -0.5 / 32 / R3)
                scale("ov3", 0, 96, 128 ** -0.5 / 32)
                scale("ov3", 96, 128, 128 ** -0.5 / 32 / R2)
                scale("sc_s", 64, 96, 1 / R3)
                scale("sc_v", 96, 128, 1 / R2)
                scale("val0", 96, 128, 1 / R2)
                n = 22
                ve.wait_ge(wprep, n)
                nc.vector.tensor_scalar_mul(W["svlin0"][:, :], W["svlin0"][:, :], W["sc_s"][:, :]).then_inc(wprep, 1)
                nc.vector.tensor_scalar_mul(W["vvlin0"][:, :], W["vvlin0"][:, :], W["sc_v"][:, :]).then_inc(wprep, 1)
                ve.wait_ge(wpe, 1)
                nc.vector.tensor_copy(W["svT"][:, :], BK[0][0:64, 0:96]).then_inc(wprep, 1)
                nc.vector.tensor_copy(W["ad"][:, :], BK[1][:, 0:64]).then_inc(wprep, 1)
                nc.vector.tensor_copy(node_a[:, :], BK[3][:, 0:NBX]).then_inc(wprep, 1)
                ve.wait_ge(wpe, 2)
                nc.vector.tensor_copy(W["alpha0"][:, 128:160], BK[2][0:96, 0:32]).then_inc(wprep, 1)
                ve.wait_ge(wprep, n + 6)
                scale("alpha0", 64, 96, 1 / R3)

            @block.gpsimd
            def _(po):
                nc.gpsimd.memset(ident[:, :], 0.0).then_inc(ramp_done, 1)
                nc.gpsimd.memset(tril[:, :], 1.0).then_inc(ramp_done, 1)
                nc.gpsimd.memset(mhalf[:, :], -0.5)
                po.wait_ge(ramp_done, 2)
                nc.gpsimd.affine_select(out=ident[:, :], in_=ident[:, :], compare_op=ALU.not_equal, fill=1.0,
                                        base=0, pattern=[[-1, P]], channel_multiplier=1).then_inc(ramp_done, 1)
                nc.gpsimd.affine_select(out=tril[:, :], in_=tril[:, :], compare_op=ALU.is_gt, fill=0.0,
                                        base=0, pattern=[[1, P]], channel_multiplier=-1).then_inc(ramp_done, 1)
                nc.gpsimd.iota(iota1[:, :], pattern=[[1, P]], base=1, channel_multiplier=0,
                               allow_small_or_imprecise_dtypes=True).then_inc(ramp_done, 1)
                nc.gpsimd.iota(bidx, pattern=[[1, NBX]], base=0, channel_multiplier=0,
                               allow_small_or_imprecise_dtypes=True).then_inc(ramp_done, 1)
                nc.gpsimd.iota(jrow, pattern=[[1, NP]], base=0, channel_multiplier=0,
                               allow_small_or_imprecise_dtypes=True).then_inc(ramp_done, 1)

            @block.tensor
            def _(pe):
                pe.wait_ge(ramp_done, 7)
                pe.wait_ge(const_ready, 1)
                pe.wait_ge(weights_in, 16 * len(loads))
                pe.wait_ge(x_in, 32)
                nc.tensor.transpose(BK[3][:, 0:NBX], a_rows[:, :], ident[0:NBX, 0:NBX])
                nc.tensor.transpose(BK[0][0:64, 0:96], W["alpha0"][:, 64:128], ident[0:96, 0:96])
                nc.tensor.matmul(BK[1][:, 0:64], ones[0:1, :], W["adr"][:, :], start=True, stop=True).then_inc(wpe, 1)
                pe.wait_ge(wprep, 26)
                nc.tensor.matmul(BK[2][0:96, 0:32], W["svT"][:, :], W["wg"][:, :], start=True, stop=True)\
                    .then_inc(wpe, 1)

        keys_split = sem("keys_split")
        pads_marked = sem("pads_marked")
        zero_tile = sem("zero_tile")
        hot = [sig(f"bucket_hot{s}") for s in range(2)]
        ranked = [sig(f"bucket_ranked{s}") for s in range(2)]
        picked = [sig(f"bucket_picked{s}") for s in range(2)]
        added = [sig(f"bucket_added{s}") for s in range(2)]
        shifted = [sig(f"bucket_shifted{s}") for s in range(2)]
        added2 = [sig(f"bucket_shift_added{s}") for s in range(2)]
        counted = sem("counted")
        off_step = sem("off_step")
        pos_done = sem("pos_done")
        pos_ready = sem("pos_ready")
        tbl_step = sem("tbl_step")
        pool_tick = sem("pool_tick")
        sp_tick = sem("sp_tick")
        ve_tick = sem("ve_tick")
        TH = [(0, min(512, T))] + ([(512, T)] if T > 512 else [])
        PADPOS = float(1 << 24)
        HB = NBX // 2
        with nc.Block() as block:
            @block.sync
            def _(sp):
                start(sp)
                sp.wait_ge(zero_tile, 1)
                for s, (r, w) in enumerate(((rec_dst, RD), (rec_src, RS))):
                    v = r.rearrange("(k p g) r -> k p (g r)", p=P, g=ZP * G)
                    for k in range(NFILL):
                        sp.dma_start(v[k], zeros_t[:, 0:ZP * G * w]).then_inc(fill_done[s], 16)
                for s in range(2):
                    sp.wait_ge(fill_done[s], 16 * NFILL)

            @block.vector
            def _(ve):
                nc.vector.memset(zeros_t, 0.0).then_inc(zero_tile, 1)
                for s in range(2):
                    if s:
                        ve.wait_ge(keys_split, 4)
                    nc.vector.tensor_scalar(blki, raw[s], 7, None, ALU.logical_shift_right).then_inc(keys_split, 1)
                    nc.vector.tensor_scalar(loci, raw[s], 127, None, ALU.bitwise_and).then_inc(keys_split, 1)
                    ve.wait_ge(keys_split, 4 * s + 2)
                    nc.vector.tensor_copy(blkf[s], blki).then_inc(keys_split, 1)
                    nc.vector.tensor_scalar_add(keyf[s], loci, 1.0).then_inc(keys_split, 1)

                for s in range(2):
                    ve.wait_ge(pads_marked, s + 1)
                    with ve.Fori(0, HB) as i:
                        for u in range(2):
                            b = bass.ds(i * 2 + u, 1)
                            ve.wait_ge(picked[s].h, picked[s].free(i, u))
                            nc.vector.tensor_scalar(eqb[:, u, :], blkf[s], bidx[:, b], None, ALU.is_equal)\
                                .then_inc(hot[s].h, 1)
                            ve.wait_ge(hot[s].h, hot[s].done(i, u))
                            nc.vector.tensor_tensor_scan(scb[:, u, :], eqb[:, u, :], zrow, 0.0, ALU.add, ALU.add)\
                                .then_inc(ranked[s].h, 1)
                            ve.wait_ge(ranked[s].h, ranked[s].done(i, u))
                            nc.vector.tensor_copy(cnt[:, b], scb[:, u, T - 1:T]).then_inc(counted, 1)
                    c = 9 * s
                    ve.wait_ge(off_step, c + 1)
                    nc.vector.tensor_copy(tot, BK[7][:, 0:NBX]).then_inc(off_step, 1)
                    ve.wait_ge(off_step, c + 2)
                    nc.vector.tensor_scalar_add(toti, tot, float(G * P - 1)).then_inc(off_step, 1)
                    ve.wait_ge(off_step, c + 3)
                    nc.vector.tensor_scalar(toti2, toti, 8, None, ALU.logical_shift_right).then_inc(off_step, 1)
                    ve.wait_ge(off_step, c + 4)
                    nc.vector.tensor_copy(prs, toti2).then_inc(off_step, 1)
                    ve.wait_ge(off_step, c + 5)
                    nc.vector.tensor_tensor_scan(endp, prs, zrow[:, 0:NBX], 0.0, ALU.add, ALU.add)\
                        .then_inc(off_step, 1)
                    ve.wait_ge(off_step, c + 6)
                    nc.vector.tensor_tensor(offp, endp, prs, ALU.subtract).then_inc(off_step, 1)
                    ve.wait_ge(off_step, c + 7)
                    nc.vector.tensor_scalar(offp, offp, float(G * P), -1.0, ALU.mult, ALU.add).then_inc(off_step, 1)
                    ve.wait_ge(off_step, c + 8)
                    nc.vector.tensor_tensor(offp, offp, BK[7][:, 64:64 + NBX], ALU.add).then_inc(off_step, 1)
                    ve.wait_ge(off_step, c + 9)
                    ve.wait_ge(picked[s].h, picked[s].done(HB - 1, 1))
                    with ve.Fori(0, HB) as i:
                        for u in range(2):
                            b = bass.ds(i * 2 + u, 1)
                            ve.wait_ge(added2[s].h, added2[s].free(i, u))
                            nc.vector.tensor_scalar(eqb[:, u, :], blkf[s], bidx[:, b], offp[:, b],
                                                    ALU.is_equal, ALU.mult).then_inc(shifted[s].h, 1)
                    ve.wait_ge(added2[s].h, added2[s].done(HB - 1, 1) + 1)
                    if s:
                        ve.wait_ge(pos_ready, 1)
                    for lo, hi in TH:
                        nc.vector.tensor_copy(posf[:, lo:hi], BK[2 * s + (lo > 0)][:, 0:hi - lo]).then_inc(pos_done, 1)
                    nc.vector.memset(blkacc[:, 0, :], 0.0).then_inc(tbl_step, 1)
                    for b in range(NB):
                        ve.wait_ge(tbl_step, s * (NB + 2) + b + 1)
                        nc.vector.scalar_tensor_tensor(blkacc[:, (b + 1) % 2, :], jrow, endp[:, b:b + 1],
                                                       blkacc[:, b % 2, :], ALU.is_ge, ALU.add).then_inc(tbl_step, 1)
                    ve.wait_ge(tbl_step, s * (NB + 2) + NB + 1)
                    nc.vector.tensor_scalar_min(pair_block[s][:, :], blkacc[0:1, NB % 2, :], float(NB - 1))\
                        .then_inc(tbl_step, 1)
                    ve.wait_ge(pads_marked, 3 + s)
                    nc.vector.tensor_copy(posi[s], posf).then_inc(pos_ready, 1)
                    ve.wait_ge(tbl_step, (s + 1) * (NB + 2))

            @block.gpsimd
            def _(po):
                for s in range(2):
                    po.wait_ge(keys_split, 4 * s + 4)
                    nc.gpsimd.affine_select(out=blkf[s], in_=blkf[s], compare_op=ALU.is_ge, fill=float(NBX),
                                            base=E - 1, pattern=[[-1, T]], channel_multiplier=-T)\
                        .then_inc(pads_marked, 1)
                for s in range(2):
                    with po.Fori(0, HB) as i:
                        for u in range(2):
                            po.wait_ge(ranked[s].h, ranked[s].done(i, u))
                            po.sem_inc(pool_tick, 1)
                            po.wait_ge(added[s].h, added[s].free(i, u))
                            nc.gpsimd.tensor_tensor(tmb[:, u, :], eqb[:, u, :], scb[:, u, :], ALU.mult)\
                                .then_inc(picked[s].h, 1)
                    po.wait_ge(pos_done, len(TH) * (s + 1))
                    nc.gpsimd.affine_select(out=posf, in_=posf, compare_op=ALU.is_ge, fill=PADPOS,
                                            base=E - 1, pattern=[[-1, T]], channel_multiplier=-T)\
                        .then_inc(pads_marked, 1)

            @block.tensor
            def _(pe):
                for s in range(2):
                    def add(rows, **kw):
                        for n, (lo, hi) in enumerate(TH):
                            last = nc.tensor.matmul(BK[2 * s + n][:, 0:hi - lo], ident[:, :], rows[:, lo:hi], **kw)
                        return last

                    add(zrow, start=True, stop=False)
                    with pe.Fori(0, HB) as i:
                        for u in range(2):
                            pe.wait_ge(picked[s].h, picked[s].done(i, u))
                            add(tmb[:, u, :], start=False, stop=False).then_inc(added[s].h, 1)
                    pe.wait_ge(counted, NBX * (s + 1))
                    nc.tensor.matmul(BK[7][:, 0:NBX], ones[:, :], cnt, start=True, stop=True)
                    nc.tensor.matmul(BK[7][:, 64:64 + NBX], tril[:, :], cnt, start=True, stop=True)\
                        .then_inc(off_step, 1)
                    with pe.Fori(0, HB) as i:
                        for u in range(2):
                            pe.wait_ge(shifted[s].h, shifted[s].done(i, u))
                            add(eqb[:, u, :], start=False, stop=False).then_inc(added2[s].h, 1)
                    add(zrow, start=False, stop=True).then_inc(added2[s].h, 1)

        attr_in = [sem(f"attr_in{u}") for u in range(2)]
        placed = [sem(f"placed{u}") for u in range(2)]
        staged = sig("staged")
        stage_i = stage.bitcast(i32)
        with nc.Block() as block:
            @block.sync
            def _(sp):
                start(sp)

                def attr(i, u, first):
                    if not first:
                        sp.wait_ge(placed[u], i * (32 * CH))
                        sp.sem_inc(sp_tick, 1)
                    sp.dma_start(stage[:, u, :, 2:89], attrs_v[:, i, u, :, :]).then_inc(attr_in[u], 16)

                for u in range(2):
                    attr(0, u, True)
                with sp.Fori(1, NCH // 2) as i:
                    for u in range(2):
                        attr(i, u, False)

            @block.vector
            def _(ve):
                def fields(i, u, first):
                    if not first:
                        ve.wait_ge(placed[u], i * (32 * CH))
                    c = bass.ds(i * (2 * CH) + u * CH, CH)
                    nc.vector.tensor_copy(stage[:, u, :, 0], keyf[0][:, c])
                    nc.vector.tensor_copy(stage_i[:, u, :, 1], raw[1][:, c])
                    nc.vector.tensor_copy(stage_i[:, u, :, 89], raw[0][:, c])
                    nc.vector.tensor_copy(stage[:, u, :, 90], keyf[1][:, c])
                    nc.vector.tensor_copy(sidx[:, u, 0, :], posi[0][:, c])
                    nc.vector.tensor_copy(sidx[:, u, 1, :], posi[1][:, c]).then_inc(staged.h, 1)

                for u in range(2):
                    fields(0, u, True)
                with ve.Fori(1, NCH // 2) as i:
                    for u in range(2):
                        fields(i, u, False)

            @block.gpsimd
            def _(po):
                with po.Fori(0, NCH // 2) as i:
                    for u in range(2):
                        po.wait_ge(attr_in[u], i * 16 + 16)
                        po.sem_inc(pool_tick, 1)
                        po.wait_ge(staged.h, staged.done(i, u))
                        po.sem_inc(pool_tick, 1)
                        for c in range(CH):
                            for s, table, lo, w in ((0, rec_dst, 0, RD), (1, rec_src, 22, RS)):
                                nc.gpsimd.indirect_dma_start(
                                    out=table[:, :], out_offset=IOff(ap=sidx[:, u, s, c:c + 1], axis=0),
                                    in_=stage[:, u, c, lo:lo + w], in_offset=None,
                                    bounds_check=NP * G * P - 1, oob_is_err=False).then_inc(placed[u], 16)
                for u in range(2):
                    po.wait_ge(placed[u], (NCH // 2) * 32 * CH)



        def product_pool(L, sv, u, slot):
            v = sv[:, :, 64:160].rearrange("p g (i c) -> p g i c", i=3)

            def bc(lo, hi):
                return yx[:, u, :, lo:hi].unsqueeze(3).to_broadcast([P, G, hi - lo, 32])
            if L.cross:
                for g in range(G):
                    nc.gpsimd.tensor_tensor(t_cr[:, slot, g, 0:2, :], v[:, g, 1:3, :], bc(2, 4)[:, g], ALU.mult)
                nc.gpsimd.tensor_tensor(t_cr[:, slot, :, 2, :], v[:, :, 0, :], bc(4, 5)[:, :, 0], ALU.mult)
            for g in range(G):
                last = nc.gpsimd.tensor_tensor(t_dot[:, slot, g], v[:, g], bc(0, 3)[:, g], ALU.mult)
            return last

        def product_vector(ve, L, i, u, sv, w, y0, slot, pooled, part1, part2):
            s, v = sv[:, :, 0:64], sv[:, :, 64:160].rearrange("p g (i c) -> p g i c", i=3)
            t = tp[:, slot]
            tv = t[:, :, 96:96 + 3 * L.vs].rearrange("p g (i f) -> p g i f", i=3)

            def bc(lo, hi, c):
                return yx[:, u % 4, :, lo:hi].unsqueeze(3).to_broadcast([P, G, hi - lo, c])

            def axes(a, c):
                return a.unsqueeze(2).to_broadcast([P, G, 3, c])

            if w is None:
                ws, wsv, wv = y0.to_broadcast([P, G, 64]), s, y0.to_broadcast([P, G, 32])
            elif y0 is None:
                ws, wsv, wv = w[:, :, 0:64], t_sv[:, :, :], w[:, :, 128:160]
            else:
                ws, wsv, wv = wy[:, :, 0:64], t_sv[:, :, :], wy[:, :, 64:96]
                nc.vector.tensor_tensor(ws, w[:, :, 0:64], y0.to_broadcast([P, G, 64]), ALU.mult)
                nc.vector.tensor_tensor(wv, w[:, :, 128:160], y0.to_broadcast([P, G, 32]), ALU.mult)
            if w is not None:
                nc.vector.tensor_tensor(wsv, w[:, :, 64:128], s, ALU.mult)
            if L.cross:
                nc.vector.tensor_tensor(t_cr2[:, :, 0:1, :], v[:, :, 2:3, :], bc(1, 2, 32), ALU.mult)
                nc.vector.tensor_tensor(t_cr2[:, :, 1:3, :], v[:, :, 0:2, :], bc(2, 4, 32), ALU.mult)
            ve.wait_ge(pooled.h, pooled.done(i, u))
            nc.vector.tensor_tensor(t_sum[:, :, :], t_dot[:, slot, :, 0, :], t_dot[:, slot, :, 1, :], ALU.add)\
                .then_inc(part1.h, 1)
            ve.wait_ge(part1.h, part1.done(i, u))
            dot = t[:, :, 64:96] if w is None else t_sum2[:, :, :]
            nc.vector.tensor_tensor(dot, t_sum[:, :, :], t_dot[:, slot, :, 2, :], ALU.add)
            if L.cross:
                cr = tv[:, :, :, 96:128] if w is None else t_cr3[:, :, :, :]
                nc.vector.tensor_tensor(cr, t_cr[:, slot], t_cr2[:, :, :, :], ALU.subtract)
            nc.vector.tensor_tensor(t[:, :, 0:64], ws, s, ALU.mult)
            nc.vector.tensor_tensor(tv[:, :, :, 0:64], axes(wsv, 64), bc(0, 3, 64), ALU.mult)
            last = nc.vector.tensor_tensor(tv[:, :, :, 64:96], v, axes(wv, 32), ALU.mult)
            if w is None:
                return last
            last.then_inc(part2.h, 1)
            ve.wait_ge(part2.h, part2.done(i, u))
            if L.cross:
                nc.vector.tensor_tensor(tv[:, :, :, 96:128], t_cr3[:, :, :, :], axes(w[:, :, 192:224], 32), ALU.mult)
            return nc.vector.tensor_tensor(t[:, :, 64:96], t_sum2[:, :, :], w[:, :, 160:192], ALU.mult)

        def directions(po, L, i, u, y_step, y_ready):
            s4 = u % 4
            r = rec[:, s4, :, L.y:L.y + 3]
            k = [0]

            def step(ins):
                k[0] += 1
                ins.then_inc(y_step.h, 1)
                po.wait_ge(y_step.h, y_step.done(i, u, k[0]))
                po.sem_inc(pool_tick, 1)

            if L.n == 1:
                step(nc.gpsimd.tensor_tensor(ysq[:, u % 2], r, r, ALU.mult))
                step(nc.gpsimd.tensor_tensor(yn[:, u % 2], ysq[:, u % 2, :, 0], ysq[:, u % 2, :, 1], ALU.add))
                step(nc.gpsimd.tensor_tensor(yr[:, u % 2], yn[:, u % 2], ysq[:, u % 2, :, 2], ALU.add))
                step(nc.gpsimd.tensor_scalar(yn[:, u % 2], rec[:, s4, :, L.key], 0.0, None, ALU.is_equal))
                step(nc.gpsimd.tensor_tensor(yr[:, u % 2], yr[:, u % 2], yn[:, u % 2], ALU.add))
                step(nc.gpsimd.tensor_tensor(yn[:, u % 2], yr[:, u % 2], mhalf[:, :], ALU.pow))
                step(nc.gpsimd.tensor_tensor(yx[:, s4, :, 0:3], r, yn[:, u % 2].unsqueeze(2).to_broadcast([P, G, 3]),
                                             ALU.mult))
                nc.gpsimd.tensor_copy(yx[:, s4, :, 3:5], yx[:, s4, :, 0:2]).then_inc(y_ready.h, 1)
            else:
                nc.gpsimd.tensor_copy(yx[:, s4, :, 0:3], r)
                nc.gpsimd.tensor_copy(yx[:, s4, :, 3:5], rec[:, s4, :, L.y:L.y + 2]).then_inc(y_ready.h, 1)

        class Layer:
            pass

        def layer(n):
            L = Layer()
            L.n = n
            L.src_order = n == 1
            L.records = rec_src_v if n == 1 else rec_dst_v
            L.head = (64, 5) if n == 1 else (0, 6)
            L.ef, L.efw = {0: (6, 16), 1: (0, 64), 2: (6, 16), 3: (22, 64)}[n]
            L.idx, L.key, L.y = (3, 4, 0) if n == 1 else (1, 0, 3)
            L.y0 = None if n == 1 else 2
            L.cross = n != 2
            L.vs = 128 if L.cross else 96
            L.width = 96 + 3 * L.vs + (n == 2)
            L.blocks = pair_block[1 if n == 1 else 0]
            return L

        def load_records(sp, L, i, u, done):
            lo, w = L.head
            sp.dma_start(rec[:, u, :, 0:w], L.records[i, u, :, :, lo:lo + w]).then_inc(done, 16)
            sp.dma_start(efr[:, u, 0:G * L.efw].rearrange("p (g f) -> p g f", g=G),
                         L.records[i, u, :, :, L.ef:L.ef + L.efw]).then_inc(done, 16)

        def edge_loop(L):
            rec_in = [mark(f"rec_in{u}", 32 * QP) for u in range(4)]
            gat_in = [mark(f"gat_in{u}", 32 * QP) for u in range(4)]
            y_ready = sig4("y_ready", 1, NP)
            y_step = sig4("y_step", 7, NP if L.n == 1 else 0)
            pooled = sig4("pooled", 1, NP)
            ef_t = sig4("ef_t", 1, NP)
            ef_ready = sig4("ef_ready", 1, NP)
            hid = sig4("hid", 1, NP)
            hid_ready = sig4("hid_ready", 1, NP)
            w_ready = sig4("w_ready", 1, NP)
            part1 = sig4("part1", 1, NP)
            part2 = sig4("part2", 1, NP)
            tp_ready = sig4("tp_ready", 1, NP)
            summed = sig4("summed", 1, NP)
            kept = sig4("kept", 1, NP)
            zeroed = mark("sums_zeroed", 1 + (L.n == 2))
            TW = L.width
            fc1, fc2 = W[f"fc1_{L.n}"], W[f"fc2_{L.n}"]
            EW = G * L.efw
            pE, pH, pW, pS = BK[0], BK[1], [BK[2], BK[3]], [BK[4], BK[5]]

            def w_of(u):
                return pW[u % 2][:, 0:448].rearrange("p (g f) -> p g f", g=G)

            with nc.Block() as block:
                @block.sync
                def _(sp):
                    start(sp)

                    def records(i, u, first=False):
                        if not first:
                            sp.wait_ge(tp_ready.h, tp_ready.free(i, u, 4))
                            sp.sem_inc(sp_tick, 1)
                        load_records(sp, L, i, u, rec_in[u].h)

                    for u in range(4):
                        records(0, u, True)
                    with sp.Fori(1, QP) as i:
                        for u in range(4):
                            records(i, u)

                @block.gpsimd
                def _(po):
                    if L.n == 2:
                        nc.gpsimd.memset(tp[:, :, :, 384:385], 1.0).then_inc(zeroed.h, 1)

                    def gather(i, u):
                        po.wait_ge(rec_in[u].h, rec_in[u].at(i * 32 + 32))
                        po.sem_inc(pool_tick, 1)
                        po.wait_ge(tp_ready.h, tp_ready.free(i, u, 4))
                        po.sem_inc(pool_tick, 1)
                        for g in range(G):
                            nc.gpsimd.indirect_dma_start(
                                out=gat[:, u, g, :], out_offset=None, in_=tables[L.n][:, :],
                                in_offset=IOff(ap=rec[:, u, g, L.idx:L.idx + 1].bitcast(i32), axis=0))\
                                .then_inc(gat_in[u].h, 16)
                        directions(po, L, i, u, y_step, y_ready)

                    def part(i, u):
                        po.wait_ge(gat_in[u].h, gat_in[u].at(i * 32 + 32))
                        po.sem_inc(pool_tick, 1)
                        po.wait_ge(tp_ready.h, tp_ready.free(i, u))
                        po.sem_inc(pool_tick, 1)
                        po.wait_ge(y_ready.h, y_ready.done(i, u))
                        product_pool(L, gat[:, u], u, u % 2).then_inc(pooled.h, 1)

                    for u in range(3):
                        gather(0, u)
                    with po.Fori(0, QP - 1) as i:
                        for u in range(4):
                            part(i, u)
                            gather(*((i, 3) if u == 0 else (i + 1, u - 1)))
                    for u in range(4):
                        part(QP - 1, u)
                        if u == 0:
                            gather(QP - 1, 3)

                @block.scalar
                def _(ac):
                    def front(i, u):
                        ac.wait_ge(ef_t.h, ef_t.done(i, u))
                        nc.scalar.activation(efT[0:EW, u % 2, :], pE[0:EW, 128 * (u % 2):128 * (u % 2) + 128], ACT.Copy)\
                            .then_inc(ef_ready.h, 1)
                        ac.wait_ge(hid.h, hid.done(i, u))
                        func, by = {1: (ACT.Relu, 1.0), 2: (ACT.Silu, 0.25), 3: (ACT.Silu, 0.125)}[L.n]
                        nc.scalar.activation(hT[:, u % 2, :], pH[:, 128 * (u % 2):128 * (u % 2) + 128], func, scale=by)\
                            .then_inc(hid_ready.h, 1)

                    with ac.Fori(0, QP) as i:
                        for u in range(4):
                            front(i, u)

                @block.tensor
                def _(pe):
                    def transposed(i, u):
                        pe.wait_ge(rec_in[u].h, rec_in[u].at(i * 32 + 32))
                        pe.wait_ge(ef_ready.h, ef_ready.free(i, u))
                        c = 128 * (u % 2)
                        nc.tensor.transpose(pE[0:EW, c:c + 128], efr[:, u, 0:G * L.efw],
                                            ident[:, :]).then_inc(ef_t.h, 1)

                    def hidden(i, u):
                        pe.wait_ge(ef_ready.h, ef_ready.done(i, u))
                        pe.wait_ge(hid_ready.h, hid_ready.free(i, u))
                        c = 128 * (u % 2)
                        nc.tensor.matmul(pH[:, c:c + 128], fc1[0:EW, :], efT[0:EW, u % 2, :],
                                         start=True, stop=True).then_inc(hid.h, 1)

                    def weights(i, u):
                        pe.wait_ge(hid_ready.h, hid_ready.done(i, u))
                        pe.wait_ge(tp_ready.h, tp_ready.free(i, u))
                        nc.tensor.matmul(pW[u % 2][:, 0:448], hT[:, u % 2, :], fc2[:, :], start=True, stop=True)\
                            .then_inc(w_ready.h, 1)

                    def sums(i, u, g):
                        if g == 0:
                            pe.wait_ge(tp_ready.h, tp_ready.done(i, u))
                            pe.wait_ge(kept.h, kept.free(i, u))
                        last = nc.tensor.matmul(pS[u % 2][:, 0:TW], oh[:, u, g, :], tp[:, u % 2, g, 0:TW],
                                                start=g == 0, stop=g == G - 1)
                        if g == G - 1:
                            last.then_inc(summed.h, 1)

                    for u in range(2):
                        transposed(0, u)
                        hidden(0, u)
                        weights(0, u)
                    def both(i, u):
                        ahead = (i, u + 2) if u < 2 else (i + 1, u - 2)
                        transposed(*ahead)
                        sums(i, u, 0)
                        hidden(*ahead)
                        sums(i, u, 1)
                        weights(*ahead)

                    with pe.Fori(0, QP - 1) as i:
                        for u in range(4):
                            both(i, u)
                    for u in range(2):
                        both(QP - 1, u)
                    for u in range(2, 4):
                        for g in range(G):
                            sums(QP - 1, u, g)

                @block.vector
                def _(ve):
                    nc.vector.memset(ACC[:, 0:NBX * TW], 0.0).then_inc(zeroed.h, 1)
                    acc = ACC[:, 0:NBX * TW].rearrange("p (b f) -> p b f", b=NBX)

                    def product(i, u):
                        ve.wait_ge(rec_in[u].h, rec_in[u].at(i * 32 + 32))
                        ve.wait_ge(summed.h, summed.free(i, u))
                        for g in range(G):
                            nc.vector.tensor_scalar(oh[:, u, g, :], iota1[:, :], rec[:, u, g, L.key:L.key + 1],
                                                    None, ALU.is_equal)
                        ve.wait_ge(w_ready.h, w_ready.done(i, u))
                        ve.wait_ge(gat_in[u].h, gat_in[u].at(i * 32 + 32))
                        ve.wait_ge(y_ready.h, y_ready.done(i, u))
                        y0 = None if L.y0 is None else rec[:, u, :, L.y0:L.y0 + 1]
                        product_vector(ve, L, i, u, gat[:, u], w_of(u), y0, u % 2, pooled, part1, part2)\
                            .then_inc(tp_ready.h, 1)

                    def keep(i, u):
                        ve.wait_ge(summed.h, summed.done(i, u))
                        b = ve.value_load(L.blocks[0:1, bass.ds(i * 4 + u, 1)], min_val=0, max_val=NB - 1)
                        row = acc[:, bass.ds(b, 1), :].rearrange("p o f -> p (o f)")
                        ve.wait_ge(kept.h, kept.free(i, u, 1))
                        nc.vector.tensor_tensor(row, row, pS[u % 2][:, 0:TW], ALU.add).then_inc(kept.h, 1)

                    ve.wait_ge(zeroed.h, zeroed.at(1 + (L.n == 2)))
                    product(0, 0)
                    with ve.Fori(0, QP - 1) as i:
                        for u in range(4):
                            product(*((i, u + 1) if u < 3 else (i + 1, 0)))
                            keep(i, u)
                    for u in range(4):
                        if u < 3:
                            product(QP - 1, u + 1)
                        keep(QP - 1, u)
                    ve.wait_ge(kept.h, kept.done(QP - 1, 3))

        HNB = NBX // 2

        def node_table(n):
            rows = sig("rows", 1, NBX)
            rows_t = sig("rows_t", 1, NBX)
            rowsT = sig("rowsT", 1, NBX)
            made = sig("made", 1, NBX)
            tb_ready = sig("tb_ready", 1, NBX)
            normed = sig("normed", 1, NBX if n else 0)
            rooted = mark("rooted", 1 if n else 2)
            rstd_ready = mark("rstd_ready", 2 if n else 3)
            stored = [mark(f"stored{u}", 16 * (NBX // 2)) for u in range(2)]
            ts, tv_ = W[f"ts{n}"], W[f"tv{n}"]
            SW, VW = (128, 192) if n == 0 else (64, 96)
            TD = ACC[:, 8400:8400 + NBX * F].rearrange("p (b f) -> p b f", b=NBX)
            pT, pM = [BK[0], BK[1]], [BK[2], BK[3]]
            with nc.Block() as block:
                @block.scalar
                def _(ac):
                    ac.wait_ge(rstd_ready.h, rstd_ready.at(1))
                    nc.scalar.activation(rstd[:, :], rstd[:, :], ACT.Sqrt).then_inc(rooted.h, 1)
                    if n == 0:
                        nc.scalar.activation(rstd_v[:, :], rstd_v[:, :], ACT.Sqrt).then_inc(rooted.h, 1)

                    def copies(i, u):
                        ac.wait_ge(rows_t.h, rows_t.done(i, u))
                        ac.wait_ge(made.h, made.free(i, u))
                        if n == 0:
                            nc.scalar.activation(xT[0:64, u, 0:128], pT[u][0:64, 0:128], ACT.Identity,
                                                 bias=W["bet_s"][:, :], scale=W["gam_s"][:, :])
                            nc.scalar.activation(xT[0:96, u, 128:256], pT[u][0:96, 128:256], ACT.Copy,
                                                 scale=W["gam_v"][:, :]).then_inc(rowsT.h, 1)
                        else:
                            nc.scalar.activation(xT[0:64, u, 0:128], pT[u][0:64, 0:128], ACT.Copy)
                            nc.scalar.activation(xT[0:96, u, 128:256], pT[u][0:96, 128:256], ACT.Copy)\
                                .then_inc(rowsT.h, 1)

                    with ac.Fori(0, HNB) as i:
                        for u in range(2):
                            copies(i, u)

                @block.vector
                def _(ve):
                    first = nc.vector.tensor_scalar_add(rstd[:, :], stat[:, :, 1], EPS)
                    if n != 0:
                        first.then_inc(rstd_ready.h, 1)
                    else:
                        nc.vector.tensor_scalar(rstd_v[:, :], vsq[:, :], 1.0 / CV, EPS, ALU.mult, ALU.add)\
                            .then_inc(rstd_ready.h, 1)
                    ve.wait_ge(rooted.h, rooted.at(2 if n == 0 else 1))
                    nc.vector.reciprocal(rstd[:, :], rstd[:, :]).then_inc(rstd_ready.h, 1)
                    if n == 0:
                        nc.vector.reciprocal(rstd_v[:, :], rstd_v[:, :]).then_inc(rstd_ready.h, 1)
                    ve.wait_ge(rstd_ready.h, rstd_ready.at(3 if n == 0 else 2))

                    def norm(i, u):
                        b = i * 2 + u
                        xb = X[:, bass.ds(b, 1), :].rearrange("p o f -> p (o f)")
                        mu = stat[:, bass.ds(b, 1), 0]
                        rs = rstd[:, bass.ds(b, 1)]
                        ve.wait_ge(rows_t.h, rows_t.free(i, u))
                        xv = xn[:, u, 64:160].rearrange("p (i c) -> p i c", i=3)
                        src = X[:, bass.ds(b, 1), 64:160].rearrange("p o (c i) -> p i (o c)", i=3)
                        if n == 0:
                            nc.vector.tensor_scalar(xn[:, u, 0:64], X[:, bass.ds(b, 1), 0:64].rearrange(
                                "p o f -> p (o f)"), mu, rs, ALU.subtract, ALU.mult)
                            nc.vector.tensor_scalar(xv, src, rstd_v[:, bass.ds(b, 1)], None, ALU.mult)\
                                .then_inc(rows.h, 1)
                        else:
                            nc.vector.tensor_scalar(xb, xb, mu, rs, ALU.subtract, ALU.mult).then_inc(normed.h, 1)
                            ve.wait_ge(normed.h, normed.done(i, u))
                            ve.sem_inc(ve_tick, 1)
                            nc.vector.tensor_copy(xn[:, u, 0:64], X[:, bass.ds(b, 1), 0:64].rearrange(
                                "p o f -> p (o f)"))
                            nc.vector.tensor_copy(xv, src).then_inc(rows.h, 1)

                    def table(i, u):
                        b = i * 2 + u
                        ve.wait_ge(made.h, made.done(i, u))
                        if not (isinstance(i, int) and i == 0):
                            ve.wait_ge(stored[u].h, stored[u].at(i * 16))
                            ve.sem_inc(ve_tick, 1)
                        if n == 0:
                            ve.sem_inc(ve_tick, 1)
                            nc.vector.tensor_copy(TD[:, bass.ds(b, 1), 0:64].rearrange("p o f -> p (o f)"),
                                                  pM[u][:, 64:128])
                            nc.vector.tensor_copy(TD[:, bass.ds(b, 1), 64:160].rearrange("p o f -> p (o f)"),
                                                  pM[u][:, 224:320])
                            nc.vector.tensor_copy(tb[:, u, 0:64], pM[u][:, 0:64])
                            nc.vector.tensor_copy(tb[:, u, 64:160], pM[u][:, 128:224]).then_inc(tb_ready.h, 1)
                        elif n == 1:
                            nc.vector.tensor_copy(tb[:, u, :], pM[u][:, 0:160]).then_inc(tb_ready.h, 1)
                        else:
                            nc.vector.tensor_scalar(tb[:, u, :], pM[u][:, 0:160], node_a[:, bass.ds(b, 1)], None,
                                                    ALU.mult).then_inc(tb_ready.h, 1)

                    norm(0, 0)
                    norm(0, 1)
                    table(0, 0)
                    table(0, 1)
                    with ve.Fori(1, HNB) as i:
                        norm(i, 0)
                        norm(i, 1)
                        table(i, 0)
                        table(i, 1)

                @block.tensor
                def _(pe):
                    def turn(i, u):
                        pe.wait_ge(rows.h, rows.done(i, u))
                        pe.wait_ge(rowsT.h, rowsT.free(i, u))
                        nc.tensor.transpose(pT[u][0:96, 128:256], xn[:, u, 64:160], ident[:, :])
                        nc.tensor.transpose(pT[u][0:64, 0:128], xn[:, u, 0:64], ident[:, :]).then_inc(rows_t.h, 1)

                    def make(i, u):
                        pe.wait_ge(rowsT.h, rowsT.done(i, u))
                        pe.wait_ge(tb_ready.h, tb_ready.free(i, u))
                        nc.tensor.matmul(pM[u][:, 0:SW], xT[0:64, u, 0:128], ts[:, :], start=True, stop=True)
                        nc.tensor.matmul(pM[u][:, SW:SW + VW], xT[0:96, u, 128:256], tv_[:, :], start=True, stop=True)\
                            .then_inc(made.h, 1)

                    with pe.Fori(0, HNB) as i:
                        for u in range(2):
                            turn(i, u)
                        for u in range(2):
                            make(i, u)

                @block.sync
                def _(sp):
                    start(sp)
                    with sp.Fori(0, HNB) as i:
                        for u in range(2):
                            sp.wait_ge(tb_ready.h, tb_ready.done(i, u))
                            sp.sem_inc(sp_tick, 1)
                            sp.dma_start(tables_v[n][i, u], tb[:, u, :]).then_inc(stored[u].h, 16)
                    for u in range(2):
                        sp.wait_ge(stored[u].h, stored[u].at(HNB * 16))

        def statistics(ve, i, u, cols, seen):
            b = i * 2 + u
            x = X[:, bass.ds(b, 1), 0:cols].rearrange("p o f -> p (o f)")
            nc.vector.bn_stats(bn6[:, u, :], x).then_inc(seen.h, 1)
            ve.wait_ge(seen.h, seen.done(i, u, 1))
            ve.sem_inc(ve_tick, 1)
            nc.vector.bn_aggr(mean_var[:, u, :], bn6[:, u, :]).then_inc(seen.h, 1)
            ve.wait_ge(seen.h, seen.done(i, u, 2))
            ve.sem_inc(ve_tick, 1)
            nc.vector.tensor_copy(stat[:, bass.ds(b, 1), :].rearrange("p o f -> p (o f)"), mean_var[:, u, :])

        def node_update(L):
            n = L.n
            copied_in = sig("copied_in", 1, NBX)
            turned = sig("turned", 1, NBX)
            copied = sig("copied", 1, NBX)
            made = sig("made", 1, NBX)
            gated = sig("gated_out", 1, NBX)
            upd = sig("upd", 3, NBX if n == 2 else 0)
            alpha_made = sig("alpha_made", 1, NBX if n == 2 else 0)
            y_made = sig("y_made", 1, NBX)
            updated = sig("updated", 1, NBX)
            seen = sig("seen", 2, NBX)
            pX_, pA, pO = [BK[0], BK[1]], [BK[2], BK[3]], [BK[4], BK[5]]
            TW, VS = L.width, L.vs
            acc = ACC[:, 0:NBX * TW].rearrange("p (b f) -> p b f", b=NBX)
            nS = 64 if n == 2 else 96
            with nc.Block() as block:
                @block.vector
                def _(ve):
                    def rows(i, u):
                        b = bass.ds(i * 2 + u, 1)
                        ve.wait_ge(turned.h, turned.free(i, u))
                        ve.sem_inc(ve_tick, 1)
                        if n == 2:
                            c = acc[:, b, 384:385].rearrange("p o f -> p (o f)")
                            nc.vector.tensor_scalar_max(nrm[:, u, 0:1], c, 1.0).then_inc(upd.h, 1)
                            ve.wait_ge(upd.h, upd.done(i, u, 1))
                            nc.vector.reciprocal(nrm[:, u, 1:2], nrm[:, u, 0:1]).then_inc(upd.h, 1)
                            ve.wait_ge(upd.h, upd.done(i, u, 2))
                            nc.vector.tensor_scalar(nrm[:, u, 2:3], nrm[:, u, 1:2], node_a[:, b], None, ALU.mult)\
                                .then_inc(upd.h, 1)
                            ve.wait_ge(upd.h, upd.done(i, u, 3))
                            ve.sem_inc(ve_tick, 1)
                        nc.vector.tensor_copy(xn[:, u, 64:160].rearrange("p (i c) -> p i c", i=3),
                                              X[:, b, 64:160].rearrange("p o (c i) -> p i (o c)", i=3))
                        nc.vector.tensor_copy(xn[:, u, 0:64], X[:, b, 0:64].rearrange("p o f -> p (o f)"))
                        a = acc[:, b, 0:96 + 3 * VS].rearrange("p o f -> p (o f)")
                        nc.vector.tensor_copy(accrow[:, u, 0:96 + 3 * VS], a).then_inc(copied_in.h, 1)

                    def outputs(i, u):
                        b = bass.ds(i * 2 + u, 1)
                        ys = y_s[:, u, 0:64]
                        yv = y_s[:, u, 64:160].rearrange("p (i c) -> p i c", i=3)
                        a = node_a[:, b]
                        if n == 2:
                            ve.wait_ge(made.h, made.done(i, u))
                            nc.vector.tensor_scalar(nrm[:, u, 3:4], pO[u][:, 224:225], nrm[:, u, 2:3], nrm[:, u, 2:3],
                                                    ALU.mult, ALU.mult).then_inc(alpha_made.h, 1)
                            ve.wait_ge(alpha_made.h, alpha_made.done(i, u))
                            nc.vector.tensor_scalar(y_s[:, u, 0:64], pO[u][:, 160:224], nrm[:, u, 3:4], None, ALU.mult)
                            nc.vector.tensor_scalar(y_s[:, u, 64:160], pO[u][:, 225:321], nrm[:, u, 3:4], None,
                                                    ALU.mult).then_inc(gated.h, 1)
                            ve.wait_ge(gated.h, gated.done(i, u))
                            nc.vector.scalar_tensor_tensor(y_s[:, u, :], pO[u][:, 0:160], a, y_s[:, u, :],
                                                           ALU.mult, ALU.add).then_inc(y_made.h, 1)
                            ve.wait_ge(y_made.h, y_made.done(i, u))
                        else:
                            ve.wait_ge(gated.h, gated.done(i, u))
                            by = a if n == 3 else 1.0
                            nc.vector.scalar_tensor_tensor(ys, pO[u][:, 0:64], by, sgm[:, u, 0:64],
                                                           ALU.mult, ALU.mult)
                            nc.vector.scalar_tensor_tensor(
                                yv, pO[u][:, 96:192].rearrange("p (i c) -> p i c", i=3), by,
                                sgm[:, u, 64:96].unsqueeze(1).to_broadcast([P, 3, 32]), ALU.mult, ALU.mult)\
                                .then_inc(y_made.h, 1)
                            ve.wait_ge(y_made.h, y_made.done(i, u))
                        xs = X[:, b, 0:64].rearrange("p o f -> p (o f)")
                        xv = X[:, b, 64:160].rearrange("p o (c i) -> p i (o c)", i=3)
                        nc.vector.tensor_tensor(xs, xs, ys, ALU.add)
                        nc.vector.tensor_tensor(xv, xv, yv, ALU.add).then_inc(updated.h, 1)
                        ve.wait_ge(updated.h, updated.done(i, u))
                        ve.sem_inc(ve_tick, 1)
                        statistics(ve, i, u, F, seen)

                    with ve.Fori(0, HNB) as i:
                        rows(i, 0)
                        rows(i, 1)
                        outputs(i, 0)
                        outputs(i, 1)

                @block.tensor
                def _(pe):
                    def turn(i, u):
                        pe.wait_ge(copied_in.h, copied_in.done(i, u))
                        pe.wait_ge(copied.h, copied.free(i, u))
                        nc.tensor.transpose(pX_[u][0:96, 128:256], xn[:, u, 64:160], ident[:, :])
                        nc.tensor.transpose(pX_[u][0:64, 0:128], xn[:, u, 0:64], ident[:, :])
                        nc.tensor.transpose(pA[u][0:96, 0:128], accrow[:, u, 0:96], ident[:, :])
                        for k in range(3):
                            last = nc.tensor.transpose(pA[u][0:VS, 128 * k + 128:128 * k + 256],
                                                       accrow[:, u, 96 + VS * k:96 + VS * k + VS], ident[:, :])
                        last.then_inc(turned.h, 1)

                    def make(i, u):
                        pe.wait_ge(copied.h, copied.done(i, u))
                        pe.wait_ge(updated.h, updated.free(i, u))
                        xs, xv, os_, ov = (W[k + str(n)] for k in ("xs", "xv", "os", "ov"))
                        o_ = pO[u]
                        if n == 2:
                            nc.tensor.matmul(o_[:, 0:64], xT[0:64, u, 0:128], xs[:, :], start=True, stop=True)
                            nc.tensor.matmul(o_[:, 64:160], xT[0:96, u, 128:256], xv[:, :], start=True, stop=True)
                            nc.tensor.matmul(o_[:, 160:225], aT[0:96, u, 0:128], os_[:, :], start=True, stop=True)
                            for k in range(3):
                                last = nc.tensor.matmul(o_[:, 225 + 32 * k:257 + 32 * k],
                                                        aT[0:96, u, 128 * k + 128:128 * k + 256], ov[:, :],
                                                        start=True, stop=True)
                        else:
                            nc.tensor.matmul(o_[:, 0:96], xT[0:64, u, 0:128], xs[:, :], start=True, stop=False)
                            nc.tensor.matmul(o_[:, 0:96], aT[0:96, u, 0:128], os_[:, :], start=False, stop=True)
                            for k in range(3):
                                oc = slice(96 + 32 * k, 128 + 32 * k)
                                nc.tensor.matmul(o_[:, oc], xT[0:96, u, 128:256], xv[:, 32 * k:32 * k + 32],
                                                 start=True, stop=False)
                                last = nc.tensor.matmul(o_[:, oc], aT[:, u, 128 * k + 128:128 * k + 256], ov[:, :],
                                                        start=False, stop=True)
                        last.then_inc(made.h, 1)

                    with pe.Fori(0, HNB) as i:
                        for u in range(2):
                            turn(i, u)
                        for u in range(2):
                            make(i, u)

                @block.scalar
                def _(ac):
                    with ac.Fori(0, HNB) as i:
                        for u in range(2):
                            ac.wait_ge(turned.h, turned.done(i, u))
                            ac.wait_ge(made.h, made.free(i, u))
                            nc.scalar.activation(xT[0:64, u, 0:128], pX_[u][0:64, 0:128], ACT.Copy)
                            nc.scalar.activation(xT[0:96, u, 128:256], pX_[u][0:96, 128:256], ACT.Copy)
                            nc.scalar.activation(aT[0:96, u, 0:128], pA[u][0:96, 0:128], ACT.Copy)
                            nc.scalar.activation(aT[0:VS, u, 128:512], pA[u][0:VS, 128:512], ACT.Copy)\
                                .then_inc(copied.h, 1)
                        for u in range(2):
                            if n == 2:
                                continue
                            ac.wait_ge(made.h, made.done(i, u))
                            ac.wait_ge(updated.h, updated.free(i, u))
                            by = node_a[:, bass.ds(i * 2 + u, 1)] if n == 3 else 1.0
                            nc.scalar.activation(sgm[:, u, :], pO[u][:, 0:96], ACT.Sigmoid, scale=by)\
                                .then_inc(gated.h, 1)

                @block.sync
                def _(sp):
                    start(sp)

        def last_norm():
            rooted = mark("rooted", 1)
            rstd_ready = mark("rstd_ready", 2)
            normed = sig("normed", 1, NBX)
            out_done = sem("out_done")
            with nc.Block() as block:
                @block.scalar
                def _(ac):
                    ac.wait_ge(rstd_ready.h, rstd_ready.at(1))
                    nc.scalar.activation(rstd[:, :], rstd[:, :], ACT.Sqrt).then_inc(rooted.h, 1)

                @block.vector
                def _(ve):
                    nc.vector.tensor_scalar_add(rstd[:, :], stat[:, :, 1], EPS).then_inc(rstd_ready.h, 1)
                    ve.wait_ge(rooted.h, rooted.at(1))
                    nc.vector.reciprocal(rstd[:, :], rstd[:, :]).then_inc(rstd_ready.h, 1)
                    ve.wait_ge(rstd_ready.h, rstd_ready.at(2))
                    with ve.Fori(0, HNB) as i:
                        for u in range(2):
                            b = bass.ds(i * 2 + u, 1)
                            xb = X[:, b, :].rearrange("p o f -> p (o f)")
                            nc.vector.tensor_scalar(xb, xb, stat[:, b, 0], rstd[:, b], ALU.subtract, ALU.mult)\
                                .then_inc(normed.h, 1)

                @block.sync
                def _(sp):
                    start(sp)
                    sp.wait_ge(normed.h, normed.done(HNB - 1, 1))
                    if NB > 1:
                        sp.dma_start(out[0:(NB - 1) * P, :].rearrange("(b p) f -> p b f", p=P), X[:, 0:NB - 1, :])\
                            .then_inc(out_done, 16)
                    sp.dma_start(out[(NB - 1) * P:N, :], X[0:LAST, NB - 1, :]).then_inc(out_done, 16)
                    sp.wait_ge(out_done, 32 if NB > 1 else 16)

        def first_statistics():
            seen = sig("seen", 2, NBX)
            squared = sig("squared", 1, NBX)
            with nc.Block() as block:
                @block.sync
                def _(sp):
                    start(sp)

                @block.vector
                def _(ve):
                    with ve.Fori(0, HNB) as i:
                        for u in range(2):
                            statistics(ve, i, u, 64, seen)

                @block.scalar
                def _(ac):
                    with ac.Fori(0, HNB) as i:
                        for u in range(2):
                            b = bass.ds(i * 2 + u, 1)
                            ac.wait_ge(squared.h, squared.free(i, u))
                            nc.scalar.activation(y_s[:, u, 64:160], X[:, b, 64:160].rearrange("p o f -> p (o f)"),
                                                 ACT.Square, accum_out=vsq[:, b]).then_inc(squared.h, 1)

        def layer0_edges(L):
            rec_in = [mark(f"rec_in{u}", 32 * QP) for u in range(4)]
            gat_in = [mark(f"gat_in{u}", 32 * QP) for u in range(4)]
            y_step, y_ready = sig4("y_step", 7, 0), sig4("y_ready", 1, NP)
            pooled1, pooled2 = sig4("pooled", 1, NP), sig4("pooled2", 1, NP)
            oh_ready = sig4("oh_ready", 1, NP)
            turned = sig4("turned_e", 1, NP)
            copied = sig4("copied_e", 1, NP)
            w_ready = sig4("w_ready", 1, NP)
            dst_ready = sig4("dst_ready", 1, NP)
            msg_ready = sig4("msg_ready", 1, NP)
            part1a, part2a, tp1_ready = sig4("part1", 1, NP), sig4("part2", 1, NP), sig4("tp_ready", 1, NP)
            part1b, part2b, tp2_ready = sig4("part1b", 1, NP), sig4("part2b", 1, NP), sig4("tp2_ready", 1, NP)
            t1, t1c = sig4("t1", 2, NP), sig4("t1c", 2, NP)
            t2, t2c = sig4("t2", 2, NP), sig4("t2c", 2, NP)
            val_ready = sig4("val_ready", 1, NP)
            squashed = sig4("squashed", 1, NP)
            gate_step = sig4("gate_step", 1, NP)
            gated = sig4("gated_e", 1, NP)
            leak = sig4("leak", 3, NP)
            xm_ready = sig4("xm_ready", 1, NP)
            xm_t = sig4("xm_t", 2, NP)
            top = sig4("top", 2, NP)
            m_step, mnew_ready = sig4("m_step", 1, NP), sig4("mnew_ready", 1, NP)
            msc_ready = sig4("msc_ready", 1, NP)
            mg_ready = sig4("mg_ready", 1, NP)
            dlt_ready = sig4("dlt_ready", 1, NP)
            pex_ready = sig4("pex_ready", 1, NP)
            h_ready = sig4("h_ready", 1, NP)
            hw_ready = sig4("hw_ready", 1, NP)
            summed = sig4("summed", 1, NP)
            scaled = sig4("scaled", 1, NP)
            kept = sig4("kept", 1, NP)
            zeroed_acc = mark("sums_zeroed", 1)
            acc = ACC[:, 0:NBX * 164].rearrange("p (b f) -> p b f", b=NBX)
            M = ACC[:, 8200:8200 + NBX * 4].rearrange("p (b h) -> p b h", b=NBX)
            TD = ACC[:, 8400:8400 + NBX * F].rearrange("p (b f) -> p b f", b=NBX)
            pE, pW, pB, pT, pV, pX = BK[0], BK[1], BK[2], [BK[3], BK[4]], BK[5], BK[6]
            pH, pG, pS = BK[7][:, 0:320], BK[7][:, 320:328], BK[7][:, 328:492]
            pVv = pV[:, :].rearrange("p (g f) -> p g f", g=G)
            pHv = pH.rearrange("p (g f) -> p g f", g=G)
            mT1, mT2 = mT, mTb

            def flat(a):
                return a.rearrange("p o f -> p (o f)")

            def pipeline(eng, step):
                for j in range(4):
                    step([(0, j - d) if j >= d else None for d in range(5)])
                with eng.Fori(1, QP) as i:
                    for u in range(4):
                        step([(i, u - d) for d in range(5)])
                for j in range(4, 8):
                    step([(QP - 1, j - d) if j - d < 4 else None for d in range(5)])

            def product_columns(k):
                return 0 if k == 0 else 96 + 128 * (k - 1)

            def block_of(eng, i, u):
                return bass.ds(eng.value_load(L.blocks[0:1, bass.ds(i * 4 + u, 1)], min_val=0, max_val=NB - 1), 1)

            with nc.Block() as block:
                @block.sync
                def _(sp):
                    start(sp)

                    def records(i, u, first=False):
                        if not first:
                            sp.wait_ge(tp2_ready.h, tp2_ready.free(i, u, 4))
                            sp.sem_inc(sp_tick, 1)
                        load_records(sp, L, i, u, rec_in[u].h)

                    for u in range(4):
                        records(0, u, True)
                    with sp.Fori(1, QP) as i:
                        for u in range(4):
                            records(i, u)

                @block.gpsimd
                def _(po):
                    def gather(i, u):
                        s4 = u % 4
                        po.wait_ge(rec_in[s4].h, rec_in[s4].at(i * 32 + 32))
                        po.sem_inc(pool_tick, 1)
                        po.wait_ge(msg_ready.h, msg_ready.free(i, u, 4))
                        po.sem_inc(pool_tick, 1)
                        for g in range(G):
                            nc.gpsimd.indirect_dma_start(
                                out=gat[:, s4, g, :], out_offset=None, in_=tables[0][:, :],
                                in_offset=IOff(ap=rec[:, s4, g, 1:2].bitcast(i32), axis=0))\
                                .then_inc(gat_in[s4].h, 16)
                        directions(po, L, i, u, y_step, y_ready)

                    def part(i, u, sv, ready, used, slot, pooled):
                        po.wait_ge(ready.h, ready.done(i, u))
                        po.sem_inc(pool_tick, 1)
                        po.wait_ge(used.h, used.free(i, u, 1))
                        po.sem_inc(pool_tick, 1)
                        po.wait_ge(y_ready.h, y_ready.done(i, u))
                        product_pool(L, sv, u % 4, slot).then_inc(pooled.h, 1)

                    def step(at):
                        a, b, c, d, e = at
                        if b:
                            part(*b, msg[:, b[1] % 2], msg_ready, tp1_ready, 0, pooled1)
                        if c:
                            part(*c, vsv[:, c[1] % 2], gated, tp2_ready, 1, pooled2)
                        if a:
                            gather(*a)

                    pipeline(po, step)

                @block.scalar
                def _(ac):
                    def copy_product(i, u, turned_, copied_, read, into):
                        ac.wait_ge(read.h, read.free(i, u, 1))
                        for g in range(G):
                            ac.wait_ge(turned_.h, turned_.done(i, u, g + 1))
                            nc.scalar.activation(into[:, g, :], pT[g][:, :], ACT.Copy).then_inc(copied_.h, 1)

                    def step(at):
                        a, b, c, d, e = at
                        if d:
                            copy_product(*d, t2, t2c, h_ready, mT2)
                            ac.wait_ge(dlt_ready.h, dlt_ready.done(*d))
                            ac.wait_ge(hw_ready.h, hw_ready.free(*d))
                            nc.scalar.activation(pex[:, d[1] % 2], dlt[:, d[1] % 2], ACT.Exp)\
                                .then_inc(pex_ready.h, 1)
                        if a:
                            ac.wait_ge(turned.h, turned.done(*a))
                            nc.scalar.activation(efT[0:32, a[1] % 2, :], pE[0:32, 0:128], ACT.Copy)
                            ac.wait_ge(mg_ready.h, mg_ready.free(*a, 4))
                            nc.scalar.activation(ohT[:, a[1] % 4].rearrange("p g e -> p (g e)"), pE[:, 128:384],
                                                 ACT.Copy).then_inc(copied.h, 1)
                        if b:
                            copy_product(*b, t1, t1c, val_ready, mT1)
                        if c:
                            ac.wait_ge(mnew_ready.h, mnew_ready.done(*c))
                            ac.wait_ge(scaled.h, scaled.free(*c, 4))
                            nc.scalar.activation(msc[:, c[1] % 4], mdiff[:, c[1] % 2], ACT.Exp)\
                                .then_inc(msc_ready.h, 1)
                        if b:
                            ac.wait_ge(val_ready.h, val_ready.done(*b))
                            ac.wait_ge(leak.h, leak.free(*b, 1))
                            nc.scalar.activation(th[:, b[1] % 2], pVv[:, :, 64:160], ACT.Tanh, scale=0.5)
                            nc.scalar.activation(lk[:, :, :], pVv[:, :, 0:64], ACT.Copy, scale=0.2)\
                                .then_inc(squashed.h, 1)

                    pipeline(ac, step)

                @block.tensor
                def _(pe):
                    def product_turned(i, u, slot, ready, turned_, other_copied, other):
                        pe.wait_ge(ready.h, ready.done(i, u))
                        for g in range(G):
                            if other:
                                pe.wait_ge(other_copied.h, other_copied.done(*other, g + 1))
                            for k in range(4):
                                lo = product_columns(k)
                                last = nc.tensor.transpose(pT[g][:, 128 * k:128 * k + 128],
                                                           tp[:, slot, g, lo:lo + 128], ident[:, :])
                            last.then_inc(turned_.h, 1)

                    def logits_turned(i, u, r):
                        if r == 0:
                            pe.wait_ge(xm_ready.h, xm_ready.done(i, u))
                            pe.wait_ge(top.h, top.free(i, u, 1))
                        else:
                            pe.wait_ge(top.h, top.done(i, u, 1))
                        for h in range(2):
                            for g in range(G):
                                c = 256 * h + 128 * g
                                last = nc.tensor.transpose(pX[:, c:c + 128], xm[:, g, 2 * r + h, :], ident[:, :])
                        last.then_inc(xm_t.h, 1)

                    def step(at):
                        a, b, c, d, e = at
                        if e:
                            pe.wait_ge(hw_ready.h, hw_ready.done(*e))
                            pe.wait_ge(kept.h, kept.free(*e, 1))
                            for g in range(G):
                                last = nc.tensor.matmul(pS, oh[:, e[1] % 4, g, :], hw[:, e[1] % 2, g, :],
                                                        start=g == 0, stop=g == G - 1)
                            last.then_inc(summed.h, 1)
                        if d:
                            pe.wait_ge(mnew_ready.h, mnew_ready.done(*d))
                            for g in range(G):
                                last = nc.tensor.matmul(pG[:, 4 * g:4 * g + 4], ohT[:, d[1] % 4, g, :],
                                                        mnew[:, d[1] % 2, :], start=True, stop=True)
                            last.then_inc(mg_ready.h, 1)
                            product_turned(*d, 1, tp2_ready, t2, t1c, c)
                        if d:
                            pe.wait_ge(dlt_ready.h, dlt_ready.done(*d))
                            for g in range(G):
                                pe.wait_ge(t2c.h, t2c.done(*d, g + 1))
                                hd = pHv[:, g, :].rearrange("p (h f) -> p h f", h=4)
                                nc.tensor.matmul(hd[:, :, 0:16], mT2[0:96, g, 0:128], W["svlin0"][:, :],
                                                 start=True, stop=True)
                                for k in range(3):
                                    last = nc.tensor.matmul(hd[:, :, 16 + 8 * k:24 + 8 * k],
                                                            mT2[:, g, 128 * k + 128:128 * k + 256],
                                                            W["vvlin0"][:, :], start=True, stop=True)
                            last.then_inc(h_ready.h, 1)
                        if c:
                            logits_turned(*c, 0)
                        if a:
                            s4 = a[1] % 4
                            pe.wait_ge(rec_in[s4].h, rec_in[s4].at(a[0] * 32 + 32))
                            pe.wait_ge(oh_ready.h, oh_ready.done(*a))
                            pe.wait_ge(copied.h, copied.free(*a, 1))
                            nc.tensor.transpose(pE[0:32, 0:128], efr[:, s4, 0:G * L.efw], ident[:, :])
                            for g in range(G):
                                last = nc.tensor.transpose(pE[:, 128 + 128 * g:256 + 128 * g], oh[:, s4, g, :],
                                                           ident[:, :])
                            last.then_inc(turned.h, 1)
                        if b:
                            product_turned(*b, 0, tp1_ready, t1, t2c, d)
                        if a:
                            row = block_of(pe, *a)
                            pe.wait_ge(copied.h, copied.done(*a))
                            pe.wait_ge(tp1_ready.h, tp1_ready.free(*a, 1))
                            nc.tensor.matmul(pW[:, 0:448], efT[0:32, a[1] % 2, :], W["rbf0"][:, :],
                                             start=True, stop=True).then_inc(w_ready.h, 1)
                            pe.wait_ge(msg_ready.h, msg_ready.free(*a, 1))
                            for g in range(G):
                                last = nc.tensor.matmul(pB[:, F * g:F * g + F], ohT[:, s4, g, :],
                                                        flat(TD[:, row, :]), start=True, stop=True)
                            last.then_inc(dst_ready.h, 1)
                        if c:
                            logits_turned(*c, 1)
                        if b:
                            pe.wait_ge(gated.h, gated.free(*b, 1))
                            pe.wait_ge(leak.h, leak.free(*b, 1))
                            for g in range(G):
                                pe.wait_ge(t1c.h, t1c.done(*b, g + 1))
                                nc.tensor.matmul(pV[:, 256 * g:256 * g + 160], mT1[0:96, g, 0:128],
                                                 W["alpha0"][:, :], start=True, stop=True)
                                for k in range(3):
                                    last = nc.tensor.matmul(pV[:, 256 * g + 160 + 32 * k:256 * g + 192 + 32 * k],
                                                            mT1[:, g, 128 * k + 128:128 * k + 256],
                                                            W["val0"][:, :], start=True, stop=True)
                            last.then_inc(val_ready.h, 1)

                    pipeline(pe, step)

                @block.vector
                def _(ve):
                    nc.vector.memset(ACC[:, 0:8200], 0.0)
                    nc.vector.memset(ACC[:, 8200:8200 + NBX * 4], -NEG).then_inc(zeroed_acc.h, 1)
                    ve.wait_ge(zeroed_acc.h, zeroed_acc.at(1))

                    def message(i, u):
                        ve.wait_ge(dst_ready.h, dst_ready.done(i, u))
                        ve.wait_ge(gat_in[u % 4].h, gat_in[u % 4].at((i + u // 4) * 32 + 32))
                        nc.vector.tensor_tensor(msg[:, u % 2], gat[:, u % 4], pB[:, 0:320].rearrange(
                            "p (g f) -> p g f", g=G), ALU.add).then_inc(msg_ready.h, 1)

                    def distances(i, u):
                        ve.wait_ge(mg_ready.h, mg_ready.done(i, u))
                        nc.vector.tensor_tensor(dlt[:, u % 2], a4[:, u % 2], pG.rearrange("p (g h) -> p g h", g=G),
                                                ALU.subtract).then_inc(dlt_ready.h, 1)

                    def gates(i, u):
                        ve.wait_ge(squashed.h, squashed.done(i, u))
                        nc.vector.tensor_scalar(th2[:, :, :], th[:, u % 2], 0.5, 0.5, ALU.mult, ALU.add)\
                            .then_inc(gate_step.h, 1)
                        nc.vector.tensor_tensor(la[:, :, :], pVv[:, :, 0:64], lk[:, :, :], ALU.max)\
                            .then_inc(leak.h, 1)
                        ve.wait_ge(gate_step.h, gate_step.done(i, u))
                        nc.vector.tensor_copy(vsv[:, u % 2, :, 0:64], th2[:, :, 0:64])
                        for g in range(G):
                            last = nc.vector.tensor_tensor(
                                vsv[:, u % 2, g, 64:160].rearrange("p (i c) -> p i c", i=3),
                                pVv[:, g, 160:256].rearrange("p (i c) -> p i c", i=3),
                                th2[:, g, 64:96].unsqueeze(1).to_broadcast([P, 3, 32]), ALU.mult)
                        last.then_inc(gated.h, 1)
                        ve.wait_ge(leak.h, leak.done(i, u, 1))
                        nc.vector.tensor_tensor(la2[:, :, :], la[:, :, :],
                                                W["ad"][:, :].unsqueeze(1).to_broadcast([P, G, 64]), ALU.mult)\
                            .then_inc(leak.h, 1)

                    def logits(i, u):
                        nc.vector.tensor_scalar(mb[:, :, :], oh[:, u % 4], 1.0, NEG, ALU.subtract, ALU.mult)
                        ve.wait_ge(leak.h, leak.done(i, u, 2))
                        nc.vector.reduce_sum(a4[:, u % 2], la2[:, :, :].rearrange("p g (h d) -> p g h d", h=4), AX.X)\
                            .then_inc(leak.h, 1)
                        ve.wait_ge(leak.h, leak.done(i, u, 3))
                        ve.wait_ge(xm_t.h, xm_t.free(i, u, 1))
                        for g in range(G):
                            last = nc.vector.tensor_tensor(
                                xm[:, g], mb[:, g, :].unsqueeze(1).to_broadcast([P, 4, P]),
                                a4[:, u % 2, g, :].unsqueeze(2).to_broadcast([P, 4, P]), ALU.add)
                        last.then_inc(xm_ready.h, 1)

                    def highest(i, u, r):
                        ve.wait_ge(xm_t.h, xm_t.done(i, u, r + 1))
                        nc.vector.reduce_max(tm[:, 2 * r:2 * r + 2], pX[:, :].rearrange("p (h e) -> p h e", h=2),
                                             AX.X).then_inc(top.h, 1)

                    def maxima(i, u):
                        mrow = flat(M[:, block_of(ve, i, u), :])
                        ve.wait_ge(top.h, top.done(i, u))
                        ve.sem_inc(ve_tick, 1)
                        nc.vector.tensor_tensor(mnew[:, u % 2, :], mrow, tm[:, :], ALU.max).then_inc(m_step.h, 1)
                        ve.wait_ge(m_step.h, m_step.done(i, u))
                        nc.vector.tensor_tensor(mdiff[:, u % 2, :], mrow, mnew[:, u % 2, :], ALU.subtract)\
                            .then_inc(mnew_ready.h, 1)
                        ve.wait_ge(mnew_ready.h, mnew_ready.done(i, u))
                        ve.sem_inc(ve_tick, 1)
                        nc.vector.tensor_copy(mrow, mnew[:, u % 2, :])

                    def one_hot(i, u):
                        s4 = u % 4
                        ve.wait_ge(rec_in[s4].h, rec_in[s4].at(i * 32 + 32))
                        ve.wait_ge(summed.h, summed.free(i, u, 4))
                        for g in range(G):
                            last = nc.vector.tensor_scalar(oh[:, s4, g, :], iota1[:, :], rec[:, s4, g, 0:1], None,
                                                           ALU.is_equal)
                        last.then_inc(oh_ready.h, 1)

                    def keep(i, u, d):
                        row = flat(acc[:, block_of(ve, i, u), :])
                        if d:
                            ve.wait_ge(h_ready.h, h_ready.done(*d))
                            ve.sem_inc(ve_tick, 1)
                        rowh = row.rearrange("p (h f) -> p h f", h=4)
                        ve.wait_ge(msc_ready.h, msc_ready.done(i, u))
                        ve.wait_ge(kept.h, kept.free(i, u, 1))
                        nc.vector.tensor_tensor(rowh, rowh, msc[:, u % 4, :].unsqueeze(2).to_broadcast([P, 4, 41]),
                                                ALU.mult).then_inc(scaled.h, 1)
                        ve.wait_ge(scaled.h, scaled.done(i, u))
                        ve.wait_ge(summed.h, summed.done(i, u))
                        nc.vector.tensor_tensor(row, row, pS, ALU.add).then_inc(kept.h, 1)

                    def weigh(i, u):
                        s2 = u % 2
                        ve.wait_ge(h_ready.h, h_ready.done(i, u))
                        ve.wait_ge(pex_ready.h, pex_ready.done(i, u))
                        ve.wait_ge(summed.h, summed.free(i, u))
                        for g in range(G):
                            hv = hw[:, s2, g, :].rearrange("p (h f) -> p h f", h=4)
                            nc.vector.tensor_tensor(
                                hv[:, :, 0:40], pHv[:, g, :].rearrange("p (h f) -> p h f", h=4),
                                pex[:, s2, g, :].unsqueeze(2).to_broadcast([P, 4, 40]), ALU.mult)
                        last = nc.vector.tensor_copy(
                            hw[:, s2].rearrange("p g (h f) -> p g h f", h=4)[:, :, :, 40], pex[:, s2])
                        last.then_inc(hw_ready.h, 1)

                    def step(at):
                        a, b, c, d, e = at
                        if b:
                            message(*b)
                        if d:
                            distances(*d)
                        if c:
                            gates(*c)
                            logits(*c)
                        if a:
                            one_hot(*a)
                        if b:
                            i, u = b
                            ve.wait_ge(msg_ready.h, msg_ready.done(i, u))
                            ve.wait_ge(w_ready.h, w_ready.done(i, u))
                            ve.wait_ge(y_ready.h, y_ready.done(i, u))
                            ve.wait_ge(t1.h, t1.free(i, u, 1))
                            product_vector(ve, L, i, u, msg[:, u % 2], pW[:, 0:448].rearrange(
                                "p (g f) -> p g f", g=G), rec[:, u % 4, :, 2:3], 0, pooled1, part1a, part2a)\
                                .then_inc(tp1_ready.h, 1)
                        if c:
                            highest(*c, 0)
                        if e:
                            keep(*e, d)
                        if d:
                            weigh(*d)
                        if c:
                            highest(*c, 1)
                            i, u = c
                            ve.wait_ge(t2.h, t2.free(i, u, 1))
                            product_vector(ve, L, i, u, vsv[:, u % 2], None, rec[:, u % 4, :, 2:3], 1, pooled2,
                                           part1b, part2b).then_inc(tp2_ready.h, 1)
                            maxima(*c)

                    pipeline(ve, step)
                    ve.wait_ge(kept.h, kept.done(QP - 1, 3))

        def layer0_update():
            den = sig("den", 2, NBX)
            divided = sig("divided", 1, NBX)
            turned = sig("turned", 1, NBX)
            copied = sig("copied", 1, NBX)
            made = sig("made", 1, NBX)
            updated = sig("updated", 1, NBX)
            seen = sig("seen", 2, NBX)
            acc = ACC[:, 0:NBX * 164].rearrange("p (b f) -> p b f", b=NBX)
            pT, pO = [BK[0], BK[1]], [BK[2], BK[3]]
            with nc.Block() as block:
                @block.sync
                def _(sp):
                    start(sp)

                @block.vector
                def _(ve):
                    def rows(i, u):
                        b = bass.ds(i * 2 + u, 1)
                        a = acc[:, b, :].rearrange("p o (h f) -> p (o h) f", h=4)
                        nc.vector.tensor_scalar_add(nrm[:, u, :], a[:, :, 40], 1e-16).then_inc(den.h, 1)
                        ve.wait_ge(den.h, den.done(i, u, 1))
                        nc.vector.reciprocal(nrm2[:, u, :], nrm[:, u, :]).then_inc(den.h, 1)
                        ve.wait_ge(den.h, den.done(i, u, 2))
                        ve.wait_ge(turned.h, turned.free(i, u))
                        nc.vector.tensor_tensor(xn[:, u, :].rearrange("p (h f) -> p h f", h=4), a[:, :, 0:40],
                                                nrm2[:, u, :].unsqueeze(2).to_broadcast([P, 4, 40]), ALU.mult)\
                            .then_inc(divided.h, 1)

                    def outputs(i, u):
                        b = bass.ds(i * 2 + u, 1)
                        ve.wait_ge(made.h, made.done(i, u))
                        xs = X[:, b, 0:64].rearrange("p o f -> p (o f)")
                        xv = X[:, b, 64:160].rearrange("p o (c i) -> p i (o c)", i=3)
                        nc.vector.scalar_tensor_tensor(xs, xs, 2.0, pO[u][:, 0:64], ALU.mult, ALU.add)
                        nc.vector.scalar_tensor_tensor(xv, xv, 2.0, pO[u][:, 64:160].rearrange(
                            "p (i c) -> p i c", i=3), ALU.mult, ALU.add).then_inc(updated.h, 1)
                        ve.wait_ge(updated.h, updated.done(i, u))
                        ve.sem_inc(ve_tick, 1)
                        statistics(ve, i, u, F, seen)

                    with ve.Fori(0, HNB) as i:
                        rows(i, 0)
                        rows(i, 1)
                        outputs(i, 0)
                        outputs(i, 1)

                @block.tensor
                def _(pe):
                    with pe.Fori(0, HNB) as i:
                        for u in range(2):
                            pe.wait_ge(divided.h, divided.done(i, u))
                            pe.wait_ge(copied.h, copied.free(i, u))
                            for k in range(2):
                                last = nc.tensor.transpose(pT[u][0:80, 128 * k:128 * k + 128],
                                                           xn[:, u, 80 * k:80 * k + 80], ident[:, :])
                            last.then_inc(turned.h, 1)
                        for u in range(2):
                            pe.wait_ge(copied.h, copied.done(i, u))
                            pe.wait_ge(updated.h, updated.free(i, u))
                            for k in range(2):
                                last = nc.tensor.matmul(pO[u][:, 0:160], xT[0:80, u, 128 * k:128 * k + 128],
                                                        W["proj0"][:, 160 * k:160 * k + 160],
                                                        start=k == 0, stop=k == 1)
                            last.then_inc(made.h, 1)

                @block.scalar
                def _(ac):
                    with ac.Fori(0, HNB) as i:
                        for u in range(2):
                            ac.wait_ge(turned.h, turned.done(i, u))
                            ac.wait_ge(made.h, made.free(i, u))
                            nc.scalar.activation(xT[0:80, u, :], pT[u][0:80, 0:256], ACT.Copy).then_inc(copied.h, 1)

        first_statistics()
        node_table(0)
        layer0_edges(layer(0))
        layer0_update()
        for k in range(1, 4):
            node_table(k)
            edge_loop(layer(k))
            node_update(layer(k))
        last_norm()


def lay_out(x, src, dst, edge_attr_16, edge_attr_3, edge_attr_4, edge_attr_64, node_vec1, ch, **weights):
    import numpy as np
    e = src.shape[0]
    _, _, t, _ = sizes(x.shape[0], e, ch)
    nbx = sizes(x.shape[0], e, ch)[1]
    attrs = np.zeros((P * t, 87), np.float32)
    attrs[:e, 0:4] = edge_attr_4
    attrs[:e, 4:20] = edge_attr_16
    attrs[:e, 20:84] = edge_attr_64
    attrs[:e, 84:87] = edge_attr_3
    ids = []
    for a in (src, dst):
        padded = np.zeros((P * t,), np.int32)
        padded[:e] = a
        ids.append(padded)
    rows = []
    for a in (x, node_vec1):
        padded = np.zeros((P * nbx, a.shape[1]), np.float32)
        padded[:a.shape[0]] = a
        rows.append(padded)
    return {"x": rows[0], "attrs": attrs, "src": ids[0], "dst": ids[1], "node_vec1": rows[1],
            **{k: np.asarray(v) for k, v in weights.items()}}


def program(nc, arrays, n, e, ch):
    aps = {name: nc.dram_tensor(f"in_{name}", a.shape, mybir.dt.from_np(a.dtype), kind="ExternalInput").ap()
           for name, a in arrays.items()}
    out = nc.dram_tensor("out", (n, F), mybir.dt.float32, kind="ExternalOutput").ap()
    build(nc, aps, out, n, e, ch)


def kernel(**inputs):
    import numpy as np
    import concourse.bacc as bacc
    from concourse.bass_utils import run_bass_kernel_spmd
    arrays = lay_out(ch=23, **inputs)
    nc = bacc.Bacc("TRN2", target_bir_lowering=False, num_devices=1)
    program(nc, arrays, inputs["x"].shape[0], inputs["src"].shape[0], 23)
    maps = {f"in_{name}": np.ascontiguousarray(a) for name, a in arrays.items()}
    return run_bass_kernel_spmd(nc, [maps], core_ids=[0]).results[0]["out"]
```

```python
import concourse.bass as bass
from concourse import mybir
from contextlib import ExitStack

P = 128
G = 2
F = 160
CS, CV = 64, 32
EA16, EA64, EA3 = 8, 24, 88
RW = EA3 + 7
RD, RS = EA3, RW - EA64
NEG = 1.0e30
EPS = 1e-5
R3, R2 = 3.0 ** 0.5, 2.0 ** 0.5


class Sig:

    def __init__(self, handle, per):
        self.h, self.per, self.base, self.total, self.unroll = handle, per, 0, 0, 2

    def done(self, i, u, m=None):
        return i * (self.unroll * self.per) + (
            self.base + 4 * self.per + u * self.per + (self.per if m is None else m))

    def free(self, i, u, slots=2):
        return i * (self.unroll * self.per) + (
            self.base + 4 * self.per + u * self.per + self.per - slots * self.per)


class Mark:

    def __init__(self, handle):
        self.h, self.base, self.total = handle, 0, 0

    def at(self, k):
        return k + self.base


def sizes(n, e, ch):
    nb = -(-n // P)
    t = -(-e // (P * 2 * ch)) * 2 * ch
    pairs = (e + nb * (G * P - 1)) // (G * P)
    pairs += -pairs % 4
    return nb, nb + nb % 2, t, pairs


def build(nc, ins, out, N, E, CH):
    fp32, i32 = mybir.dt.float32, mybir.dt.int32
    ALU, ACT, AX = mybir.AluOpType, mybir.ActivationFunctionType, mybir.AxisListType
    IOff = bass.IndirectOffsetOnAxis
    NB, NBX, T, NP = sizes(N, E, CH)
    LAST = N - (NB - 1) * P
    NCH = T // CH
    ACCW = max(NBX * 480, 16000)
    ctx = ExitStack()
    with ctx:
        def sb(name, shape, dt=fp32):
            return ctx.enter_context(nc.sbuf_tensor(name, shape, dt))

        def ps(name):
            return ctx.enter_context(nc.psum_tensor(name, [P, 512], fp32))

        def sem(name):
            return ctx.enter_context(nc.semaphore(name))

        fresh, known = [], {}

        def sig(name, per=1, steps=0, unroll=2):
            if name not in known:
                known[name] = Sig(sem(name), per)
                fresh.append(known[name])
            s = known[name]
            assert s.per == per
            s.base += s.total
            s.total = per * steps
            s.unroll = unroll
            return s

        def sig4(name, per=1, steps=0):
            return sig(name, per, steps, 4)

        def mark(name, total):
            if name not in known:
                known[name] = Mark(sem(name))
            known[name].base += known[name].total
            known[name].total = total
            return known[name]

        def start(eng):
            while fresh:
                s = fresh.pop()
                eng.sem_inc(s.h, 4 * s.per)

        QP = NP // 4
        rec_dst = nc.dram_tensor("rec_dst", (NP * G * P, RD), fp32).ap()
        rec_src = nc.dram_tensor("rec_src", (NP * G * P, RS), fp32).ap()
        tables = [nc.dram_tensor(f"table{n}", (NBX * P, F), fp32).ap() for n in range(4)]
        rec_dst_v = rec_dst.rearrange("(i u p g) r -> i u p g r", u=4, g=G, p=P)
        rec_src_v = rec_src.rearrange("(i u p g) r -> i u p g r", u=4, g=G, p=P)
        tables_v = [t.rearrange("(i u p) f -> i u p f", u=2, p=P) for t in tables]

        X = sb("X", [P, NBX, F])
        ACC = sb("ACC", [P, ACCW])
        node_a = sb("node_a", [P, NBX])
        a_rows = sb("a_rows", [NBX, P])
        ident = sb("ident", [P, P])
        iota1 = sb("iota1", [P, P])
        ones = sb("ones", [P, P])
        tril = sb("tril", [P, P])
        pair_block = [sb(f"pair_block{s}", [1, NP], i32) for s in range(2)]
        bn6 = sb("bn6", [P, 2, 6])
        mean_var = sb("mean_var", [P, 2, 2])
        stat = sb("stat", [P, NBX, 2])
        rstd = sb("rstd", [P, NBX])
        vsq = sb("vsq", [P, NBX])
        rstd_v = sb("rstd_v", [P, NBX])

        w_specs = {
            "rbf0": (32, 448), "alpha0": (96, 160), "val0": (P, 32), "svlin0": (96, 64), "vvlin0": (P, 32),
            "proj0": (80, 320), "ts0": (64, 128), "tv0": (96, 192), "gam_s": (64, 1), "bet_s": (64, 1),
            "gam_v": (96, 1), "sc_s": (96, 1), "sc_v": (P, 1), "adr": (1, 64), "wg": (64, 32),
            "svT": (64, 96), "ad": (P, 64),
            "fc1_1": (P, P), "fc2_1": (P, 448), "ts1": (64, 64), "tv1": (96, 96),
            "xs1": (64, 96), "xv1": (96, 96), "os1": (96, 96), "ov1": (P, 32),
            "fc1_2": (32, P), "fc2_2": (P, 448), "ts2": (64, 64), "tv2": (96, 96),
            "xs2": (64, 64), "xv2": (96, 96), "os2": (96, 65), "ov2": (96, 32),
            "fc1_3": (P, P), "fc2_3": (P, 448), "ts3": (64, 64), "tv3": (96, 96),
            "xs3": (64, 96), "xv3": (96, 96), "os3": (96, 96), "ov3": (P, 32),
        }
        W = {k: sb("w_" + k, list(s)) for k, s in w_specs.items()}

        rec = sb("rec", [P, 4, G, 8])
        efr = sb("efr", [P, 4, G * 64])
        gat = sb("gat", [P, 4, G, F])
        oh = sb("oh", [P, 4, G, P])
        efT = sb("efT", [P, 2, P])
        hT = sb("hT", [P, 2, P])
        tp = sb("tp", [P, 2, G, 480])
        t_sv = sb("t_sv", [P, G, 64])
        t_dot = sb("t_dot", [P, 2, G, 3, 32])
        t_cr = sb("t_cr", [P, 2, G, 3, 32])
        t_cr2 = sb("t_cr2", [P, G, 3, 32])
        t_cr3 = sb("t_cr3", [P, G, 3, 32])
        t_sum = sb("t_sum", [P, G, 32])
        t_sum2 = sb("t_sum2", [P, G, 32])
        msg = sb("msg", [P, 2, G, F])
        ohT = sb("ohT", [P, 4, G, P])
        mT = sb("mT", [P, G, 512])
        mTb = sb("mTb", [P, G, 512])
        th = sb("th", [P, 2, G, 96])
        th2 = sb("th2", [P, G, 96])
        la2 = sb("la2", [P, G, 64])
        lk = sb("lk", [P, G, 64])
        la = sb("la", [P, G, 64])
        a4 = sb("a4", [P, 2, G, 4])
        mb = sb("mb", [P, 2, G, P])
        xm = sb("xm", [P, G, 4, P])
        tm = sb("tm", [P, 4])
        mnew = sb("mnew", [P, 2, 4])
        mdiff = sb("mdiff", [P, 2, 4])
        msc = sb("msc", [P, 4, 4])
        dlt = sb("dlt", [P, 2, G, 4])
        pex = sb("pex", [P, 2, G, 4])
        vsv = sb("vsv", [P, 2, G, F])
        hw = sb("hw", [P, 2, G, 164])
        xn = msg[:, :, 0, :]
        xT = mTb[:, :, 0:256]
        aT = mT
        accrow = tp[:, :, 0, :]
        tb = vsv[:, :, 0, :]
        nrm = sb("nrm", [P, 2, 4])
        nrm2 = sb("nrm2", [P, 2, 4])
        y_s = hw[:, :, 0, 0:160]
        sgm = th[:, :, 0, :]

        BK = [ps(f"bank{k}") for k in range(8)]

        setup_zero = sem("setup_zero")
        weights_in = sem("weights_in")
        x_in = sem("x_in")
        const_ready = sem("const_ready")
        ramp_done = sem("ramp_done")
        fill_done = [sem("fill_dst_done"), sem("fill_src_done")]
        keys_in = sem("keys_in")
        wprep = sem("wprep")
        wpe = sem("wpe")

        ZP = max(d for d in range(1, 12) if NP % d == 0)
        ZCOL = ZP * G * RD
        zeros_t = ACC[:, ACCW - ZCOL:ACCW]
        o = [0]

        def scratch(cols):
            o[0] += cols
            return ACC[:, o[0] - cols:o[0]]

        raw = [scratch(T).bitcast(i32) for _ in range(2)]
        blki = scratch(T).bitcast(i32)
        loci = scratch(T).bitcast(i32)
        keyf = [scratch(T) for _ in range(2)]
        blkf = [scratch(T) for _ in range(2)]
        posi = [scratch(T).bitcast(i32) for _ in range(2)]
        posf = scratch(T)
        zrow = scratch(T)
        eqb = scratch(2 * T).rearrange("p (u t) -> p u t", u=2)
        scb = scratch(2 * T).rearrange("p (u t) -> p u t", u=2)
        tmb = scratch(2 * T).rearrange("p (u t) -> p u t", u=2)
        bidx = scratch(NBX)
        cnt = scratch(NBX)
        tot = scratch(NBX)
        toti = scratch(NBX).bitcast(i32)
        toti2 = scratch(NBX).bitcast(i32)
        prs = scratch(NBX)
        endp = scratch(NBX)
        offp = scratch(NBX)
        jrow = scratch(NP)
        blkacc = scratch(2 * NP).rearrange("p (u t) -> p u t", u=2)
        stage = scratch(2 * CH * RW).rearrange("p (u c r) -> p u c r", u=2, r=RW)
        squares = scratch(2 * CH * 3).rearrange("p (u c r) -> p u c r", u=2, r=3)
        norms = scratch(6 * CH).rearrange("p (k u c) -> p k u c", k=3, u=2)
        sidx = scratch(4 * CH).bitcast(i32).rearrange("p (u s c) -> p u s c", u=2, s=2)
        assert o[0] <= ACCW - ZCOL

        attrs_v = ins["attrs"].rearrange("(p i u c) r -> p i u c r", p=P, u=2, c=CH)
        loads = []

        def load(dst, src):
            loads.append((dst, src))

        A = ins
        for g in range(G):
            load(W["rbf0"][16 * g:16 * g + 16, 224 * g:224 * g + 224], A["L0_gnn_W_rbf"])
            load(W["fc1_1"][64 * g:64 * g + 64, 64 * g:64 * g + 64], A["L1_gnn_W_fc1"])
            load(W["fc2_1"][64 * g:64 * g + 64, 224 * g:224 * g + 224], A["L1_gnn_W_fc2"])
            load(W["fc1_2"][16 * g:16 * g + 16, 64 * g:64 * g + 64], A["L2_gnn_Wfc1"])
            load(W["fc2_2"][64 * g:64 * g + 64, 224 * g:224 * g + 192], A["L2_gnn_Wfc2"])
            load(W["fc1_3"][64 * g:64 * g + 64, 64 * g:64 * g + 64], A["L3_gnn_fc_w1"])
            load(W["fc2_3"][64 * g:64 * g + 64, 224 * g:224 * g + 224], A["L3_gnn_fc_w2"])
        load(W["alpha0"][:, 0:64], A["L0_gnn_W_alpha"])
        load(W["alpha0"][:, 64:128], A["L0_gnn_Ws_val"])
        load(W["val0"][:, :], A["L0_gnn_Wv_val"])
        load(W["svlin0"][:, :], A["L0_gnn_Ws_vlin"])
        load(W["vvlin0"][:, :], A["L0_gnn_Wv_vlin"])
        for h in range(4):
            k, r = h // 2, 40 * (h % 2)
            load(W["proj0"][r:r + 16, 160 * k:160 * k + 64], A["L0_gnn_Wps"][16 * h:16 * h + 16, :])
            for i in range(3):
                load(W["proj0"][r + 16 + 8 * i:r + 24 + 8 * i, 160 * k + 64 + 32 * i:160 * k + 96 + 32 * i],
                     A["L0_gnn_Wpv"][8 * h:8 * h + 8, :])
        load(W["ts0"][:, 0:64], A["L0_gnn_Ws_src"])
        load(W["ts0"][:, 64:128], A["L0_gnn_Ws_dst"])
        for i in range(3):
            r = slice(32 * i, 32 * i + 32)
            load(W["tv0"][r, 32 * i:32 * i + 32], A["L0_gnn_Wv_src"])
            load(W["tv0"][r, 96 + 32 * i:128 + 32 * i], A["L0_gnn_Wv_dst"])
            load(W["gam_v"][r, :], A["L0_gnn_gamma_v"].rearrange("(c o) -> c o", o=1))
            load(W["tv1"][r, r], A["L1_gnn_W_nl1"])
            load(W["xv1"][r, r], A["L1_gnn_W_skip1"])
            load(W["tv2"][r, r], A["L2_gnn_Wl1_1"])
            load(W["xv2"][r, r], A["L2_gnn_Wsc1"])
            load(W["tv3"][r, r], A["L3_gnn_lin1_wv"])
            load(W["xv3"][r, r], A["L3_gnn_sc_wv"])
        load(W["gam_s"][:, :], A["L0_gnn_gamma_s"].rearrange("(c o) -> c o", o=1))
        load(W["bet_s"][:, :], A["L0_gnn_beta_s"].rearrange("(c o) -> c o", o=1))
        load(W["sc_s"][0:64, :], A["L0_gnn_w2_ss"].rearrange("(c o) -> c o", o=1))
        load(W["sc_s"][64:96, :], A["L0_gnn_w2_vv0"].rearrange("(c o) -> c o", o=1))
        load(W["sc_v"][0:64, :], A["L0_gnn_w2_sv"].rearrange("(c o) -> c o", o=1))
        load(W["sc_v"][64:96, :], A["L0_gnn_w2_vs"].rearrange("(c o) -> c o", o=1))
        load(W["sc_v"][96:128, :], A["L0_gnn_w2_vv1"].rearrange("(c o) -> c o", o=1))
        load(W["adr"][:, :], A["L0_gnn_alpha_dot"].rearrange("o h d -> o (h d)"))
        load(W["wg"][:, :], A["L0_gnn_Wg"])
        load(W["ts1"][:, :], A["L1_gnn_W_nl0"])
        load(W["xs1"][:, :], A["L1_gnn_W_skip0"])
        load(W["os1"][:, :], A["L1_gnn_W_out_s"])
        load(W["ov1"][:, :], A["L1_gnn_W_out_v"])
        load(W["ts2"][:, :], A["L2_gnn_Wl1_0"])
        load(W["xs2"][:, :], A["L2_gnn_Wsc0"])
        load(W["os2"][:, 0:64], A["L2_gnn_Wl2_s"])
        load(W["os2"][:, 64:65], A["L2_gnn_Wa"])
        load(W["ov2"][:, :], A["L2_gnn_Wl2_v"])
        load(W["ts3"][:, :], A["L3_gnn_lin1_ws"])
        load(W["xs3"][:, :], A["L3_gnn_sc_ws"])
        load(W["os3"][:, :], A["L3_gnn_lin2_ws"])
        load(W["ov3"][:, :], A["L3_gnn_lin2_wv"])
        zeroed = ["rbf0", "fc1_1", "fc2_1", "fc1_2", "fc2_2", "fc1_3", "fc2_3", "proj0", "tv0", "tv1", "xv1",
                  "tv2", "xv2", "tv3", "xv3"]
        NFILL = NP // ZP

        with nc.Block() as block:
            @block.sync
            def _(sp):
                sp.wait_ge(setup_zero, 1)
                sp.dma_start(X[:, :, :], A["x"].rearrange("(b p) f -> p b f", p=P)).then_inc(x_in, 16)
                sp.dma_start(a_rows[:, :], A["node_vec1"].rearrange("(b p) o -> b (p o)", p=P)).then_inc(x_in, 16)
                sp.dma_start(raw[0], A["dst"].rearrange("(p t) -> p t", p=P)).then_inc(keys_in, 16)
                sp.dma_start(raw[1], A["src"].rearrange("(p t) -> p t", p=P)).then_inc(keys_in, 16)
                for dst, src in loads:
                    sp.dma_start(dst, src, allow_slow_non_contiguous=dst.shape[-1] == 1).then_inc(weights_in, 16)
                sp.wait_ge(x_in, 32)
                sp.wait_ge(keys_in, 32)
                sp.wait_ge(weights_in, 16 * len(loads))

            @block.vector
            def _(ve):
                for k in zeroed:
                    nc.vector.memset(W[k][:, :], 0.0)
                nc.vector.memset(zrow, 0.0).then_inc(setup_zero, 1)
                nc.vector.memset(ones[:, :], 1.0).then_inc(const_ready, 1)

                def scale(name, r0, r1, by):
                    nc.vector.tensor_scalar_mul(W[name][r0:r1, :], W[name][r0:r1, :], by).then_inc(wprep, 1)

                ve.wait_ge(weights_in, 16 * len(loads))
                scale("os1", 0, 96, 1 / 32)
                scale("ov1", 0, 64, R3 / 32)
                scale("ov1", 64, 96, 1 / 32)
                scale("ov1", 96, 128, R3 / R2 / 32)
                scale("ts2", 0, 64, 1 / 8)
                scale("tv2", 0, 96, 32 ** -0.5)
                scale("xs2", 0, 64, 1 / 8)
                scale("xv2", 0, 96, 32 ** -0.5)
                scale("os2", 0, 64, 96 ** -0.5 / 8)
                scale("os2", 64, 96, 96 ** -0.5 / 8 / R3)
                scale("ov2", 0, 96, 96 ** -0.5 / 8)
                scale("ts3", 0, 64, 1 / 8)
                scale("tv3", 0, 96, 32 ** -0.5)
                scale("xs3", 0, 64, 1 / 8)
                scale("xv3", 0, 96, 32 ** -0.5)
                scale("os3", 0, 64, 96 ** -0.5 / 32)
                scale("os3", 64, 96, 96 ** -0.5 / 32 / R3)
                scale("ov3", 0, 96, 128 ** -0.5 / 32)
                scale("ov3", 96, 128, 128 ** -0.5 / 32 / R2)
                scale("sc_s", 64, 96, 1 / R3)
                scale("sc_v", 96, 128, 1 / R2)
                scale("val0", 96, 128, 1 / R2)
                n = 22
                ve.wait_ge(wprep, n)
                nc.vector.tensor_scalar_mul(W["svlin0"][:, :], W["svlin0"][:, :], W["sc_s"][:, :]).then_inc(wprep, 1)
                nc.vector.tensor_scalar_mul(W["vvlin0"][:, :], W["vvlin0"][:, :], W["sc_v"][:, :]).then_inc(wprep, 1)
                ve.wait_ge(wpe, 1)
                nc.vector.tensor_copy(W["svT"][:, :], BK[0][0:64, 0:96]).then_inc(wprep, 1)
                nc.vector.tensor_copy(W["ad"][:, :], BK[1][:, 0:64]).then_inc(wprep, 1)
                nc.vector.tensor_copy(node_a[:, :], BK[3][:, 0:NBX]).then_inc(wprep, 1)
                ve.wait_ge(wpe, 2)
                nc.vector.tensor_copy(W["alpha0"][:, 128:160], BK[2][0:96, 0:32]).then_inc(wprep, 1)
                ve.wait_ge(wprep, n + 6)
                scale("alpha0", 64, 96, 1 / R3)

            @block.gpsimd
            def _(po):
                nc.gpsimd.memset(ident[:, :], 0.0).then_inc(ramp_done, 1)
                nc.gpsimd.memset(tril[:, :], 1.0).then_inc(ramp_done, 1)
                po.wait_ge(ramp_done, 2)
                nc.gpsimd.affine_select(out=ident[:, :], in_=ident[:, :], compare_op=ALU.not_equal, fill=1.0,
                                        base=0, pattern=[[-1, P]], channel_multiplier=1).then_inc(ramp_done, 1)
                nc.gpsimd.affine_select(out=tril[:, :], in_=tril[:, :], compare_op=ALU.is_gt, fill=0.0,
                                        base=0, pattern=[[1, P]], channel_multiplier=-1).then_inc(ramp_done, 1)
                nc.gpsimd.iota(iota1[:, :], pattern=[[1, P]], base=1, channel_multiplier=0,
                               allow_small_or_imprecise_dtypes=True).then_inc(ramp_done, 1)
                nc.gpsimd.iota(bidx, pattern=[[1, NBX]], base=0, channel_multiplier=0,
                               allow_small_or_imprecise_dtypes=True).then_inc(ramp_done, 1)
                nc.gpsimd.iota(jrow, pattern=[[1, NP]], base=0, channel_multiplier=0,
                               allow_small_or_imprecise_dtypes=True).then_inc(ramp_done, 1)

            @block.tensor
            def _(pe):
                pe.wait_ge(ramp_done, 7)
                pe.wait_ge(const_ready, 1)
                pe.wait_ge(weights_in, 16 * len(loads))
                pe.wait_ge(x_in, 32)
                nc.tensor.transpose(BK[3][:, 0:NBX], a_rows[:, :], ident[0:NBX, 0:NBX])
                nc.tensor.transpose(BK[0][0:64, 0:96], W["alpha0"][:, 64:128], ident[0:96, 0:96])
                nc.tensor.matmul(BK[1][:, 0:64], ones[0:1, :], W["adr"][:, :], start=True, stop=True).then_inc(wpe, 1)
                pe.wait_ge(wprep, 26)
                nc.tensor.matmul(BK[2][0:96, 0:32], W["svT"][:, :], W["wg"][:, :], start=True, stop=True)\
                    .then_inc(wpe, 1)

        keys_split = sem("keys_split")
        pads_marked = sem("pads_marked")
        zero_tile = sem("zero_tile")
        hot = [sig(f"bucket_hot{s}") for s in range(2)]
        ranked = [sig(f"bucket_ranked{s}") for s in range(2)]
        picked = [sig(f"bucket_picked{s}") for s in range(2)]
        added = [sig(f"bucket_added{s}") for s in range(2)]
        shifted = [sig(f"bucket_shifted{s}") for s in range(2)]
        added2 = [sig(f"bucket_shift_added{s}") for s in range(2)]
        counted = sem("counted")
        off_step = sem("off_step")
        pos_done = sem("pos_done")
        pos_ready = sem("pos_ready")
        tbl_step = sem("tbl_step")
        pool_tick = sem("pool_tick")
        sp_tick = sem("sp_tick")
        ve_tick = sem("ve_tick")
        TH = [(0, min(512, T))] + ([(512, T)] if T > 512 else [])
        PADPOS = float(1 << 24)
        HB = NBX // 2
        with nc.Block() as block:
            @block.sync
            def _(sp):
                start(sp)
                sp.wait_ge(zero_tile, 1)
                for s, (r, w) in enumerate(((rec_dst, RD), (rec_src, RS))):
                    v = r.rearrange("(k p g) r -> k p (g r)", p=P, g=ZP * G)
                    for k in range(NFILL):
                        sp.dma_start(v[k], zeros_t[:, 0:ZP * G * w]).then_inc(fill_done[s], 16)
                for s in range(2):
                    sp.wait_ge(fill_done[s], 16 * NFILL)

            @block.vector
            def _(ve):
                nc.vector.memset(zeros_t, 0.0).then_inc(zero_tile, 1)
                for s in range(2):
                    if s:
                        ve.wait_ge(keys_split, 4)
                    nc.vector.tensor_scalar(blki, raw[s], 7, None, ALU.logical_shift_right).then_inc(keys_split, 1)
                    nc.vector.tensor_scalar(loci, raw[s], 127, None, ALU.bitwise_and).then_inc(keys_split, 1)
                    ve.wait_ge(keys_split, 4 * s + 2)
                    nc.vector.tensor_copy(blkf[s], blki).then_inc(keys_split, 1)
                    nc.vector.tensor_scalar_add(keyf[s], loci, 1.0).then_inc(keys_split, 1)

                for s in range(2):
                    ve.wait_ge(pads_marked, s + 1)
                    with ve.Fori(0, HB) as i:
                        for u in range(2):
                            b = bass.ds(i * 2 + u, 1)
                            ve.wait_ge(picked[s].h, picked[s].free(i, u))
                            nc.vector.tensor_scalar(eqb[:, u, :], blkf[s], bidx[:, b], None, ALU.is_equal)\
                                .then_inc(hot[s].h, 1)
                            ve.wait_ge(hot[s].h, hot[s].done(i, u))
                            nc.vector.tensor_tensor_scan(scb[:, u, :], eqb[:, u, :], zrow, 0.0, ALU.add, ALU.add)\
                                .then_inc(ranked[s].h, 1)
                            ve.wait_ge(ranked[s].h, ranked[s].done(i, u))
                            nc.vector.tensor_copy(cnt[:, b], scb[:, u, T - 1:T]).then_inc(counted, 1)
                    c = 9 * s
                    ve.wait_ge(off_step, c + 1)
                    nc.vector.tensor_copy(tot, BK[7][:, 0:NBX]).then_inc(off_step, 1)
                    ve.wait_ge(off_step, c + 2)
                    nc.vector.tensor_scalar_add(toti, tot, float(G * P - 1)).then_inc(off_step, 1)
                    ve.wait_ge(off_step, c + 3)
                    nc.vector.tensor_scalar(toti2, toti, 8, None, ALU.logical_shift_right).then_inc(off_step, 1)
                    ve.wait_ge(off_step, c + 4)
                    nc.vector.tensor_copy(prs, toti2).then_inc(off_step, 1)
                    ve.wait_ge(off_step, c + 5)
                    nc.vector.tensor_tensor_scan(endp, prs, zrow[:, 0:NBX], 0.0, ALU.add, ALU.add)\
                        .then_inc(off_step, 1)
                    ve.wait_ge(off_step, c + 6)
                    nc.vector.tensor_tensor(offp, endp, prs, ALU.subtract).then_inc(off_step, 1)
                    ve.wait_ge(off_step, c + 7)
                    nc.vector.tensor_scalar(offp, offp, float(G * P), -1.0, ALU.mult, ALU.add).then_inc(off_step, 1)
                    ve.wait_ge(off_step, c + 8)
                    nc.vector.tensor_tensor(offp, offp, BK[7][:, 64:64 + NBX], ALU.add).then_inc(off_step, 1)
                    ve.wait_ge(off_step, c + 9)
                    ve.wait_ge(picked[s].h, picked[s].done(HB - 1, 1))
                    with ve.Fori(0, HB) as i:
                        for u in range(2):
                            b = bass.ds(i * 2 + u, 1)
                            ve.wait_ge(added2[s].h, added2[s].free(i, u))
                            nc.vector.tensor_scalar(eqb[:, u, :], blkf[s], bidx[:, b], offp[:, b],
                                                    ALU.is_equal, ALU.mult).then_inc(shifted[s].h, 1)
                    ve.wait_ge(added2[s].h, added2[s].done(HB - 1, 1) + 1)
                    if s:
                        ve.wait_ge(pos_ready, 1)
                    for lo, hi in TH:
                        nc.vector.tensor_copy(posf[:, lo:hi], BK[2 * s + (lo > 0)][:, 0:hi - lo]).then_inc(pos_done, 1)
                    nc.vector.memset(blkacc[:, 0, :], 0.0).then_inc(tbl_step, 1)
                    for b in range(NB):
                        ve.wait_ge(tbl_step, s * (NB + 2) + b + 1)
                        nc.vector.scalar_tensor_tensor(blkacc[:, (b + 1) % 2, :], jrow, endp[:, b:b + 1],
                                                       blkacc[:, b % 2, :], ALU.is_ge, ALU.add).then_inc(tbl_step, 1)
                    ve.wait_ge(tbl_step, s * (NB + 2) + NB + 1)
                    nc.vector.tensor_scalar_min(pair_block[s][:, :], blkacc[0:1, NB % 2, :], float(NB - 1))\
                        .then_inc(tbl_step, 1)
                    ve.wait_ge(pads_marked, 3 + s)
                    nc.vector.tensor_copy(posi[s], posf).then_inc(pos_ready, 1)
                    ve.wait_ge(tbl_step, (s + 1) * (NB + 2))

            @block.gpsimd
            def _(po):
                for s in range(2):
                    po.wait_ge(keys_split, 4 * s + 4)
                    nc.gpsimd.affine_select(out=blkf[s], in_=blkf[s], compare_op=ALU.is_ge, fill=float(NBX),
                                            base=E - 1, pattern=[[-1, T]], channel_multiplier=-T)\
                        .then_inc(pads_marked, 1)
                for s in range(2):
                    with po.Fori(0, HB) as i:
                        for u in range(2):
                            po.wait_ge(ranked[s].h, ranked[s].done(i, u))
                            po.sem_inc(pool_tick, 1)
                            po.wait_ge(added[s].h, added[s].free(i, u))
                            nc.gpsimd.tensor_tensor(tmb[:, u, :], eqb[:, u, :], scb[:, u, :], ALU.mult)\
                                .then_inc(picked[s].h, 1)
                    po.wait_ge(pos_done, len(TH) * (s + 1))
                    nc.gpsimd.affine_select(out=posf, in_=posf, compare_op=ALU.is_ge, fill=PADPOS,
                                            base=E - 1, pattern=[[-1, T]], channel_multiplier=-T)\
                        .then_inc(pads_marked, 1)

            @block.tensor
            def _(pe):
                for s in range(2):
                    def add(rows, **kw):
                        for n, (lo, hi) in enumerate(TH):
                            last = nc.tensor.matmul(BK[2 * s + n][:, 0:hi - lo], ident[:, :], rows[:, lo:hi], **kw)
                        return last

                    add(zrow, start=True, stop=False)
                    with pe.Fori(0, HB) as i:
                        for u in range(2):
                            pe.wait_ge(picked[s].h, picked[s].done(i, u))
                            add(tmb[:, u, :], start=False, stop=False).then_inc(added[s].h, 1)
                    pe.wait_ge(counted, NBX * (s + 1))
                    nc.tensor.matmul(BK[7][:, 0:NBX], ones[:, :], cnt, start=True, stop=True)
                    nc.tensor.matmul(BK[7][:, 64:64 + NBX], tril[:, :], cnt, start=True, stop=True)\
                        .then_inc(off_step, 1)
                    with pe.Fori(0, HB) as i:
                        for u in range(2):
                            pe.wait_ge(shifted[s].h, shifted[s].done(i, u))
                            add(eqb[:, u, :], start=False, stop=False).then_inc(added2[s].h, 1)
                    add(zrow, start=False, stop=True).then_inc(added2[s].h, 1)

        attr_in = [sem(f"attr_in{u}") for u in range(2)]
        placed = [sem(f"placed{u}") for u in range(2)]
        staged = sig("staged")
        unit = sig("unit", 5)
        rooted_e = sig("rooted_e")
        stage_i = stage.bitcast(i32)
        with nc.Block() as block:
            @block.sync
            def _(sp):
                start(sp)

                def attr(i, u, first):
                    if not first:
                        sp.wait_ge(placed[u], i * (32 * CH))
                        sp.sem_inc(sp_tick, 1)
                    sp.dma_start(stage[:, u, :, 2:EA3 + 3], attrs_v[:, i, u, :, :]).then_inc(attr_in[u], 16)

                for u in range(2):
                    attr(0, u, True)
                with sp.Fori(1, NCH // 2) as i:
                    for u in range(2):
                        attr(i, u, False)

            @block.vector
            def _(ve):
                def fields(i, u, first):
                    if not first:
                        ve.wait_ge(placed[u], i * (32 * CH))
                    c = bass.ds(i * (2 * CH) + u * CH, CH)
                    nc.vector.tensor_copy(stage[:, u, :, 0], keyf[0][:, c])
                    nc.vector.tensor_copy(stage_i[:, u, :, 1], raw[1][:, c])
                    nc.vector.tensor_copy(stage_i[:, u, :, EA3 + 5], raw[0][:, c])
                    nc.vector.tensor_copy(stage[:, u, :, EA3 + 6], keyf[1][:, c])
                    nc.vector.tensor_copy(sidx[:, u, 0, :], posi[0][:, c])
                    nc.vector.tensor_copy(sidx[:, u, 1, :], posi[1][:, c]).then_inc(staged.h, 1)
                    r = stage[:, u, :, EA3:EA3 + 3]
                    ve.wait_ge(attr_in[u], i * 16 + 16)
                    ve.sem_inc(ve_tick, 1)
                    nc.vector.tensor_tensor(squares[:, u], r, r, ALU.mult).then_inc(unit.h, 1)
                    ve.wait_ge(unit.h, unit.done(i, u, 1))
                    nc.vector.reduce_sum(norms[:, 0, u], squares[:, u], AX.X).then_inc(unit.h, 1)
                    ve.wait_ge(unit.h, unit.done(i, u, 2))
                    ve.wait_ge(rooted_e.h, rooted_e.done(i, u))
                    nc.vector.reciprocal(norms[:, 2, u], norms[:, 1, u]).then_inc(unit.h, 1)
                    ve.wait_ge(unit.h, unit.done(i, u, 3))
                    nc.vector.tensor_tensor(r, r, norms[:, 2, u].unsqueeze(2).to_broadcast([P, CH, 3]), ALU.mult)\
                        .then_inc(unit.h, 1)
                    ve.wait_ge(unit.h, unit.done(i, u, 4))
                    nc.vector.tensor_copy(stage[:, u, :, EA3 + 3:EA3 + 5], stage[:, u, :, EA3:EA3 + 2])\
                        .then_inc(unit.h, 1)

                for u in range(2):
                    fields(0, u, True)
                with ve.Fori(1, NCH // 2) as i:
                    for u in range(2):
                        fields(i, u, False)

            @block.scalar
            def _(ac):
                with ac.Fori(0, NCH // 2) as i:
                    for u in range(2):
                        ac.wait_ge(unit.h, unit.done(i, u, 2))
                        nc.scalar.activation(norms[:, 1, u], norms[:, 0, u], ACT.Sqrt).then_inc(rooted_e.h, 1)

            @block.gpsimd
            def _(po):
                with po.Fori(0, NCH // 2) as i:
                    for u in range(2):
                        po.wait_ge(attr_in[u], i * 16 + 16)
                        po.sem_inc(pool_tick, 1)
                        po.wait_ge(staged.h, staged.done(i, u))
                        po.sem_inc(pool_tick, 1)
                        po.wait_ge(unit.h, unit.done(i, u))
                        po.sem_inc(pool_tick, 1)
                        for c in range(CH):
                            for s, table, lo, w in ((0, rec_dst, 0, RD), (1, rec_src, EA64, RS)):
                                nc.gpsimd.indirect_dma_start(
                                    out=table[:, :], out_offset=IOff(ap=sidx[:, u, s, c:c + 1], axis=0),
                                    in_=stage[:, u, c, lo:lo + w], in_offset=None,
                                    bounds_check=NP * G * P - 1, oob_is_err=False).then_inc(placed[u], 16)
                for u in range(2):
                    po.wait_ge(placed[u], (NCH // 2) * 32 * CH)



        def product_pool(L, sv, u, slot):
            v = sv[:, :, 64:160].rearrange("p g (i c) -> p g i c", i=3)

            def bc(lo, hi):
                return rec[:, u, :, L.y + lo:L.y + hi].unsqueeze(3).to_broadcast([P, G, hi - lo, 32])
            if L.cross:
                for g in range(G):
                    nc.gpsimd.tensor_tensor(t_cr[:, slot, g, 0:2, :], v[:, g, 1:3, :], bc(2, 4)[:, g], ALU.mult)
                nc.gpsimd.tensor_tensor(t_cr[:, slot, :, 2, :], v[:, :, 0, :], bc(4, 5)[:, :, 0], ALU.mult)
            for g in range(G):
                last = nc.gpsimd.tensor_tensor(t_dot[:, slot, g], v[:, g], bc(0, 3)[:, g], ALU.mult)
            return last

        def product_scalar(i, u, s, slot, L):
            t = tp[:, slot]
            for g in range(G):
                for k in range(3):
                    lo = 96 + L.vs * k
                    last = nc.scalar.activation(t[:, g, lo:lo + 64], s[:, g, :], ACT.Copy,
                                                scale=rec[:, u % 4, g, L.y + k:L.y + k + 1])
            return last

        def product_vector(ve, L, i, u, sv, w, y0, slot, pooled, part1, part2, sv_ready, axes_done):
            s, v = sv[:, :, 0:64], sv[:, :, 64:160].rearrange("p g (i c) -> p g i c", i=3)
            t = tp[:, slot]
            tv = t[:, :, 96:96 + 3 * L.vs].rearrange("p g (i f) -> p g i f", i=3)

            def bc(lo, hi, c):
                return rec[:, u % 4, :, L.y + lo:L.y + hi].unsqueeze(3).to_broadcast([P, G, hi - lo, c])

            def axes(a, c):
                return a.unsqueeze(2).to_broadcast([P, G, 3, c])

            if w is not None:
                ve.wait_ge(axes_done.h, axes_done.free(i, u, 1))
                nc.vector.tensor_tensor(t_sv[:, :, :], w[:, :, 64:128], s, ALU.mult).then_inc(sv_ready.h, 1)
            if L.cross:
                nc.vector.tensor_tensor(t_cr2[:, :, 0:1, :], v[:, :, 2:3, :], bc(1, 2, 32), ALU.mult)
                nc.vector.tensor_tensor(t_cr2[:, :, 1:3, :], v[:, :, 0:2, :], bc(2, 4, 32), ALU.mult)
            if w is None:
                nc.vector.tensor_tensor(t[:, :, 0:64], y0.to_broadcast([P, G, 64]), s, ALU.mult)
                nc.vector.tensor_tensor(tv[:, :, :, 64:96], v, axes(y0.to_broadcast([P, G, 32]), 32), ALU.mult)
            elif y0 is None:
                nc.vector.tensor_tensor(t[:, :, 0:64], w[:, :, 0:64], s, ALU.mult)
                nc.vector.tensor_tensor(tv[:, :, :, 64:96], v, axes(w[:, :, 128:160], 32), ALU.mult)
            else:
                for g in range(G):
                    nc.vector.scalar_tensor_tensor(t[:, g, 0:64], w[:, g, 0:64], y0[:, g, :], s[:, g, :],
                                                   ALU.mult, ALU.mult)
                    nc.vector.scalar_tensor_tensor(tv[:, g, :, 64:96], v[:, g], y0[:, g, :],
                                                   w[:, g, 128:160].unsqueeze(1).to_broadcast([P, 3, 32]),
                                                   ALU.mult, ALU.mult)
            ve.wait_ge(pooled.h, pooled.done(i, u))
            nc.vector.tensor_tensor(t_sum[:, :, :], t_dot[:, slot, :, 0, :], t_dot[:, slot, :, 1, :], ALU.add)\
                .then_inc(part1.h, 1)
            ve.wait_ge(part1.h, part1.done(i, u))
            dot = t[:, :, 64:96] if w is None else t_sum2[:, :, :]
            last = nc.vector.tensor_tensor(dot, t_sum[:, :, :], t_dot[:, slot, :, 2, :], ALU.add)
            if L.cross:
                cr = tv[:, :, :, 96:128] if w is None else t_cr3[:, :, :, :]
                last = nc.vector.tensor_tensor(cr, t_cr[:, slot], t_cr2[:, :, :, :], ALU.subtract)
            if w is None:
                return last
            last.then_inc(part2.h, 1)
            ve.wait_ge(part2.h, part2.done(i, u))
            if L.cross:
                nc.vector.tensor_tensor(tv[:, :, :, 96:128], t_cr3[:, :, :, :], axes(w[:, :, 192:224], 32), ALU.mult)
            return nc.vector.tensor_tensor(t[:, :, 64:96], t_sum2[:, :, :], w[:, :, 160:192], ALU.mult)

        class Layer:
            pass

        def layer(n):
            L = Layer()
            L.n = n
            L.src_order = n == 1
            L.records = rec_src_v if n == 1 else rec_dst_v
            L.head = (EA3 - EA64, 7) if n == 1 else (0, 8)
            L.ef, L.efw = {0: (EA16, 16), 1: (0, 64), 2: (EA16, 16), 3: (EA64, 64)}[n]
            L.idx, L.key, L.y = (5, 6, 0) if n == 1 else (1, 0, 3)
            L.y0 = None if n == 1 else 2
            L.cross = n != 2
            L.vs = 128 if L.cross else 96
            L.width = 96 + 3 * L.vs + (n == 2)
            L.blocks = pair_block[1 if n == 1 else 0]
            return L

        def load_records(sp, L, i, u, done):
            lo, w = L.head
            sp.dma_start(rec[:, u, :, 0:w], L.records[i, u, :, :, lo:lo + w]).then_inc(done, 16)
            sp.dma_start(efr[:, u, 0:G * L.efw].rearrange("p (g f) -> p g f", g=G),
                         L.records[i, u, :, :, L.ef:L.ef + L.efw]).then_inc(done, 16)

        def edge_loop(L):
            rec_in = [mark(f"rec_in{u}", 32 * QP) for u in range(4)]
            gat_in = [mark(f"gat_in{u}", 32 * QP) for u in range(4)]
            pooled = sig4("pooled", 1, NP)
            ef_t = sig4("ef_t", 1, NP)
            ef_ready = sig4("ef_ready", 1, NP)
            hid = sig4("hid", 1, NP)
            hid_ready = sig4("hid_ready", 1, NP)
            w_ready = sig4("w_ready", 1, NP)
            sv_ready = sig4("sv_ready", 1, NP)
            axes_done = sig4("axes_done", 1, NP)
            part1 = sig4("part1", 1, NP)
            part2 = sig4("part2", 1, NP)
            tp_ready = sig4("tp_ready", 1, NP)
            summed = sig4("summed", 1, NP)
            kept = sig4("kept", 1, NP)
            zeroed = mark("sums_zeroed", 1 + (L.n == 2))
            TW = L.width
            fc1, fc2 = W[f"fc1_{L.n}"], W[f"fc2_{L.n}"]
            EW = G * L.efw
            pE, pH, pW, pS = BK[0], BK[1], [BK[2], BK[3]], [BK[4], BK[5]]

            def w_of(u):
                return pW[u % 2][:, 0:448].rearrange("p (g f) -> p g f", g=G)

            with nc.Block() as block:
                @block.sync
                def _(sp):
                    start(sp)

                    def records(i, u, first=False):
                        if not first:
                            sp.wait_ge(tp_ready.h, tp_ready.free(i, u, 4))
                            sp.sem_inc(sp_tick, 1)
                            sp.wait_ge(axes_done.h, axes_done.free(i, u, 4))
                            sp.sem_inc(sp_tick, 1)
                        load_records(sp, L, i, u, rec_in[u].h)

                    for u in range(4):
                        records(0, u, True)
                    with sp.Fori(1, QP) as i:
                        for u in range(4):
                            records(i, u)

                @block.gpsimd
                def _(po):
                    if L.n == 2:
                        nc.gpsimd.memset(tp[:, :, :, 384:385], 1.0).then_inc(zeroed.h, 1)

                    def gather(i, u):
                        po.wait_ge(rec_in[u].h, rec_in[u].at(i * 32 + 32))
                        po.sem_inc(pool_tick, 1)
                        po.wait_ge(tp_ready.h, tp_ready.free(i, u, 4))
                        po.sem_inc(pool_tick, 1)
                        for g in range(G):
                            nc.gpsimd.indirect_dma_start(
                                out=gat[:, u, g, :], out_offset=None, in_=tables[L.n][:, :],
                                in_offset=IOff(ap=rec[:, u, g, L.idx:L.idx + 1].bitcast(i32), axis=0))\
                                .then_inc(gat_in[u].h, 16)

                    def part(i, u):
                        po.wait_ge(gat_in[u].h, gat_in[u].at(i * 32 + 32))
                        po.sem_inc(pool_tick, 1)
                        po.wait_ge(tp_ready.h, tp_ready.free(i, u))
                        po.sem_inc(pool_tick, 1)
                        product_pool(L, gat[:, u], u, u % 2).then_inc(pooled.h, 1)

                    for u in range(2):
                        gather(0, u)
                    with po.Fori(0, QP - 1) as i:
                        for u in range(4):
                            part(i, u)
                            gather(*((i, u + 2) if u < 2 else (i + 1, u - 2)))
                    for u in range(4):
                        part(QP - 1, u)
                        if u < 2:
                            gather(QP - 1, u + 2)

                @block.scalar
                def _(ac):
                    def features(i, u):
                        ac.wait_ge(ef_t.h, ef_t.done(i, u))
                        nc.scalar.activation(efT[0:EW, u % 2, :], pE[0:EW, 128 * (u % 2):128 * (u % 2) + 128], ACT.Copy)\
                            .then_inc(ef_ready.h, 1)

                    def activated(i, u):
                        ac.wait_ge(hid.h, hid.done(i, u))
                        func, by = {1: (ACT.Relu, 1.0), 2: (ACT.Silu, 0.25), 3: (ACT.Silu, 0.125)}[L.n]
                        nc.scalar.activation(hT[:, u % 2, :], pH[:, 128 * (u % 2):128 * (u % 2) + 128], func, scale=by)\
                            .then_inc(hid_ready.h, 1)

                    def axes(i, u):
                        ac.wait_ge(sv_ready.h, sv_ready.done(i, u))
                        product_scalar(i, u, t_sv, u % 2, L).then_inc(axes_done.h, 1)

                    def step(i, u, ahead):
                        if ahead:
                            features(*ahead)
                        axes(i, u)
                        if ahead:
                            activated(*ahead)

                    features(0, 0)
                    activated(0, 0)
                    with ac.Fori(0, QP - 1) as i:
                        for u in range(4):
                            step(i, u, (i, u + 1) if u < 3 else (i + 1, 0))
                    for u in range(4):
                        step(QP - 1, u, (QP - 1, u + 1) if u < 3 else None)

                @block.tensor
                def _(pe):
                    def transposed(i, u):
                        pe.wait_ge(rec_in[u].h, rec_in[u].at(i * 32 + 32))
                        pe.wait_ge(ef_ready.h, ef_ready.free(i, u))
                        c = 128 * (u % 2)
                        nc.tensor.transpose(pE[0:EW, c:c + 128], efr[:, u, 0:G * L.efw],
                                            ident[:, :]).then_inc(ef_t.h, 1)

                    def hidden(i, u):
                        pe.wait_ge(ef_ready.h, ef_ready.done(i, u))
                        pe.wait_ge(hid_ready.h, hid_ready.free(i, u))
                        c = 128 * (u % 2)
                        nc.tensor.matmul(pH[:, c:c + 128], fc1[0:EW, :], efT[0:EW, u % 2, :],
                                         start=True, stop=True).then_inc(hid.h, 1)

                    def weights(i, u):
                        pe.wait_ge(hid_ready.h, hid_ready.done(i, u))
                        pe.wait_ge(tp_ready.h, tp_ready.free(i, u))
                        nc.tensor.matmul(pW[u % 2][:, 0:448], hT[:, u % 2, :], fc2[:, :], start=True, stop=True)\
                            .then_inc(w_ready.h, 1)

                    def sums(i, u, g):
                        if g == 0:
                            pe.wait_ge(tp_ready.h, tp_ready.done(i, u))
                            pe.wait_ge(axes_done.h, axes_done.done(i, u))
                            pe.wait_ge(kept.h, kept.free(i, u))
                        last = nc.tensor.matmul(pS[u % 2][:, 0:TW], oh[:, u, g, :], tp[:, u % 2, g, 0:TW],
                                                start=g == 0, stop=g == G - 1)
                        if g == G - 1:
                            last.then_inc(summed.h, 1)

                    for u in range(2):
                        transposed(0, u)
                        hidden(0, u)
                        weights(0, u)
                    def both(i, u):
                        ahead = (i, u + 2) if u < 2 else (i + 1, u - 2)
                        transposed(*ahead)
                        sums(i, u, 0)
                        hidden(*ahead)
                        sums(i, u, 1)
                        weights(*ahead)

                    with pe.Fori(0, QP - 1) as i:
                        for u in range(4):
                            both(i, u)
                    for u in range(2):
                        both(QP - 1, u)
                    for u in range(2, 4):
                        for g in range(G):
                            sums(QP - 1, u, g)

                @block.vector
                def _(ve):
                    nc.vector.memset(ACC[:, 0:NBX * TW], 0.0).then_inc(zeroed.h, 1)
                    acc = ACC[:, 0:NBX * TW].rearrange("p (b f) -> p b f", b=NBX)

                    def product(i, u):
                        ve.wait_ge(rec_in[u].h, rec_in[u].at(i * 32 + 32))
                        ve.wait_ge(summed.h, summed.free(i, u))
                        for g in range(G):
                            nc.vector.tensor_scalar(oh[:, u, g, :], iota1[:, :], rec[:, u, g, L.key:L.key + 1],
                                                    None, ALU.is_equal)
                        ve.wait_ge(w_ready.h, w_ready.done(i, u))
                        ve.wait_ge(gat_in[u].h, gat_in[u].at(i * 32 + 32))
                        y0 = None if L.y0 is None else rec[:, u, :, L.y0:L.y0 + 1]
                        product_vector(ve, L, i, u, gat[:, u], w_of(u), y0, u % 2, pooled, part1, part2,
                                       sv_ready, axes_done)\
                            .then_inc(tp_ready.h, 1)

                    def block_of(i, u):
                        return ve.value_load(L.blocks[0:1, bass.ds(i * 4 + u, 1)], min_val=0, max_val=NB - 1)

                    def keep(i, u, b):
                        ve.wait_ge(summed.h, summed.done(i, u))
                        row = acc[:, bass.ds(b, 1), :].rearrange("p o f -> p (o f)")
                        ve.wait_ge(kept.h, kept.free(i, u, 1))
                        nc.vector.tensor_tensor(row, row, pS[u % 2][:, 0:TW], ALU.add).then_inc(kept.h, 1)

                    ve.wait_ge(zeroed.h, zeroed.at(1 + (L.n == 2)))
                    product(0, 0)
                    with ve.Fori(0, QP - 1) as i:
                        for u in range(4):
                            b = block_of(i, u)
                            product(*((i, u + 1) if u < 3 else (i + 1, 0)))
                            keep(i, u, b)
                    for u in range(4):
                        b = block_of(QP - 1, u)
                        if u < 3:
                            product(QP - 1, u + 1)
                        keep(QP - 1, u, b)
                    ve.wait_ge(kept.h, kept.done(QP - 1, 3))

        HNB = NBX // 2

        def node_table(n):
            rows = sig("rows", 1, NBX)
            rows_t = sig("rows_t", 1, NBX)
            rowsT = sig("rowsT", 1, NBX)
            made = sig("made", 1, NBX)
            tb_ready = sig("tb_ready", 1, NBX)
            normed = sig("normed", 1, NBX if n else 0)
            rooted = mark("rooted", 1 if n else 2)
            rstd_ready = mark("rstd_ready", 2 if n else 3)
            stored = [mark(f"stored{u}", 16 * (NBX // 2)) for u in range(2)]
            ts, tv_ = W[f"ts{n}"], W[f"tv{n}"]
            SW, VW = (128, 192) if n == 0 else (64, 96)
            TD = ACC[:, 8400:8400 + NBX * F].rearrange("p (b f) -> p b f", b=NBX)
            pT, pM = [BK[0], BK[1]], [BK[2], BK[3]]
            with nc.Block() as block:
                @block.scalar
                def _(ac):
                    ac.wait_ge(rstd_ready.h, rstd_ready.at(1))
                    nc.scalar.activation(rstd[:, :], rstd[:, :], ACT.Sqrt).then_inc(rooted.h, 1)
                    if n == 0:
                        nc.scalar.activation(rstd_v[:, :], rstd_v[:, :], ACT.Sqrt).then_inc(rooted.h, 1)

                    def copies(i, u):
                        ac.wait_ge(rows_t.h, rows_t.done(i, u))
                        ac.wait_ge(made.h, made.free(i, u))
                        if n == 0:
                            nc.scalar.activation(xT[0:64, u, 0:128], pT[u][0:64, 0:128], ACT.Identity,
                                                 bias=W["bet_s"][:, :], scale=W["gam_s"][:, :])
                            nc.scalar.activation(xT[0:96, u, 128:256], pT[u][0:96, 128:256], ACT.Copy,
                                                 scale=W["gam_v"][:, :]).then_inc(rowsT.h, 1)
                        else:
                            nc.scalar.activation(xT[0:64, u, 0:128], pT[u][0:64, 0:128], ACT.Copy)
                            nc.scalar.activation(xT[0:96, u, 128:256], pT[u][0:96, 128:256], ACT.Copy)\
                                .then_inc(rowsT.h, 1)

                    with ac.Fori(0, HNB) as i:
                        for u in range(2):
                            copies(i, u)

                @block.vector
                def _(ve):
                    first = nc.vector.tensor_scalar_add(rstd[:, :], stat[:, :, 1], EPS)
                    if n != 0:
                        first.then_inc(rstd_ready.h, 1)
                    else:
                        nc.vector.tensor_scalar(rstd_v[:, :], vsq[:, :], 1.0 / CV, EPS, ALU.mult, ALU.add)\
                            .then_inc(rstd_ready.h, 1)
                    ve.wait_ge(rooted.h, rooted.at(2 if n == 0 else 1))
                    nc.vector.reciprocal(rstd[:, :], rstd[:, :]).then_inc(rstd_ready.h, 1)
                    if n == 0:
                        nc.vector.reciprocal(rstd_v[:, :], rstd_v[:, :]).then_inc(rstd_ready.h, 1)
                    ve.wait_ge(rstd_ready.h, rstd_ready.at(3 if n == 0 else 2))

                    def norm(i, u):
                        b = i * 2 + u
                        xb = X[:, bass.ds(b, 1), :].rearrange("p o f -> p (o f)")
                        mu = stat[:, bass.ds(b, 1), 0]
                        rs = rstd[:, bass.ds(b, 1)]
                        ve.wait_ge(rows_t.h, rows_t.free(i, u))
                        xv = xn[:, u, 64:160].rearrange("p (i c) -> p i c", i=3)
                        src = X[:, bass.ds(b, 1), 64:160].rearrange("p o (c i) -> p i (o c)", i=3)
                        if n == 0:
                            nc.vector.tensor_scalar(xn[:, u, 0:64], X[:, bass.ds(b, 1), 0:64].rearrange(
                                "p o f -> p (o f)"), mu, rs, ALU.subtract, ALU.mult)
                            nc.vector.tensor_scalar(xv, src, rstd_v[:, bass.ds(b, 1)], None, ALU.mult)\
                                .then_inc(rows.h, 1)
                        else:
                            nc.vector.tensor_scalar(xb, xb, mu, rs, ALU.subtract, ALU.mult).then_inc(normed.h, 1)
                            ve.wait_ge(normed.h, normed.done(i, u))
                            ve.sem_inc(ve_tick, 1)
                            nc.vector.tensor_copy(xn[:, u, 0:64], X[:, bass.ds(b, 1), 0:64].rearrange(
                                "p o f -> p (o f)"))
                            nc.vector.tensor_copy(xv, src).then_inc(rows.h, 1)

                    def table(i, u):
                        b = i * 2 + u
                        ve.wait_ge(made.h, made.done(i, u))
                        if not (isinstance(i, int) and i == 0):
                            ve.wait_ge(stored[u].h, stored[u].at(i * 16))
                            ve.sem_inc(ve_tick, 1)
                        if n == 0:
                            ve.sem_inc(ve_tick, 1)
                            nc.vector.tensor_copy(TD[:, bass.ds(b, 1), 0:64].rearrange("p o f -> p (o f)"),
                                                  pM[u][:, 64:128])
                            nc.vector.tensor_copy(TD[:, bass.ds(b, 1), 64:160].rearrange("p o f -> p (o f)"),
                                                  pM[u][:, 224:320])
                            nc.vector.tensor_copy(tb[:, u, 0:64], pM[u][:, 0:64])
                            nc.vector.tensor_copy(tb[:, u, 64:160], pM[u][:, 128:224]).then_inc(tb_ready.h, 1)
                        elif n == 1:
                            nc.vector.tensor_copy(tb[:, u, :], pM[u][:, 0:160]).then_inc(tb_ready.h, 1)
                        else:
                            nc.vector.tensor_scalar(tb[:, u, :], pM[u][:, 0:160], node_a[:, bass.ds(b, 1)], None,
                                                    ALU.mult).then_inc(tb_ready.h, 1)

                    for u in range(2):
                        norm(0, u)
                    for u in range(2):
                        norm(1, u)
                    for u in range(2):
                        table(0, u)
                    with ve.Fori(1, HNB - 1) as i:
                        for u in range(2):
                            norm(i + 1, u)
                        for u in range(2):
                            table(i, u)
                    for u in range(2):
                        table(HNB - 1, u)

                @block.tensor
                def _(pe):
                    def turn(i, u):
                        pe.wait_ge(rows.h, rows.done(i, u))
                        pe.wait_ge(rowsT.h, rowsT.free(i, u))
                        nc.tensor.transpose(pT[u][0:96, 128:256], xn[:, u, 64:160], ident[:, :])
                        nc.tensor.transpose(pT[u][0:64, 0:128], xn[:, u, 0:64], ident[:, :]).then_inc(rows_t.h, 1)

                    def make(i, u):
                        pe.wait_ge(rowsT.h, rowsT.done(i, u))
                        pe.wait_ge(tb_ready.h, tb_ready.free(i, u))
                        nc.tensor.matmul(pM[u][:, 0:SW], xT[0:64, u, 0:128], ts[:, :], start=True, stop=True)
                        nc.tensor.matmul(pM[u][:, SW:SW + VW], xT[0:96, u, 128:256], tv_[:, :], start=True, stop=True)\
                            .then_inc(made.h, 1)

                    for u in range(2):
                        turn(0, u)
                    with pe.Fori(0, HNB - 1) as i:
                        for u in range(2):
                            turn(i + 1, u)
                        for u in range(2):
                            make(i, u)
                    for u in range(2):
                        make(HNB - 1, u)

                @block.sync
                def _(sp):
                    start(sp)
                    with sp.Fori(0, HNB) as i:
                        for u in range(2):
                            sp.wait_ge(tb_ready.h, tb_ready.done(i, u))
                            sp.sem_inc(sp_tick, 1)
                            sp.dma_start(tables_v[n][i, u], tb[:, u, :]).then_inc(stored[u].h, 16)
                    for u in range(2):
                        sp.wait_ge(stored[u].h, stored[u].at(HNB * 16))

        def statistics(ve, i, u, cols, seen):
            b = i * 2 + u
            x = X[:, bass.ds(b, 1), 0:cols].rearrange("p o f -> p (o f)")
            nc.vector.bn_stats(bn6[:, u, :], x).then_inc(seen.h, 1)
            ve.wait_ge(seen.h, seen.done(i, u, 1))
            ve.sem_inc(ve_tick, 1)
            nc.vector.bn_aggr(mean_var[:, u, :], bn6[:, u, :]).then_inc(seen.h, 1)
            ve.wait_ge(seen.h, seen.done(i, u, 2))
            ve.sem_inc(ve_tick, 1)
            nc.vector.tensor_copy(stat[:, bass.ds(b, 1), :].rearrange("p o f -> p (o f)"), mean_var[:, u, :])

        def node_update(L):
            n = L.n
            copied_in = sig("copied_in", 1, NBX)
            turned = sig("turned", 1, NBX)
            copied = sig("copied", 1, NBX)
            made = sig("made", 1, NBX)
            gated = sig("gated_out", 1, NBX)
            upd = sig("upd", 3, NBX if n == 2 else 0)
            alpha_made = sig("alpha_made", 1, NBX if n == 2 else 0)
            y_made = sig("y_made", 1, NBX)
            updated = sig("updated", 1, NBX)
            seen = sig("seen", 2, NBX)
            pX_, pA, pO = [BK[0], BK[1]], [BK[2], BK[3]], [BK[4], BK[5]]
            TW, VS = L.width, L.vs
            acc = ACC[:, 0:NBX * TW].rearrange("p (b f) -> p b f", b=NBX)
            nS = 64 if n == 2 else 96
            with nc.Block() as block:
                @block.vector
                def _(ve):
                    def rows(i, u):
                        b = bass.ds(i * 2 + u, 1)
                        ve.wait_ge(turned.h, turned.free(i, u))
                        ve.sem_inc(ve_tick, 1)
                        nc.vector.tensor_copy(xn[:, u, 64:160].rearrange("p (i c) -> p i c", i=3),
                                              X[:, b, 64:160].rearrange("p o (c i) -> p i (o c)", i=3))
                        nc.vector.tensor_copy(xn[:, u, 0:64], X[:, b, 0:64].rearrange("p o f -> p (o f)"))
                        a = acc[:, b, 0:96 + 3 * VS].rearrange("p o f -> p (o f)")
                        nc.vector.tensor_copy(accrow[:, u, 0:96 + 3 * VS], a).then_inc(copied_in.h, 1)

                    def outputs(i, u):
                        b = bass.ds(i * 2 + u, 1)
                        ys = y_s[:, u, 0:64]
                        yv = y_s[:, u, 64:160].rearrange("p (i c) -> p i c", i=3)
                        a = node_a[:, b]
                        if n == 2:
                            c = acc[:, b, 384:385].rearrange("p o f -> p (o f)")
                            nc.vector.tensor_scalar_max(nrm[:, u, 0:1], c, 1.0).then_inc(upd.h, 1)
                            ve.wait_ge(upd.h, upd.done(i, u, 1))
                            nc.vector.reciprocal(nrm[:, u, 1:2], nrm[:, u, 0:1]).then_inc(upd.h, 1)
                            ve.wait_ge(upd.h, upd.done(i, u, 2))
                            nc.vector.tensor_scalar(nrm[:, u, 2:3], nrm[:, u, 1:2], node_a[:, b], None, ALU.mult)\
                                .then_inc(upd.h, 1)
                            ve.wait_ge(upd.h, upd.done(i, u, 3))
                            ve.wait_ge(made.h, made.done(i, u))
                            nc.vector.tensor_scalar(nrm[:, u, 3:4], pO[u][:, 224:225], nrm[:, u, 2:3], nrm[:, u, 2:3],
                                                    ALU.mult, ALU.mult).then_inc(alpha_made.h, 1)
                            ve.wait_ge(alpha_made.h, alpha_made.done(i, u))
                            nc.vector.tensor_scalar(y_s[:, u, 0:64], pO[u][:, 160:224], nrm[:, u, 3:4], None, ALU.mult)
                            nc.vector.tensor_scalar(y_s[:, u, 64:160], pO[u][:, 225:321], nrm[:, u, 3:4], None,
                                                    ALU.mult).then_inc(gated.h, 1)
                            ve.wait_ge(gated.h, gated.done(i, u))
                            nc.vector.scalar_tensor_tensor(y_s[:, u, :], pO[u][:, 0:160], a, y_s[:, u, :],
                                                           ALU.mult, ALU.add).then_inc(y_made.h, 1)
                            ve.wait_ge(y_made.h, y_made.done(i, u))
                        else:
                            ve.wait_ge(gated.h, gated.done(i, u))
                            by = a if n == 3 else 1.0
                            nc.vector.scalar_tensor_tensor(ys, pO[u][:, 0:64], by, sgm[:, u, 0:64],
                                                           ALU.mult, ALU.mult)
                            nc.vector.scalar_tensor_tensor(
                                yv, pO[u][:, 96:192].rearrange("p (i c) -> p i c", i=3), by,
                                sgm[:, u, 64:96].unsqueeze(1).to_broadcast([P, 3, 32]), ALU.mult, ALU.mult)\
                                .then_inc(y_made.h, 1)
                            ve.wait_ge(y_made.h, y_made.done(i, u))
                        xs = X[:, b, 0:64].rearrange("p o f -> p (o f)")
                        xv = X[:, b, 64:160].rearrange("p o (c i) -> p i (o c)", i=3)
                        nc.vector.tensor_tensor(xs, xs, ys, ALU.add)
                        nc.vector.tensor_tensor(xv, xv, yv, ALU.add).then_inc(updated.h, 1)
                        ve.wait_ge(updated.h, updated.done(i, u))
                        ve.sem_inc(ve_tick, 1)
                        statistics(ve, i, u, F, seen)

                    rows(0, 0)
                    rows(0, 1)
                    with ve.Fori(0, HNB - 1) as i:
                        rows(i + 1, 0)
                        rows(i + 1, 1)
                        outputs(i, 0)
                        outputs(i, 1)
                    outputs(HNB - 1, 0)
                    outputs(HNB - 1, 1)

                @block.tensor
                def _(pe):
                    def turn(i, u):
                        pe.wait_ge(copied_in.h, copied_in.done(i, u))
                        pe.wait_ge(copied.h, copied.free(i, u))
                        nc.tensor.transpose(pX_[u][0:96, 128:256], xn[:, u, 64:160], ident[:, :])
                        nc.tensor.transpose(pX_[u][0:64, 0:128], xn[:, u, 0:64], ident[:, :])
                        nc.tensor.transpose(pA[u][0:96, 0:128], accrow[:, u, 0:96], ident[:, :])
                        for k in range(3):
                            last = nc.tensor.transpose(pA[u][0:VS, 128 * k + 128:128 * k + 256],
                                                       accrow[:, u, 96 + VS * k:96 + VS * k + VS], ident[:, :])
                        last.then_inc(turned.h, 1)

                    def make(i, u):
                        pe.wait_ge(copied.h, copied.done(i, u))
                        pe.wait_ge(updated.h, updated.free(i, u))
                        xs, xv, os_, ov = (W[k + str(n)] for k in ("xs", "xv", "os", "ov"))
                        o_ = pO[u]
                        if n == 2:
                            nc.tensor.matmul(o_[:, 0:64], xT[0:64, u, 0:128], xs[:, :], start=True, stop=True)
                            nc.tensor.matmul(o_[:, 64:160], xT[0:96, u, 128:256], xv[:, :], start=True, stop=True)
                            nc.tensor.matmul(o_[:, 160:225], aT[0:96, u, 0:128], os_[:, :], start=True, stop=True)
                            for k in range(3):
                                last = nc.tensor.matmul(o_[:, 225 + 32 * k:257 + 32 * k],
                                                        aT[0:96, u, 128 * k + 128:128 * k + 256], ov[:, :],
                                                        start=True, stop=True)
                        else:
                            nc.tensor.matmul(o_[:, 0:96], xT[0:64, u, 0:128], xs[:, :], start=True, stop=False)
                            nc.tensor.matmul(o_[:, 0:96], aT[0:96, u, 0:128], os_[:, :], start=False, stop=True)
                            for k in range(3):
                                oc = slice(96 + 32 * k, 128 + 32 * k)
                                nc.tensor.matmul(o_[:, oc], xT[0:96, u, 128:256], xv[:, 32 * k:32 * k + 32],
                                                 start=True, stop=False)
                                last = nc.tensor.matmul(o_[:, oc], aT[:, u, 128 * k + 128:128 * k + 256], ov[:, :],
                                                        start=False, stop=True)
                        last.then_inc(made.h, 1)

                    for u in range(2):
                        turn(0, u)
                    with pe.Fori(0, HNB - 1) as i:
                        for u in range(2):
                            turn(i + 1, u)
                        for u in range(2):
                            make(i, u)
                    for u in range(2):
                        make(HNB - 1, u)

                @block.scalar
                def _(ac):
                    def copies(i):
                        for u in range(2):
                            ac.wait_ge(turned.h, turned.done(i, u))
                            ac.wait_ge(made.h, made.free(i, u))
                            nc.scalar.activation(xT[0:64, u, 0:128], pX_[u][0:64, 0:128], ACT.Copy)
                            nc.scalar.activation(xT[0:96, u, 128:256], pX_[u][0:96, 128:256], ACT.Copy)
                            nc.scalar.activation(aT[0:96, u, 0:128], pA[u][0:96, 0:128], ACT.Copy)
                            nc.scalar.activation(aT[0:VS, u, 128:512], pA[u][0:VS, 128:512], ACT.Copy)\
                                .then_inc(copied.h, 1)

                    def gates(i):
                        for u in range(0 if n == 2 else 2):
                            ac.wait_ge(made.h, made.done(i, u))
                            ac.wait_ge(updated.h, updated.free(i, u))
                            by = node_a[:, bass.ds(i * 2 + u, 1)] if n == 3 else 1.0
                            nc.scalar.activation(sgm[:, u, :], pO[u][:, 0:96], ACT.Sigmoid, scale=by)\
                                .then_inc(gated.h, 1)

                    copies(0)
                    with ac.Fori(0, HNB - 1) as i:
                        copies(i + 1)
                        gates(i)
                    gates(HNB - 1)

                @block.sync
                def _(sp):
                    start(sp)

        def last_norm():
            rooted = mark("rooted", 1)
            rstd_ready = mark("rstd_ready", 2)
            normed = sig("normed", 1, NBX)
            out_done = sem("out_done")
            with nc.Block() as block:
                @block.scalar
                def _(ac):
                    ac.wait_ge(rstd_ready.h, rstd_ready.at(1))
                    nc.scalar.activation(rstd[:, :], rstd[:, :], ACT.Sqrt).then_inc(rooted.h, 1)

                @block.vector
                def _(ve):
                    nc.vector.tensor_scalar_add(rstd[:, :], stat[:, :, 1], EPS).then_inc(rstd_ready.h, 1)
                    ve.wait_ge(rooted.h, rooted.at(1))
                    nc.vector.reciprocal(rstd[:, :], rstd[:, :]).then_inc(rstd_ready.h, 1)
                    ve.wait_ge(rstd_ready.h, rstd_ready.at(2))
                    with ve.Fori(0, HNB) as i:
                        for u in range(2):
                            b = bass.ds(i * 2 + u, 1)
                            xb = X[:, b, :].rearrange("p o f -> p (o f)")
                            nc.vector.tensor_scalar(xb, xb, stat[:, b, 0], rstd[:, b], ALU.subtract, ALU.mult)\
                                .then_inc(normed.h, 1)

                @block.sync
                def _(sp):
                    start(sp)
                    sp.wait_ge(normed.h, normed.done(HNB - 1, 1))
                    if NB > 1:
                        sp.dma_start(out[0:(NB - 1) * P, :].rearrange("(b p) f -> p b f", p=P), X[:, 0:NB - 1, :])\
                            .then_inc(out_done, 16)
                    sp.dma_start(out[(NB - 1) * P:N, :], X[0:LAST, NB - 1, :]).then_inc(out_done, 16)
                    sp.wait_ge(out_done, 32 if NB > 1 else 16)

        def first_statistics():
            seen = sig("seen", 2, NBX)
            squared = sig("squared", 1, NBX)
            with nc.Block() as block:
                @block.sync
                def _(sp):
                    start(sp)

                @block.vector
                def _(ve):
                    with ve.Fori(0, HNB) as i:
                        for u in range(2):
                            statistics(ve, i, u, 64, seen)

                @block.scalar
                def _(ac):
                    with ac.Fori(0, HNB) as i:
                        for u in range(2):
                            b = bass.ds(i * 2 + u, 1)
                            ac.wait_ge(squared.h, squared.free(i, u))
                            nc.scalar.activation(y_s[:, u, 64:160], X[:, b, 64:160].rearrange("p o f -> p (o f)"),
                                                 ACT.Square, accum_out=vsq[:, b]).then_inc(squared.h, 1)

        def layer0_edges(L):
            rec_in = [mark(f"rec_in{u}", 32 * QP) for u in range(4)]
            gat_in = [mark(f"gat_in{u}", 32 * QP) for u in range(4)]
            pooled1, pooled2 = sig4("pooled", 1, NP), sig4("pooled2", 1, NP)
            oh_ready = sig4("oh_ready", 1, NP)
            turned = sig4("turned_e", 1, NP)
            copied = sig4("copied_e", 1, NP)
            w_ready = sig4("w_ready", 1, NP)
            dst_ready = sig4("dst_ready", 1, NP)
            msg_ready = sig4("msg_ready", 1, NP)
            part1a, part2a, tp1_ready = sig4("part1", 1, NP), sig4("part2", 1, NP), sig4("tp_ready", 1, NP)
            sv1_ready, axes1 = sig4("sv_ready", 1, NP), sig4("axes_done", 1, NP)
            axes2 = sig4("axes2_done", 1, NP)
            minus_ready = sig4("minus_ready", 1, NP)
            xm0_ready = sig4("xm0_ready", 1, NP)
            part1b, part2b, tp2_ready = sig4("part1b", 1, NP), sig4("part2b", 1, NP), sig4("tp2_ready", 1, NP)
            t1, t1c = sig4("t1", 2, NP), sig4("t1c", 2, NP)
            t2, t2c = sig4("t2", 2, NP), sig4("t2c", 2, NP)
            val_ready = sig4("val_ready", 1, NP)
            squashed = sig4("squashed", 1, NP)
            gate_step = sig4("gate_step", 1, NP)
            gated = sig4("gated_e", 1, NP)
            leak = sig4("leak", 3, NP)
            xm_ready = sig4("xm_ready", 1, NP)
            xm_t = sig4("xm_t", 1, NP)
            top = sig4("top", 1, NP)
            m_step, mnew_ready = sig4("m_step", 1, NP), sig4("mnew_ready", 1, NP)
            msc_ready = sig4("msc_ready", 1, NP)
            mg_ready = sig4("mg_ready", 1, NP)
            dlt_ready = sig4("dlt_ready", 1, NP)
            pex_ready = sig4("pex_ready", 1, NP)
            h_ready = sig4("h_ready", 1, NP)
            hw_ready = sig4("hw_ready", 1, NP)
            summed = sig4("summed", 1, NP)
            scaled = sig4("scaled", 1, NP)
            kept = sig4("kept", 1, NP)
            zeroed_acc = mark("sums_zeroed", 1)
            acc = ACC[:, 0:NBX * 164].rearrange("p (b f) -> p b f", b=NBX)
            M = ACC[:, 8200:8200 + NBX * 4].rearrange("p (b h) -> p b h", b=NBX)
            TD = ACC[:, 8400:8400 + NBX * F].rearrange("p (b f) -> p b f", b=NBX)
            pE, pW, pB, pT, pV, pX = BK[0], BK[1], BK[2], [BK[3], BK[4]], BK[5], BK[6]
            pH, pG, pS = BK[7][:, 0:320], BK[7][:, 320:328], BK[7][:, 328:492]
            pVv = pV[:, :].rearrange("p (g f) -> p g f", g=G)
            pHv = pH.rearrange("p (g f) -> p g f", g=G)
            mT1, mT2 = mT, mTb

            def flat(a):
                return a.rearrange("p o f -> p (o f)")

            def pipeline(eng, step):
                for j in range(4):
                    step([(0, j - d) if j >= d else None for d in range(5)])
                with eng.Fori(1, QP) as i:
                    for u in range(4):
                        step([(i, u - d) for d in range(5)])
                for j in range(4, 8):
                    step([(QP - 1, j - d) if j - d < 4 else None for d in range(5)])

            def product_columns(k):
                return 0 if k == 0 else 96 + 128 * (k - 1)

            def block_of(eng, i, u):
                return bass.ds(eng.value_load(L.blocks[0:1, bass.ds(i * 4 + u, 1)], min_val=0, max_val=NB - 1), 1)

            with nc.Block() as block:
                @block.sync
                def _(sp):
                    start(sp)

                    def records(i, u, first=False):
                        if not first:
                            sp.wait_ge(tp2_ready.h, tp2_ready.free(i, u, 4))
                            sp.sem_inc(sp_tick, 1)
                            sp.wait_ge(axes2.h, axes2.free(i, u, 4))
                            sp.sem_inc(sp_tick, 1)
                        load_records(sp, L, i, u, rec_in[u].h)

                    for u in range(4):
                        records(0, u, True)
                    with sp.Fori(1, QP) as i:
                        for u in range(4):
                            records(i, u)

                @block.gpsimd
                def _(po):
                    def gather(i, u):
                        s4 = u % 4
                        po.wait_ge(rec_in[s4].h, rec_in[s4].at(i * 32 + 32))
                        po.sem_inc(pool_tick, 1)
                        po.wait_ge(msg_ready.h, msg_ready.free(i, u, 4))
                        po.sem_inc(pool_tick, 1)
                        for g in range(G):
                            nc.gpsimd.indirect_dma_start(
                                out=gat[:, s4, g, :], out_offset=None, in_=tables[0][:, :],
                                in_offset=IOff(ap=rec[:, s4, g, 1:2].bitcast(i32), axis=0))\
                                .then_inc(gat_in[s4].h, 16)

                    def part(i, u, sv, ready, used, slot, pooled):
                        po.wait_ge(ready.h, ready.done(i, u))
                        po.sem_inc(pool_tick, 1)
                        po.wait_ge(used.h, used.free(i, u, 1))
                        po.sem_inc(pool_tick, 1)
                        product_pool(L, sv, u % 4, slot).then_inc(pooled.h, 1)

                    def step(at):
                        a, b, c, d, e = at
                        if b:
                            part(*b, msg[:, b[1] % 2], msg_ready, tp1_ready, 0, pooled1)
                        if a:
                            gather(*a)
                        if c:
                            part(*c, vsv[:, c[1] % 2], gated, tp2_ready, 1, pooled2)

                    pipeline(po, step)

                @block.scalar
                def _(ac):
                    def copy_product(i, u, turned_, copied_, read, into):
                        ac.wait_ge(read.h, read.free(i, u, 1))
                        for g in range(G):
                            ac.wait_ge(turned_.h, turned_.done(i, u, g + 1))
                            nc.scalar.activation(into[:, g, :], pT[g][:, :], ACT.Copy).then_inc(copied_.h, 1)

                    def step(at):
                        a, b, c, d, e = at
                        if d:
                            copy_product(*d, t2, t2c, h_ready, mT2)
                        if a:
                            ac.wait_ge(turned.h, turned.done(*a))
                            nc.scalar.activation(efT[0:32, a[1] % 2, :], pE[0:32, 0:128], ACT.Copy)
                            ac.wait_ge(mg_ready.h, mg_ready.free(*a, 4))
                            nc.scalar.activation(ohT[:, a[1] % 4].rearrange("p g e -> p (g e)"), pE[:, 128:384],
                                                 ACT.Copy).then_inc(copied.h, 1)
                        if b:
                            ac.wait_ge(sv1_ready.h, sv1_ready.done(*b))
                            product_scalar(*b, t_sv, 0, L).then_inc(axes1.h, 1)
                        if d:
                            ac.wait_ge(dlt_ready.h, dlt_ready.done(*d))
                            ac.wait_ge(hw_ready.h, hw_ready.free(*d))
                            nc.scalar.activation(pex[:, d[1] % 2], dlt[:, d[1] % 2], ACT.Exp)\
                                .then_inc(pex_ready.h, 1)
                            ac.wait_ge(mnew_ready.h, mnew_ready.done(*d))
                            ac.wait_ge(scaled.h, scaled.free(*d, 4))
                            nc.scalar.activation(msc[:, d[1] % 4], mdiff[:, d[1] % 2], ACT.Exp)\
                                .then_inc(msc_ready.h, 1)
                        if b:
                            copy_product(*b, t1, t1c, val_ready, mT1)
                        if c:
                            ac.wait_ge(minus_ready.h, minus_ready.done(*c))
                            ac.wait_ge(leak.h, leak.done(*c))
                            for h in range(4):
                                last = nc.scalar.activation(xm[:, 0, h, :], mb[:, c[1] % 2, 0, :], ACT.Identity,
                                                            bias=a4[:, c[1] % 2, 0, h:h + 1])
                            last.then_inc(xm0_ready.h, 1)
                            ac.wait_ge(squashed.h, squashed.done(*c))
                            ac.wait_ge(t2.h, t2.free(*c, 1))
                            product_scalar(*c, vsv[:, c[1] % 2, :, 0:64], 1, L).then_inc(axes2.h, 1)
                        if b:
                            ac.wait_ge(xm_ready.h, xm_ready.free(*b))
                            nc.scalar.activation(mb[:, b[1] % 2], oh[:, b[1] % 4], ACT.Copy, bias=-NEG, scale=NEG)\
                                .then_inc(minus_ready.h, 1)
                        if b:
                            s2 = b[1] % 2
                            ac.wait_ge(val_ready.h, val_ready.done(*b))
                            nc.scalar.activation(th[:, s2], pVv[:, :, 64:160], ACT.Tanh, scale=0.5)\
                                .then_inc(gate_step.h, 1)
                            ac.wait_ge(leak.h, leak.free(*b, 1))
                            nc.scalar.activation(lk[:, :, :], pVv[:, :, 0:64], ACT.Copy, scale=0.2)
                            ac.wait_ge(gate_step.h, gate_step.done(*b))
                            ac.wait_ge(tp2_ready.h, tp2_ready.free(*b))
                            ac.wait_ge(gated.h, gated.free(*b, 1))
                            nc.scalar.activation(vsv[:, s2, :, 0:64], th[:, s2, :, 0:64], ACT.Copy,
                                                 bias=0.5, scale=0.5)
                            nc.scalar.activation(th2[:, :, 64:96], th[:, s2, :, 64:96], ACT.Copy,
                                                 bias=0.5, scale=0.5).then_inc(squashed.h, 1)

                    pipeline(ac, step)

                @block.tensor
                def _(pe):
                    def product_turned(i, u, slot, ready, axes_, turned_, other_copied, other):
                        pe.wait_ge(axes_.h, axes_.done(i, u))
                        pe.wait_ge(ready.h, ready.done(i, u))
                        for g in range(G):
                            if other:
                                pe.wait_ge(other_copied.h, other_copied.done(*other, g + 1))
                            for k in range(4):
                                lo = product_columns(k)
                                last = nc.tensor.transpose(pT[g][:, 128 * k:128 * k + 128],
                                                           tp[:, slot, g, lo:lo + 128], ident[:, :])
                            last.then_inc(turned_.h, 1)

                    def logits_turned(i, u):
                        pe.wait_ge(xm_ready.h, xm_ready.done(i, u))
                        pe.wait_ge(top.h, top.free(i, u, 1))
                        for h in range(4):
                            last = nc.tensor.transpose(pX[:, 128 * h:128 * h + 128], xm[:, 1, h, :], ident[:, :])
                        last.then_inc(xm_t.h, 1)

                    def step(at):
                        a, b, c, d, e = at
                        if e:
                            pe.wait_ge(hw_ready.h, hw_ready.done(*e))
                            pe.wait_ge(kept.h, kept.free(*e, 1))
                            for g in range(G):
                                last = nc.tensor.matmul(pS, oh[:, e[1] % 4, g, :], hw[:, e[1] % 2, g, :],
                                                        start=g == 0, stop=g == G - 1)
                            last.then_inc(summed.h, 1)
                        if d:
                            product_turned(*d, 1, tp2_ready, axes2, t2, t1c, c)
                            pe.wait_ge(mnew_ready.h, mnew_ready.done(*d))
                            for g in range(G):
                                last = nc.tensor.matmul(pG[:, 4 * g:4 * g + 4], ohT[:, d[1] % 4, g, :],
                                                        mnew[:, d[1] % 2, :], start=True, stop=True)
                            last.then_inc(mg_ready.h, 1)
                        if a:
                            s4 = a[1] % 4
                            pe.wait_ge(rec_in[s4].h, rec_in[s4].at(a[0] * 32 + 32))
                            pe.wait_ge(oh_ready.h, oh_ready.done(*a))
                            pe.wait_ge(copied.h, copied.free(*a, 1))
                            nc.tensor.transpose(pE[0:32, 0:128], efr[:, s4, 0:G * L.efw], ident[:, :])
                            for g in range(G):
                                last = nc.tensor.transpose(pE[:, 128 + 128 * g:256 + 128 * g], oh[:, s4, g, :],
                                                           ident[:, :])
                            last.then_inc(turned.h, 1)
                        if d:
                            pe.wait_ge(dlt_ready.h, dlt_ready.done(*d))
                            for g in range(G):
                                pe.wait_ge(t2c.h, t2c.done(*d, g + 1))
                                hd = pHv[:, g, :].rearrange("p (h f) -> p h f", h=4)
                                nc.tensor.matmul(hd[:, :, 0:16], mT2[0:96, g, 0:128], W["svlin0"][:, :],
                                                 start=True, stop=True)
                                for k in range(3):
                                    last = nc.tensor.matmul(hd[:, :, 16 + 8 * k:24 + 8 * k],
                                                            mT2[:, g, 128 * k + 128:128 * k + 256],
                                                            W["vvlin0"][:, :], start=True, stop=True)
                            last.then_inc(h_ready.h, 1)
                        if b:
                            product_turned(*b, 0, tp1_ready, axes1, t1, t2c, d)
                        if a:
                            row = block_of(pe, *a)
                            pe.wait_ge(copied.h, copied.done(*a))
                            pe.wait_ge(msg_ready.h, msg_ready.free(*a, 1))
                            for g in range(G):
                                last = nc.tensor.matmul(pB[:, F * g:F * g + F], ohT[:, s4, g, :],
                                                        flat(TD[:, row, :]), start=True, stop=True)
                            last.then_inc(dst_ready.h, 1)
                            pe.wait_ge(tp1_ready.h, tp1_ready.free(*a, 1))
                            nc.tensor.matmul(pW[:, 0:448], efT[0:32, a[1] % 2, :], W["rbf0"][:, :],
                                             start=True, stop=True).then_inc(w_ready.h, 1)
                        if b:
                            pe.wait_ge(gated.h, gated.free(*b, 1))
                            pe.wait_ge(leak.h, leak.free(*b, 1))
                            for g in range(G):
                                pe.wait_ge(t1c.h, t1c.done(*b, g + 1))
                                nc.tensor.matmul(pV[:, 256 * g:256 * g + 160], mT1[0:96, g, 0:128],
                                                 W["alpha0"][:, :], start=True, stop=True)
                                for k in range(3):
                                    last = nc.tensor.matmul(pV[:, 256 * g + 160 + 32 * k:256 * g + 192 + 32 * k],
                                                            mT1[:, g, 128 * k + 128:128 * k + 256],
                                                            W["val0"][:, :], start=True, stop=True)
                            last.then_inc(val_ready.h, 1)
                        if c:
                            logits_turned(*c)

                    pipeline(pe, step)

                @block.vector
                def _(ve):
                    nc.vector.memset(ACC[:, 0:8200], 0.0)
                    nc.vector.memset(ACC[:, 8200:8200 + NBX * 4], -NEG).then_inc(zeroed_acc.h, 1)
                    ve.wait_ge(zeroed_acc.h, zeroed_acc.at(1))

                    def message(i, u):
                        ve.wait_ge(dst_ready.h, dst_ready.done(i, u))
                        ve.wait_ge(gat_in[u % 4].h, gat_in[u % 4].at((i + u // 4) * 32 + 32))
                        nc.vector.tensor_tensor(msg[:, u % 2], gat[:, u % 4], pB[:, 0:320].rearrange(
                            "p (g f) -> p g f", g=G), ALU.add).then_inc(msg_ready.h, 1)

                    def distances(i, u):
                        ve.wait_ge(mg_ready.h, mg_ready.done(i, u))
                        nc.vector.tensor_tensor(dlt[:, u % 2], a4[:, u % 2], pG.rearrange("p (g h) -> p g h", g=G),
                                                ALU.subtract).then_inc(dlt_ready.h, 1)

                    def logits(i, u):
                        ve.wait_ge(squashed.h, squashed.done(i, u))
                        nc.vector.tensor_tensor(la[:, :, :], pVv[:, :, 0:64], lk[:, :, :], ALU.max)\
                            .then_inc(leak.h, 1)
                        ve.wait_ge(leak.h, leak.done(i, u, 1))
                        nc.vector.tensor_tensor(la2[:, :, :], la[:, :, :],
                                                W["ad"][:, :].unsqueeze(1).to_broadcast([P, G, 64]), ALU.mult)\
                            .then_inc(leak.h, 1)
                        ve.wait_ge(leak.h, leak.done(i, u, 2))
                        nc.vector.reduce_sum(a4[:, u % 2], la2[:, :, :].rearrange("p g (h d) -> p g h d", h=4), AX.X)\
                            .then_inc(leak.h, 1)

                    def gates(i, u):
                        for g in range(G):
                            last = nc.vector.tensor_tensor(
                                vsv[:, u % 2, g, 64:160].rearrange("p (i c) -> p i c", i=3),
                                pVv[:, g, 160:256].rearrange("p (i c) -> p i c", i=3),
                                th2[:, g, 64:96].unsqueeze(1).to_broadcast([P, 3, 32]), ALU.mult)
                        last.then_inc(gated.h, 1)

                    def spread(i, u):
                        ve.wait_ge(xm0_ready.h, xm0_ready.done(i, u))
                        ve.wait_ge(leak.h, leak.done(i, u, 3))
                        ve.wait_ge(xm_t.h, xm_t.free(i, u, 1))
                        for h in range(4):
                            last = nc.vector.scalar_tensor_tensor(
                                xm[:, 1, h, :], mb[:, u % 2, 1, :], a4[:, u % 2, 1, h:h + 1], xm[:, 0, h, :],
                                ALU.add, ALU.max)
                        last.then_inc(xm_ready.h, 1)

                    def highest(i, u):
                        ve.wait_ge(xm_t.h, xm_t.done(i, u))
                        nc.vector.reduce_max(tm[:, :], pX[:, :].rearrange("p (h e) -> p h e", h=4),
                                             AX.X).then_inc(top.h, 1)

                    def maxima(i, u, block):
                        mrow = flat(M[:, block, :])
                        ve.wait_ge(top.h, top.done(i, u))
                        ve.sem_inc(ve_tick, 1)
                        nc.vector.tensor_tensor(mnew[:, u % 2, :], mrow, tm[:, :], ALU.max).then_inc(m_step.h, 1)
                        ve.wait_ge(m_step.h, m_step.done(i, u))
                        nc.vector.tensor_tensor(mdiff[:, u % 2, :], mrow, mnew[:, u % 2, :], ALU.subtract)\
                            .then_inc(mnew_ready.h, 1)
                        ve.wait_ge(mnew_ready.h, mnew_ready.done(i, u))
                        ve.sem_inc(ve_tick, 1)
                        nc.vector.tensor_copy(mrow, mnew[:, u % 2, :])

                    def one_hot(i, u):
                        s4 = u % 4
                        ve.wait_ge(rec_in[s4].h, rec_in[s4].at(i * 32 + 32))
                        ve.wait_ge(summed.h, summed.free(i, u, 4))
                        for g in range(G):
                            last = nc.vector.tensor_scalar(oh[:, s4, g, :], iota1[:, :], rec[:, s4, g, 0:1], None,
                                                           ALU.is_equal)
                        last.then_inc(oh_ready.h, 1)

                    def keep(i, u, block, d):
                        row = flat(acc[:, block, :])
                        if d:
                            ve.wait_ge(h_ready.h, h_ready.done(*d))
                            ve.sem_inc(ve_tick, 1)
                        rowh = row.rearrange("p (h f) -> p h f", h=4)
                        ve.wait_ge(msc_ready.h, msc_ready.done(i, u))
                        ve.wait_ge(kept.h, kept.free(i, u, 1))
                        nc.vector.tensor_tensor(rowh, rowh, msc[:, u % 4, :].unsqueeze(2).to_broadcast([P, 4, 41]),
                                                ALU.mult).then_inc(scaled.h, 1)
                        ve.wait_ge(scaled.h, scaled.done(i, u))
                        ve.wait_ge(summed.h, summed.done(i, u))
                        nc.vector.tensor_tensor(row, row, pS, ALU.add).then_inc(kept.h, 1)

                    def weigh(i, u):
                        s2 = u % 2
                        ve.wait_ge(h_ready.h, h_ready.done(i, u))
                        ve.wait_ge(pex_ready.h, pex_ready.done(i, u))
                        ve.wait_ge(summed.h, summed.free(i, u))
                        for g in range(G):
                            hv = hw[:, s2, g, :].rearrange("p (h f) -> p h f", h=4)
                            nc.vector.tensor_tensor(
                                hv[:, :, 0:40], pHv[:, g, :].rearrange("p (h f) -> p h f", h=4),
                                pex[:, s2, g, :].unsqueeze(2).to_broadcast([P, 4, 40]), ALU.mult)
                        last = nc.vector.tensor_copy(
                            hw[:, s2].rearrange("p g (h f) -> p g h f", h=4)[:, :, :, 40], pex[:, s2])
                        last.then_inc(hw_ready.h, 1)

                    def step(at):
                        a, b, c, d, e = at
                        if d:
                            block_d = block_of(ve, *d)
                        if e:
                            block_e = block_of(ve, *e)
                        if b:
                            message(*b)
                        if d:
                            highest(*d)
                            maxima(*d, block_d)
                        if a:
                            one_hot(*a)
                        if d:
                            distances(*d)
                        if b:
                            i, u = b
                            ve.wait_ge(msg_ready.h, msg_ready.done(i, u))
                            ve.wait_ge(w_ready.h, w_ready.done(i, u))
                            ve.wait_ge(t1.h, t1.free(i, u, 1))
                            product_vector(ve, L, i, u, msg[:, u % 2], pW[:, 0:448].rearrange(
                                "p (g f) -> p g f", g=G), rec[:, u % 4, :, 2:3], 0, pooled1, part1a, part2a,
                                           sv1_ready, axes1)\
                                .then_inc(tp1_ready.h, 1)
                        if c:
                            logits(*c)
                            gates(*c)
                        if e:
                            keep(*e, block_e, d)
                        if d:
                            weigh(*d)
                        if c:
                            i, u = c
                            ve.wait_ge(t2.h, t2.free(i, u, 1))
                            ve.wait_ge(gated.h, gated.done(i, u))
                            product_vector(ve, L, i, u, vsv[:, u % 2], None, rec[:, u % 4, :, 2:3], 1, pooled2,
                                           part1b, part2b, None, None).then_inc(tp2_ready.h, 1)
                            spread(*c)

                    pipeline(ve, step)
                    ve.wait_ge(kept.h, kept.done(QP - 1, 3))

        def layer0_update():
            den = sig("den", 2, NBX)
            divided = sig("divided", 1, NBX)
            turned = sig("turned", 1, NBX)
            copied = sig("copied", 1, NBX)
            made = sig("made", 1, NBX)
            updated = sig("updated", 1, NBX)
            seen = sig("seen", 2, NBX)
            acc = ACC[:, 0:NBX * 164].rearrange("p (b f) -> p b f", b=NBX)
            pT, pO = [BK[0], BK[1]], [BK[2], BK[3]]
            with nc.Block() as block:
                @block.sync
                def _(sp):
                    start(sp)

                @block.vector
                def _(ve):
                    def rows(i, u):
                        b = bass.ds(i * 2 + u, 1)
                        a = acc[:, b, :].rearrange("p o (h f) -> p (o h) f", h=4)
                        nc.vector.tensor_scalar_add(nrm[:, u, :], a[:, :, 40], 1e-16).then_inc(den.h, 1)
                        ve.wait_ge(den.h, den.done(i, u, 1))
                        nc.vector.reciprocal(nrm2[:, u, :], nrm[:, u, :]).then_inc(den.h, 1)
                        ve.wait_ge(den.h, den.done(i, u, 2))
                        ve.wait_ge(turned.h, turned.free(i, u))
                        nc.vector.tensor_tensor(xn[:, u, :].rearrange("p (h f) -> p h f", h=4), a[:, :, 0:40],
                                                nrm2[:, u, :].unsqueeze(2).to_broadcast([P, 4, 40]), ALU.mult)\
                            .then_inc(divided.h, 1)

                    def outputs(i, u):
                        b = bass.ds(i * 2 + u, 1)
                        ve.wait_ge(made.h, made.done(i, u))
                        xs = X[:, b, 0:64].rearrange("p o f -> p (o f)")
                        xv = X[:, b, 64:160].rearrange("p o (c i) -> p i (o c)", i=3)
                        nc.vector.scalar_tensor_tensor(xs, xs, 2.0, pO[u][:, 0:64], ALU.mult, ALU.add)
                        nc.vector.scalar_tensor_tensor(xv, xv, 2.0, pO[u][:, 64:160].rearrange(
                            "p (i c) -> p i c", i=3), ALU.mult, ALU.add).then_inc(updated.h, 1)
                        ve.wait_ge(updated.h, updated.done(i, u))
                        ve.sem_inc(ve_tick, 1)
                        statistics(ve, i, u, F, seen)

                    rows(0, 0)
                    rows(0, 1)
                    with ve.Fori(0, HNB - 1) as i:
                        rows(i + 1, 0)
                        rows(i + 1, 1)
                        outputs(i, 0)
                        outputs(i, 1)
                    outputs(HNB - 1, 0)
                    outputs(HNB - 1, 1)

                @block.tensor
                def _(pe):
                    def turn(i):
                        for u in range(2):
                            pe.wait_ge(divided.h, divided.done(i, u))
                            pe.wait_ge(copied.h, copied.free(i, u))
                            for k in range(2):
                                last = nc.tensor.transpose(pT[u][0:80, 128 * k:128 * k + 128],
                                                           xn[:, u, 80 * k:80 * k + 80], ident[:, :])
                            last.then_inc(turned.h, 1)

                    def make(i):
                        for u in range(2):
                            pe.wait_ge(copied.h, copied.done(i, u))
                            pe.wait_ge(updated.h, updated.free(i, u))
                            for k in range(2):
                                last = nc.tensor.matmul(pO[u][:, 0:160], xT[0:80, u, 128 * k:128 * k + 128],
                                                        W["proj0"][:, 160 * k:160 * k + 160],
                                                        start=k == 0, stop=k == 1)
                            last.then_inc(made.h, 1)

                    turn(0)
                    with pe.Fori(0, HNB - 1) as i:
                        turn(i + 1)
                        make(i)
                    make(HNB - 1)

                @block.scalar
                def _(ac):
                    with ac.Fori(0, HNB) as i:
                        for u in range(2):
                            ac.wait_ge(turned.h, turned.done(i, u))
                            ac.wait_ge(made.h, made.free(i, u))
                            nc.scalar.activation(xT[0:80, u, :], pT[u][0:80, 0:256], ACT.Copy).then_inc(copied.h, 1)

        first_statistics()
        node_table(0)
        layer0_edges(layer(0))
        layer0_update()
        for k in range(1, 4):
            node_table(k)
            edge_loop(layer(k))
            node_update(layer(k))
        last_norm()


def lay_out(x, src, dst, edge_attr_16, edge_attr_3, edge_attr_4, edge_attr_64, node_vec1, ch, **weights):
    import numpy as np
    e = src.shape[0]
    _, _, t, _ = sizes(x.shape[0], e, ch)
    nbx = sizes(x.shape[0], e, ch)[1]
    attrs = np.ones((P * t, EA3 + 1), np.float32)
    attrs[:e, 0:4] = edge_attr_4
    attrs[:e, 4:6] = edge_attr_4[:, 1:3]
    attrs[:e, EA16 - 2:EA64 - 2] = edge_attr_16
    attrs[:e, EA64 - 2:EA3 - 2] = edge_attr_64
    attrs[:e, EA3 - 2:] = edge_attr_3
    ids = []
    for a in (src, dst):
        padded = np.zeros((P * t,), np.int32)
        padded[:e] = a
        ids.append(padded)
    rows = []
    for a in (x, node_vec1):
        padded = np.zeros((P * nbx, a.shape[1]), np.float32)
        padded[:a.shape[0]] = a
        rows.append(padded)
    return {"x": rows[0], "attrs": attrs, "src": ids[0], "dst": ids[1], "node_vec1": rows[1],
            **{k: np.asarray(v) for k, v in weights.items()}}


def program(nc, arrays, n, e, ch):
    aps = {name: nc.dram_tensor(f"in_{name}", a.shape, mybir.dt.from_np(a.dtype), kind="ExternalInput").ap()
           for name, a in arrays.items()}
    out = nc.dram_tensor("out", (n, F), mybir.dt.float32, kind="ExternalOutput").ap()
    build(nc, aps, out, n, e, ch)


def kernel(**inputs):
    import numpy as np
    import concourse.bacc as bacc
    from concourse.bass_utils import run_bass_kernel_spmd
    arrays = lay_out(ch=23, **inputs)
    nc = bacc.Bacc("TRN2", target_bir_lowering=False, num_devices=1)
    program(nc, arrays, inputs["x"].shape[0], inputs["src"].shape[0], 23)
    maps = {f"in_{name}": np.ascontiguousarray(a) for name, a in arrays.items()}
    return run_bass_kernel_spmd(nc, [maps], core_ids=[0]).results[0]["out"]
```
